# Optimizing a Trainium2 kernel written in Bass

```python
import numpy as np
import jax
import jax.numpy as jnp

def _softmax(x, axis=-1):
    return jax.nn.softmax(x, axis=axis)

def _gelu(x):
    return jax.nn.gelu(x, approximate=True)

def _silu(x):
    return jax.nn.silu(x)

def _sigmoid(x):
    return jax.nn.sigmoid(x)

def _layernorm(x, axis=-1, eps=1e-05):
    m = jnp.mean(x, axis=axis, keepdims=True)
    v = jnp.var(x, axis=axis, keepdims=True)
    return (x - m) / jnp.sqrt(v + eps)

def _scatter_add(tgt, idx, src, axis=0):
    return tgt.at[idx].add(src)

def _segment_sum(src, seg, n):
    return jax.ops.segment_sum(src, seg, n)
kernel_name = 'mk_xattn_ffn_d2_seqx_r8_d1ad93'

def setup_inputs(seed: int=0):
    np.random.seed(seed)
    _w = jnp.asarray

    def _rec_inputs():
        import jax
        import jax.numpy as jnp
        _rk = jax.random.key(seed)
        x = 4.136e-05 + 0.9999 * jax.random.normal(jax.random.fold_in(_rk, 1), (4, 256, 256), jnp.float32)
        _lenS = 256 - jax.random.randint(jax.random.fold_in(_rk, 7), (4,), 0, max(1, 256 // 4) + 1, jnp.int32)
        _lenS2 = 256 - jax.random.randint(jax.random.fold_in(_rk, 8), (4,), 0, max(1, 256 // 4) + 1, jnp.int32)
        _ctx_1024P = jax.random.normal(jax.random.fold_in(_rk, 11), (4, 16, 128), jnp.float32)
        _ctx_1024c = jax.random.dirichlet(jax.random.fold_in(_rk, 511), 0.3 * jnp.ones((16,), jnp.float32), (4, 256))
        _ctx_1024t = jnp.einsum('bsk,bkd->bsd', _ctx_1024c, _ctx_1024P)
        _ctx_1024t = _ctx_1024t * jax.lax.rsqrt(jnp.mean(jnp.square(_ctx_1024t)) + 1e-12) * 0.953939
        ctx_1024 = -0.000292821 + 1.00034 * (_ctx_1024t + 0.3 * jax.random.normal(jax.random.fold_in(_rk, 611), (4, 256, 128), jnp.float32))
        _validS = jnp.arange(256)[None, :] < _lenS[:, None]
        _validS2 = jnp.arange(256)[None, :] < _lenS2[:, None]
        _causal = jnp.tril(jnp.ones((256, 256), dtype=bool))
        mask_BxS2_bf1 = jnp.ones((4, 256), dtype=bool)
        return (x, ctx_1024, mask_BxS2_bf1)
    x, ctx_1024, mask_BxS2_bf1 = _rec_inputs()

    def _L0_xattn_setup():
        import jax, jax.numpy as jnp
        import numpy as np
        import math
        B, L, DM = (2, 256, 128)
        DS, DC, EXP = (16, 4, 2)
        DI = EXP * DM
        DR = math.ceil(DM / 16)
        DT_MIN, DT_MAX, DT_FLOOR = (0.001, 0.1, 0.0001)

        def _ssm_forward(hidden_states, z, in_proj_w, conv_w, conv_b, x_proj_w, dt_proj_w, dt_proj_b, A_log, D):
            b = hidden_states.shape[0]
            x = jnp.einsum('ed,bld->bel', in_proj_w, hidden_states)
            xp = jnp.pad(x, ((0, 0), (0, 0), (DC - 1, 0)))
            xc = jax.lax.conv_general_dilated(xp, conv_w[:, None, :], window_strides=(1,), padding='VALID', dimension_numbers=('NCH', 'OIH', 'NCH'), feature_group_count=DI)
            u = jax.nn.silu(xc + conv_b[None, :, None])
            x_dbl = jnp.einsum('ke,bel->bkl', x_proj_w, u)
            dt_lo = x_dbl[:, :DR]
            Bm = x_dbl[:, DR:DR + DS]
            Cm = x_dbl[:, DR + DS:]
            delta = jax.nn.softplus(jnp.einsum('er,brl->bel', dt_proj_w, dt_lo) + dt_proj_b[None, :, None])
            A = -jnp.exp(A_log)

            def step(state, xs):
                d_t, B_t, C_t, u_t = xs
                dA = jnp.exp(d_t[..., None] * A)
                state = state * dA + (d_t * u_t)[..., None] * B_t[:, None, :]
                y_t = jnp.einsum('ben,bn->be', state, C_t)
                return (state, y_t)
            xs = (jnp.moveaxis(delta, -1, 0), jnp.moveaxis(Bm, -1, 0), jnp.moveaxis(Cm, -1, 0), jnp.moveaxis(u, -1, 0))
            state0 = jnp.zeros((b, DI, DS), delta.dtype)
            _, ys = jax.lax.scan(step, state0, xs)
            y = jnp.moveaxis(ys, 0, -1)
            y = y + D[None, :, None] * u
            y = y * jax.nn.silu(z)
            return jnp.swapaxes(y, 1, 2)
        key = jax.random.key(seed)
        ks = jax.random.split(key, 8)
        hidden_states = jax.random.normal(ks[0], (B, L, DM), jnp.float32)
        z = jax.random.normal(ks[1], (B, DI, L), jnp.float32)
        in_proj_w = jax.random.normal(ks[2], (DI, DM), jnp.float32) * DM ** (-0.5)
        conv_w = jax.random.normal(ks[3], (DI, DC), jnp.float32) * DC ** (-0.5)
        conv_b = jnp.zeros((DI,), jnp.float32)
        x_proj_w = jax.random.normal(ks[4], (DR + 2 * DS, DI), jnp.float32) * DI ** (-0.5)
        dt_std = DR ** (-0.5)
        dt_proj_w = jax.random.uniform(ks[5], (DI, DR), jnp.float32, -dt_std, dt_std)
        dt = jnp.exp(jax.random.uniform(ks[6], (DI,), jnp.float32) * (math.log(DT_MAX) - math.log(DT_MIN)) + math.log(DT_MIN))
        dt = jnp.clip(dt, DT_FLOOR)
        dt_proj_b = dt + jnp.log(-jnp.expm1(-dt))
        A_log = jnp.log(jnp.broadcast_to(jnp.arange(1, DS + 1, dtype=jnp.float32), (DI, DS)))
        D = jnp.ones((DI,), jnp.float32)
        return dict(hidden_states=hidden_states, z=z, in_proj_w=in_proj_w, conv_w=conv_w, conv_b=conv_b, x_proj_w=x_proj_w, dt_proj_w=dt_proj_w, dt_proj_b=dt_proj_b, A_log=A_log, D=D)
    _L0_xattn_all = _L0_xattn_setup()
    _L0_xattn_in = {k: v for k, v in _L0_xattn_all.items() if k in ('in_proj_w', 'conv_w', 'conv_b', 'x_proj_w', 'dt_proj_w', 'dt_proj_b', 'A_log', 'D')}
    del _L0_xattn_all

    def _L0_ffn_setup():
        import jax, jax.numpy as jnp
        import numpy as np
        TOP_K = 8

        def _masked_routing(router_logits):
            T, E = router_logits.shape
            sel_w, sel_e = jax.lax.top_k(router_logits, TOP_K)
            sel_w = jax.nn.softmax(sel_w.astype(jnp.float32), axis=1)
            rows = jnp.arange(T)[:, None]
            masked = jnp.zeros((T, E), dtype=jnp.float32).at[rows, sel_e].set(sel_w)
            count = jnp.zeros((E,), dtype=jnp.int32).at[sel_e.reshape(-1)].add(1)
            return (masked, count)
        key = jax.random.key(seed)
        k1, k2, k3, k4, k5 = jax.random.split(key, 5)
        B, S, H, E, I = (1, 256, 256, 32, 96)
        return {'hidden_states': jax.random.normal(k1, (B, S, H), dtype=jnp.float32), 'gate_w': jax.random.normal(k2, (E, H), dtype=jnp.float32) * H ** (-0.5), 'w_gate_proj': jax.random.normal(k3, (E, I, H), dtype=jnp.float32) * H ** (-0.5), 'w_up_proj': jax.random.normal(k4, (E, I, H), dtype=jnp.float32) * H ** (-0.5), 'w_down_proj': jax.random.normal(k5, (E, H, I), dtype=jnp.float32) * I ** (-0.5)}
    _L0_ffn_all = _L0_ffn_setup()
    _L0_ffn_in = {k: v for k, v in _L0_ffn_all.items() if k in ('gate_w', 'w_gate_proj', 'w_up_proj', 'w_down_proj')}
    del _L0_ffn_all

    def _L1_xattn_setup():
        import jax, jax.numpy as jnp
        import numpy as np
        N_HEADS = 16
        N_KV_HEADS = 8
        HEAD_DIM = 128
        D_TEXT = 256
        D_VISION = 128
        GROUPS = N_HEADS // N_KV_HEADS
        key = jax.random.key(seed)
        ks = jax.random.split(key, 6)
        B, T_text, T_vis = (4, 256, 72)
        text_hidden = jax.random.normal(ks[0], (B, T_text, D_TEXT), dtype=jnp.float32)
        vision_tokens = jax.random.normal(ks[1], (B, T_vis, D_VISION), dtype=jnp.float32)
        vision_mask = jnp.ones((B, T_vis), dtype=bool)
        s = 0.02
        Wq = jax.random.normal(ks[2], (D_TEXT, N_HEADS * HEAD_DIM), dtype=jnp.float32) * s
        Wk = jax.random.normal(ks[3], (D_VISION, N_KV_HEADS * HEAD_DIM), dtype=jnp.float32) * s
        Wv = jax.random.normal(ks[4], (D_VISION, N_KV_HEADS * HEAD_DIM), dtype=jnp.float32) * s
        Wo = jax.random.normal(ks[5], (N_HEADS * HEAD_DIM, D_TEXT), dtype=jnp.float32) * s
        return {'text_hidden': text_hidden, 'vision_tokens': vision_tokens, 'vision_mask': vision_mask, 'Wq': Wq, 'Wk': Wk, 'Wv': Wv, 'Wo': Wo}
    _L1_xattn_all = _L1_xattn_setup()
    _L1_xattn_in = {k: v for k, v in _L1_xattn_all.items() if k in ('Wq', 'Wk', 'Wv', 'Wo')}
    del _L1_xattn_all

    def _L1_ffn_setup():
        import jax, jax.numpy as jnp
        import numpy as np
        B, S, H = (4, 128, 256)
        E = 16
        K = 2
        I = 128
        N_SHARED = 2
        I_SHARED = I * N_SHARED
        RATIO = 0.1
        EPS = 1e-09

        def _swiglu(x, wg, wu, wd):
            return jax.nn.silu(x @ wg) * (x @ wu) @ wd
        key = jax.random.key(seed)
        ks = jax.random.split(key, 9)
        scale = 0.02
        x = jax.random.normal(ks[0], (B, S, H), dtype=jnp.float32)
        centroids = jax.random.normal(ks[1], (E, H), dtype=jnp.float32)
        gate_bias = jnp.zeros((E,), dtype=jnp.float32)
        wg_s = jax.random.normal(ks[2], (H, I_SHARED), dtype=jnp.float32) * scale
        wu_s = jax.random.normal(ks[3], (H, I_SHARED), dtype=jnp.float32) * scale
        wd_s = jax.random.normal(ks[4], (I_SHARED, H), dtype=jnp.float32) * scale
        wg = jax.random.normal(ks[5], (E, H, I), dtype=jnp.float32) * scale
        wu = jax.random.normal(ks[6], (E, H, I), dtype=jnp.float32) * scale
        wd = jax.random.normal(ks[7], (E, I, H), dtype=jnp.float32) * scale
        return {'x': x, 'centroids': centroids, 'gate_bias': gate_bias, 'wg_s': wg_s, 'wu_s': wu_s, 'wd_s': wd_s, 'wg': wg, 'wu': wu, 'wd': wd}
    _L1_ffn_all = _L1_ffn_setup()
    _L1_ffn_in = {k: v for k, v in _L1_ffn_all.items() if k in ('centroids', 'gate_bias', 'wg_s', 'wu_s', 'wd_s', 'wg', 'wu', 'wd')}
    del _L1_ffn_all
    return {'x': x, 'ctx_1024': ctx_1024, 'mask_BxS2_bf1': mask_BxS2_bf1, 'L0_xattn_in_proj_w': _L0_xattn_in['in_proj_w'], 'L0_xattn_conv_w': _L0_xattn_in['conv_w'], 'L0_xattn_conv_b': _L0_xattn_in['conv_b'], 'L0_xattn_x_proj_w': _L0_xattn_in['x_proj_w'], 'L0_xattn_dt_proj_w': _L0_xattn_in['dt_proj_w'], 'L0_xattn_dt_proj_b': _L0_xattn_in['dt_proj_b'], 'L0_xattn_A_log': _L0_xattn_in['A_log'], 'L0_xattn_D': _L0_xattn_in['D'], 'L0_ffn_gate_w': _L0_ffn_in['gate_w'], 'L0_ffn_w_gate_proj': _L0_ffn_in['w_gate_proj'], 'L0_ffn_w_up_proj': _L0_ffn_in['w_up_proj'], 'L0_ffn_w_down_proj': _L0_ffn_in['w_down_proj'], 'L1_xattn_Wq': _L1_xattn_in['Wq'], 'L1_xattn_Wk': _L1_xattn_in['Wk'], 'L1_xattn_Wv': _L1_xattn_in['Wv'], 'L1_xattn_Wo': _L1_xattn_in['Wo'], 'L1_ffn_centroids': _L1_ffn_in['centroids'], 'L1_ffn_gate_bias': _L1_ffn_in['gate_bias'], 'L1_ffn_wg_s': _L1_ffn_in['wg_s'], 'L1_ffn_wu_s': _L1_ffn_in['wu_s'], 'L1_ffn_wd_s': _L1_ffn_in['wd_s'], 'L1_ffn_wg': _L1_ffn_in['wg'], 'L1_ffn_wu': _L1_ffn_in['wu'], 'L1_ffn_wd': _L1_ffn_in['wd']}

def reference(x, ctx_1024, mask_BxS2_bf1, L0_xattn_in_proj_w, L0_xattn_conv_w, L0_xattn_conv_b, L0_xattn_x_proj_w, L0_xattn_dt_proj_w, L0_xattn_dt_proj_b, L0_xattn_A_log, L0_xattn_D, L0_ffn_gate_w, L0_ffn_w_gate_proj, L0_ffn_w_up_proj, L0_ffn_w_down_proj, L1_xattn_Wq, L1_xattn_Wk, L1_xattn_Wv, L1_xattn_Wo, L1_ffn_centroids, L1_ffn_gate_bias, L1_ffn_wg_s, L1_ffn_wu_s, L1_ffn_wd_s, L1_ffn_wg, L1_ffn_wu, L1_ffn_wd):
    import jax
    import jax.numpy as jnp

    def _L0_xattn_ref(hidden_states, z, in_proj_w, conv_w, conv_b, x_proj_w, dt_proj_w, dt_proj_b, A_log, D):
        import jax, jax.numpy as jnp
        import numpy as np
        import math
        B, L, DM = (2, 256, 128)
        DS, DC, EXP = (16, 4, 2)
        DI = EXP * DM
        DR = math.ceil(DM / 16)
        DT_MIN, DT_MAX, DT_FLOOR = (0.001, 0.1, 0.0001)

        def _ssm_forward(hidden_states, z, in_proj_w, conv_w, conv_b, x_proj_w, dt_proj_w, dt_proj_b, A_log, D):
            b = hidden_states.shape[0]
            x = jnp.einsum('ed,bld->bel', in_proj_w, hidden_states)
            xp = jnp.pad(x, ((0, 0), (0, 0), (DC - 1, 0)))
            xc = jax.lax.conv_general_dilated(xp, conv_w[:, None, :], window_strides=(1,), padding='VALID', dimension_numbers=('NCH', 'OIH', 'NCH'), feature_group_count=DI)
            u = jax.nn.silu(xc + conv_b[None, :, None])
            x_dbl = jnp.einsum('ke,bel->bkl', x_proj_w, u)
            dt_lo = x_dbl[:, :DR]
            Bm = x_dbl[:, DR:DR + DS]
            Cm = x_dbl[:, DR + DS:]
            delta = jax.nn.softplus(jnp.einsum('er,brl->bel', dt_proj_w, dt_lo) + dt_proj_b[None, :, None])
            A = -jnp.exp(A_log)

            def step(state, xs):
                d_t, B_t, C_t, u_t = xs
                dA = jnp.exp(d_t[..., None] * A)
                state = state * dA + (d_t * u_t)[..., None] * B_t[:, None, :]
                y_t = jnp.einsum('ben,bn->be', state, C_t)
                return (state, y_t)
            xs = (jnp.moveaxis(delta, -1, 0), jnp.moveaxis(Bm, -1, 0), jnp.moveaxis(Cm, -1, 0), jnp.moveaxis(u, -1, 0))
            state0 = jnp.zeros((b, DI, DS), delta.dtype)
            _, ys = jax.lax.scan(step, state0, xs)
            y = jnp.moveaxis(ys, 0, -1)
            y = y + D[None, :, None] * u
            y = y * jax.nn.silu(z)
            return jnp.swapaxes(y, 1, 2)
        return _ssm_forward(hidden_states, z, in_proj_w, conv_w, conv_b, x_proj_w, dt_proj_w, dt_proj_b, A_log, D)

    def _L0_ffn_ref(hidden_states, gate_w, w_gate_proj, w_up_proj, w_down_proj):
        import jax, jax.numpy as jnp
        import numpy as np
        TOP_K = 8

        def _masked_routing(router_logits):
            T, E = router_logits.shape
            sel_w, sel_e = jax.lax.top_k(router_logits, TOP_K)
            sel_w = jax.nn.softmax(sel_w.astype(jnp.float32), axis=1)
            rows = jnp.arange(T)[:, None]
            masked = jnp.zeros((T, E), dtype=jnp.float32).at[rows, sel_e].set(sel_w)
            count = jnp.zeros((E,), dtype=jnp.int32).at[sel_e.reshape(-1)].add(1)
            return (masked, count)
        B, S, H = hidden_states.shape
        x = hidden_states.reshape(-1, H)
        router_logits = x @ gate_w.T
        masked_w, _count = _masked_routing(router_logits)
        g = jnp.einsum('th,eih->tei', x, w_gate_proj)
        u = jnp.einsum('th,eih->tei', x, w_up_proj)
        h = jax.nn.silu(g) * u
        h = h * masked_w[:, :, None]
        out = jnp.einsum('tei,ehi->th', h, w_down_proj)
        return out.reshape(B, S, H)

    def _L1_xattn_ref(text_hidden, vision_tokens, vision_mask, Wq, Wk, Wv, Wo):
        import jax, jax.numpy as jnp
        import numpy as np
        N_HEADS = 16
        N_KV_HEADS = 8
        HEAD_DIM = 128
        D_TEXT = 256
        D_VISION = 128
        GROUPS = N_HEADS // N_KV_HEADS
        B, T_text, _ = text_hidden.shape
        T_vis = vision_tokens.shape[1]
        scale = jnp.float32(np.sqrt(HEAD_DIM))
        q = (text_hidden @ Wq).reshape(B, T_text, N_HEADS, HEAD_DIM).transpose(0, 2, 1, 3)
        k = (vision_tokens @ Wk).reshape(B, T_vis, N_KV_HEADS, HEAD_DIM).transpose(0, 2, 1, 3)
        v = (vision_tokens @ Wv).reshape(B, T_vis, N_KV_HEADS, HEAD_DIM).transpose(0, 2, 1, 3)
        k = jnp.repeat(k, GROUPS, axis=1)
        v = jnp.repeat(v, GROUPS, axis=1)
        scores = jnp.einsum('bhtd,bhsd->bhts', q, k) / scale
        mask = vision_mask[:, None, None, :]
        scores = jnp.where(mask, scores, -jnp.inf)
        attn = jax.nn.softmax(scores, axis=-1)
        attn = jnp.nan_to_num(attn, nan=0.0)
        out = jnp.einsum('bhts,bhsd->bhtd', attn, v)
        out = out.transpose(0, 2, 1, 3).reshape(B, T_text, N_HEADS * HEAD_DIM)
        return out @ Wo

    def _L1_ffn_ref(x, centroids, gate_bias, wg_s, wu_s, wd_s, wg, wu, wd):
        import jax, jax.numpy as jnp
        import numpy as np
        B, S, H = (4, 128, 256)
        E = 16
        K = 2
        I = 128
        N_SHARED = 2
        I_SHARED = I * N_SHARED
        RATIO = 0.1
        EPS = 1e-09

        def _swiglu(x, wg, wu, wd):
            return jax.nn.silu(x @ wg) * (x @ wu) @ wd
        shared = _swiglu(x, wg_s, wu_s, wd_s) * RATIO
        affinity = jax.nn.sigmoid(jnp.einsum('bsh,eh->bse', x, centroids))
        biased = affinity + gate_bias
        _, top_idx = jax.lax.top_k(biased, K)
        top_aff = jnp.take_along_axis(affinity, top_idx, axis=-1)
        weights = top_aff / (top_aff.sum(-1, keepdims=True) + EPS)
        mask = (jax.nn.one_hot(top_idx, E, dtype=x.dtype) * weights[..., None]).sum(-2)
        routed = jnp.zeros_like(x)
        for e in range(E):
            routed = routed + mask[..., e:e + 1] * _swiglu(x, wg[e], wu[e], wd[e])
        return shared + routed
    x = x + _L0_xattn_ref(ctx_1024, _layernorm(x, axis=-1), L0_xattn_in_proj_w, L0_xattn_conv_w, L0_xattn_conv_b, L0_xattn_x_proj_w, L0_xattn_dt_proj_w, L0_xattn_dt_proj_b, L0_xattn_A_log, L0_xattn_D)
    x = x + _L0_ffn_ref(_layernorm(x, axis=-1), L0_ffn_gate_w, L0_ffn_w_gate_proj, L0_ffn_w_up_proj, L0_ffn_w_down_proj)
    x = x + _L1_xattn_ref(_layernorm(x, axis=-1), ctx_1024, mask_BxS2_bf1, L1_xattn_Wq, L1_xattn_Wk, L1_xattn_Wv, L1_xattn_Wo)
    x = x + _L1_ffn_ref(_layernorm(x, axis=-1), L1_ffn_centroids, L1_ffn_gate_bias, L1_ffn_wg_s, L1_ffn_wu_s, L1_ffn_wd_s, L1_ffn_wg, L1_ffn_wu, L1_ffn_wd)
    return x

_drawn_inputs = setup_inputs


def setup_inputs(seed=0):
    import zlib

    import numpy as np

    out = dict(_drawn_inputs(seed))
    spreads = {'L0_xattn_conv_b': (0.0, 0.1), 'L0_xattn_D': (1.0, 0.2), 'L1_ffn_gate_bias': (0.0, 0.8)}
    factors = {'L0_xattn_dt_proj_w': 4.396,
     'L1_xattn_Wq': 8.0,
     'L1_xattn_Wk': 8.0,
     'L1_ffn_centroids': 8.0,
     'L1_ffn_wg_s': 8.0,
     'L1_ffn_wu_s': 8.0,
     'L1_ffn_wd_s': 8.0,
     'L1_ffn_wg': 7.474,
     'L1_ffn_wu': 7.357,
     'L1_ffn_wd': 7.4}
    for name, (base, spread) in spreads.items():
        noise = np.random.default_rng([zlib.crc32(name.encode()), seed]).standard_normal(out[name].shape)
        drawn = base * np.exp(spread * noise) if base else spread * noise
        out[name] = jnp.asarray(drawn.astype(out[name].dtype))
    for name, factor in factors.items():
        out[name] = (out[name] * factor).astype(out[name].dtype)
    return out
```

```python
from contextlib import ExitStack

import concourse.bass as bass
from concourse import mybir

F32 = mybir.dt.float32
F32R = mybir.dt.float32r
U8 = mybir.dt.uint8
U32 = mybir.dt.uint32
ALU = mybir.AluOpType
ACT = mybir.ActivationFunctionType
AX_X = mybir.AxisListType.X

P = 128
BATCHES, SEQ, WIDTH = 4, 256, 256
TOKENS = BATCHES * SEQ
CHUNKS = TOKENS // P
HALVES = 2
HT = TOKENS // HALVES
HC = CHUNKS // HALVES
HB = BATCHES // HALVES
WH = WIDTH // P
CTX = 128
DI, DS, DC, DR = 256, 16, 4, 8
EH = DI // P
E0, I0, TOP0 = 32, 96, 8
E1, I1, TOP1 = 16, 128, 2
SHARED = 2 * I1
SHARED_RATIO = 0.1
FFN0_CHUNKS = E0 * I0 // P
SHARED_CHUNKS = SHARED // P
FFN1_CHUNKS = SHARED_CHUNKS + E1
HEADS, KV_HEADS, HD = 16, 8, 128
GROUP = HEADS // KV_HEADS
SCALE = float(HD) ** -0.5
LN_EPS = 1e-5
TOP_EPS = 1e-9
MASKED = -1e30
PIECE = 3 * WIDTH
WO_PIECE = GROUP * WIDTH


class Lane:

    def __init__(self, sem, weight=1):
        self.sem, self.weight, self.steps = sem, weight, []


class Step:

    def __init__(self, lane):
        self.lane, self.awaited, self.value = lane, lane.weight == 16, None
        lane.steps.append(self)


class Queue:

    def __init__(self, lane):
        self.lane, self.todo = lane, []

    def __call__(self, emit, after=(), lane=None):
        step = Step(lane or self.lane)
        after = [s for s in after if s is not None]
        for s in after:
            s.awaited = True
        self.todo.append((emit, after, step))
        return step

    def run(self, engine):
        reached = {}
        for emit, after, step in self.todo:
            need = {}
            for s in after:
                need[s.lane] = max(need.get(s.lane, 0), s.value)
            for lane, value in need.items():
                if reached.get(lane, 0) < value:
                    engine.wait_ge(lane.sem, value)
                    reached[lane] = value
            last = emit(engine)
            if step.awaited:
                last.then_inc(step.lane.sem, step.lane.weight)


class Slot:

    def __init__(self, t, extra=None):
        self.t, self.extra, self.readers = t, extra, []


class Ring:
    def __init__(self, slots):
        self.slots, self.n = slots, 0

    def take(self):
        slot = self.slots[self.n % len(self.slots)]
        self.n += 1
        return slot

    def peek(self):
        return self.slots[self.n % len(self.slots)]


def product3(e, out, w_hi, w_lo, m_hi, m_lo, first, last):
    e.matmul(out, w_hi, m_hi, start=first, stop=False)
    e.matmul(out, w_hi, m_lo, start=False, stop=False)
    return e.matmul(out, w_lo, m_hi, start=False, stop=last)


def complete(work):
    while True:
        try:
            next(work)
        except StopIteration as end:
            return end.value


class Below:

    def __init__(self, work):
        self.work, self.result = work, None

    def advance(self):
        if self.result is None:
            try:
                next(self.work)
            except StopIteration as end:
                self.result = end.value

    def finish(self):
        if self.result is None:
            self.result = complete(self.work)
        return self.result


def build(nc, x, ctx_t, key_mask, in_proj_t, ssm_small, x_proj_t, dt_proj_t, gate_t, centroids_t, gate_bias,
          ffn0_w, attn_proj_w, attn_out_w, ffn1_w, out):
    stack = ExitStack()
    with stack:
        def lane(name, weight=1):
            return Lane(stack.enter_context(nc.semaphore(name)), weight)

        pe = Queue(lane("tensor_steps"))
        act = Queue(lane("scalar_steps"))
        dve = Queue(lane("vector_steps"))
        pool = Queue(lane("gpsimd_steps"))
        sp = Queue(lane("sync_steps"))
        stores = []

        def load_once(name, dst, src, after=()):
            return sp(lambda e: e.dma_start(dst, src), after, lane("landed_" + name, 16))

        top = [(nc.sbuf_base + 63) // 64 * 64]

        def place(name, shape, dtype=F32):
            size = 1
            for n in shape[1:]:
                size *= n
            size *= 1 if dtype == U8 else 4
            t = nc.alloc_sbuf_tensor_at(name, shape, dtype, offset=top[0])
            top[0] += (size + 31) // 32 * 32
            return t

        identity = place("identity", [P, P])
        x_tok = place("x_tok", [P, CHUNKS, WIDTH])
        ctx_sb = place("ctx_sb", [P, TOKENS])
        in_proj_sb = place("in_proj_sb", [P, DI])
        small_sb = place("small_sb", [P, EH, DC + 3 + DS])
        x_proj_sb = place("x_proj_sb", [P, EH, DR + 2 * DS])
        dt_proj_sb = place("dt_proj_sb", [DR, DI])
        decay = place("decay", [P, EH, DS])
        gate_raw = place("gate_raw", [P, WH, E0])
        gate_hi = place("gate_hi", [P, WH, E0], F32R)
        gate_lo = place("gate_lo", [P, WH, E0], F32R)
        cent_raw = place("cent_raw", [P, WH, E1])
        cent_hi = place("cent_hi", [P, WH, E1], F32R)
        cent_lo = place("cent_lo", [P, WH, E1], F32R)
        bias_bc = place("bias_bc", [P, E1])
        expert_ids = place("expert_ids", [P, E1])
        half_power = place("half_power", [P, HC])
        mask_u8 = place("mask_u8", [P, BATCHES, SEQ], U8)
        any_valid = place("any_valid", [P, BATCHES])
        stats = place("stats", [P, HC, 6])
        mean_var = place("mean_var", [P, HC, 2])
        rstd = place("rstd", [P, HC])
        x_norm = place("x_norm", [P, HC, WIDTH])
        xt_hi = [place(f"xt_hi{h}", [P, WH, HT], F32R) for h in range(HALVES)]
        xt_lo = [place(f"xt_lo{h}", [P, WH, HT], F32R) for h in range(HALVES)]
        acc_sb = place("acc_sb", [P, WH, HT])
        logits = place("logits", [P, HC, E0])
        top8 = place("top8", [P, HC, 8])
        top_idx = place("top_idx", [P, HC, 8], U32)
        top_idx_f = place("top_idx_f", [P, HC, TOP1])
        route_a = place("route_a", [P, 2, HC, E0])
        route_w = place("route_w", [P, HC, E0])
        route_sum = place("route_sum", [P, HC])
        route_t = place("route_t", [E0, HT])
        raw_slots = Ring([Slot(place(f"w_raw{i}", [P, PIECE]), lane(f"landed_w_raw{i}", 16)) for i in range(3)])
        split_slots = Ring([Slot((place(f"w_hi{i}", [P, PIECE], F32R), place(f"w_lo{i}", [P, PIECE], F32R)))
                            for i in range(4)])
        gated_slots = Ring([Slot(place(f"gated{i}", [P, HT])) for i in range(2)])
        hidden_slots = Ring([Slot(place(f"hidden{i}", [P, HT])) for i in range(2)])
        hidden_split = Ring([Slot((place(f"hidden_hi{i}", [P, HT], F32R), place(f"hidden_lo{i}", [P, HT], F32R)))
                             for i in range(3)])
        mask_slots = Ring([Slot(place(f"route_bc{i}", [P, HT]), lane(f"landed_route_bc{i}", 16)) for i in range(4)])

        shared_region = top[0]
        u_sb = place("u_sb", [P, HALVES, EH, HT])
        delta = place("delta", [P, HALVES, EH, HT])
        delta_u = place("delta_u", [P, HALVES, EH, HT])
        z_gate = place("z_gate", [P, CHUNKS, WIDTH])
        x_dbl = place("x_dbl", [DR + 2 * DS, TOKENS])
        bc_slots = Ring([Slot(place(f"bc{i}", [P, 2, HT]), lane(f"landed_bc{i}", 16)) for i in range(3)])
        da_slots = Ring([Slot(place(f"decay_t{i}", [P, EH, HT])) for i in range(5)])
        conv_in_at = top[0]
        hc_slots = Ring([Slot(place(f"read_out{i}", [P, EH, HT])) for i in range(4)])
        h_slots = Ring([Slot(place(f"state{i}", [P, EH, HT])) for i in range(2)])
        dbu_slots = Ring([Slot(place(f"drive{i}", [P, EH, HT])) for i in range(2)])
        scan_end = top[0]
        top[0] = conv_in_at
        conv_in = place("conv_in", [P, EH, BATCHES, DC - 1 + SEQ])
        assert top[0] <= scan_end

        top[0] = shared_region
        ctx_hi = place("ctx_hi", [P, TOKENS], F32R)
        ctx_lo = place("ctx_lo", [P, TOKENS], F32R)
        mask_bias = place("mask_bias", [P, BATCHES, SEQ])

        def split_pair(name, shape):
            return (place(name + "_hi", shape, F32R), place(name + "_lo", shape, F32R))

        k_slots = Ring([Slot(split_pair(f"k_t{i}", [P, HT])) for i in range(2)])
        v_slots = Ring([Slot(split_pair(f"v{i}", [P, HC, HD])) for i in range(2)])
        q_slots = Ring([Slot(split_pair(f"q_t{i}", [P, HT])) for i in range(4)])
        score_slots = Ring([Slot(place(f"scores{i}", [P, 2, SEQ]),
                                 (place(f"row_max{i}", [P, 2]), place(f"row_bias{i}", [P, 2]))) for i in range(2)])
        prob_slots = Ring([Slot(place(f"probs{i}", [P, 2, SEQ]),
                                (place(f"row_sum{i}", [P, 2]), place(f"row_scale{i}", [P, 2]))) for i in range(3)])
        prob_t_slots = Ring([Slot(split_pair(f"probs_t{i}", [P, 2, SEQ])) for i in range(2)])
        head_slots = Ring([Slot(split_pair(f"head_out{i}", [P, HT])) for i in range(2)])
        assert max(scan_end, top[0]) <= nc.sbuf_usable_end

        banks = [Slot(stack.enter_context(nc.psum_tensor(f"bank{i}", [P, 512], F32))) for i in range(8)]
        spare = Ring(banks[0:2])

        bc_dram = nc.dram_tensor("bc_scratch", (2 * DS, TOKENS), F32).ap()
        route_dram = [[nc.dram_tensor(f"route_scratch{layer}_{h}", (n, HT), F32).ap() for h in range(HALVES)]
                      for layer, n in ((0, E0), (1, E1))]

        def rows(src, p):
            return src.partition_broadcast(p).rearrange("p a n -> p (a n)")

        in_proj_in = load_once("in_proj", in_proj_sb[:, :], in_proj_t)
        ctx_in = [load_once(f"ctx{h}", ctx_sb[:, h * HT:(h + 1) * HT], ctx_t[:, h * HT:(h + 1) * HT])
                  for h in range(HALVES)]
        small_in = load_once("ssm_small", small_sb[:, :, :], ssm_small)
        x_dram = x.rearrange("b (c p) w -> p (b c) w", p=P)
        out_dram = out.rearrange("b (c p) w -> p (b c) w", p=P)
        x_in = [load_once(f"x{h}", x_tok[:, h * HC:(h + 1) * HC, :], x_dram[:, h * HC:(h + 1) * HC, :])
                for h in range(HALVES)]
        x_proj_in = load_once("x_proj", x_proj_sb[:, :, :], x_proj_t)
        dt_proj_in = load_once("dt_proj", dt_proj_sb[:, :], dt_proj_t)
        gate_in = load_once("gate", gate_raw[:, :, :], gate_t)
        cent_in = load_once("centroids", cent_raw[:, :, :], centroids_t)
        bias_in = load_once("gate_bias", bias_bc[:, :], rows(gate_bias, P))
        mask_in = load_once("key_mask", mask_u8[:, :, :].rearrange("p b s -> p (b s)"), rows(key_mask, P))

        conv_w = [small_sb[:, :, j] for j in range(DC)]
        conv_b, skip_d, dt_bias = (small_sb[:, :, DC + j] for j in range(3))
        a_log = small_sb[:, :, DC + 3:]

        ident_zero = pool(lambda e: e.memset(identity[:, :], 0.0))
        ident_ready = pool(lambda e: e.affine_select(
            out=identity[:, :], in_=identity[:, :], compare_op=ALU.not_equal, fill=1.0, base=0,
            pattern=[[-1, P]], channel_multiplier=1), [ident_zero])
        pad_ready = pool(lambda e: e.memset(conv_in[:, :, :, 0:DC - 1].rearrange("p h b s -> p (h b) s"), 0.0))
        power_ready = pool(lambda e: e.memset(half_power[:, :], -0.5))
        ids_ready = pool(lambda e: e.iota(expert_ids[:, :], pattern=[[1, E1]], base=0, channel_multiplier=0,
                                          allow_small_or_imprecise_dtypes=True))

        pieces = {("ffn0", h, c): ffn0_w[c] for h in range(HALVES) for c in range(FFN0_CHUNKS)}
        for h in range(HALVES):
            for kv in range(KV_HEADS + 1):
                if kv < KV_HEADS:
                    pieces["proj", h, kv] = attn_proj_w[kv]
                if kv > 0:
                    pieces["out", h, kv - 1] = attn_out_w[kv - 1]
        pieces.update({("ffn1", c): ffn1_w[c] for c in range(FFN1_CHUNKS)})
        order = {key: n for n, key in enumerate(pieces)}
        pieces = list(pieces.values())
        fetched, pieces_split = [], []

        def fetch_piece():
            if len(fetched) < len(pieces):
                src = pieces[len(fetched)]
                slot = raw_slots.take()
                n = src.shape[-1]
                landed = sp(lambda e: e.dma_start(slot.t[:, 0:n], src), slot.readers, slot.extra)
                fetched.append((slot, n, landed))

        def split_piece():
            if len(pieces_split) == len(pieces) or split_slots.peek().readers is None:
                return
            if len(fetched) < len(pieces_split) + 3:
                fetch_piece()
            raw, n, landed = fetched[len(pieces_split)]
            slot = split_slots.take()
            hi, lo = slot.t
            rounded = act(lambda e: e.activation(hi[:, 0:n], raw.t[:, 0:n], ACT.Copy), [landed, *slot.readers])
            rest = pool(lambda e: e.tensor_tensor(lo[:, 0:n], raw.t[:, 0:n], hi[:, 0:n].bitcast(F32), ALU.subtract),
                        [landed, rounded, *slot.readers])
            raw.readers = [rounded, rest]
            slot.readers = None
            pieces_split.append((slot, rest))

        def split_weights(*key):
            while len(pieces_split) <= order[key]:
                done = len(pieces_split)
                split_piece()
                assert len(pieces_split) > done, "no slot is free"
            return pieces_split[order[key]]

        for _ in range(3):
            fetch_piece()

        def layer_norm(half, source):
            done = []
            for j in range(HC):
                t = half * HC + j
                done.append(dve(lambda e, j=j, t=t: e.bn_stats(stats[:, j, :], x_tok[:, t, :]),
                                [*source, *norm_slot.readers]))
            for j in range(HC):
                moments = dve(lambda e, j=j: e.bn_aggr(mean_var[:, j, :], stats[:, j, :]), [done[j]])
            variance = pool(lambda e: e.tensor_scalar(rstd[:, :], mean_var[:, :, 1], LN_EPS, None, ALU.add), [moments])
            scale = pool(lambda e: e.tensor_tensor(rstd[:, :], rstd[:, :], half_power[:, :], ALU.pow),
                         [variance, power_ready])
            normed = []
            for j in range(HC):
                t = half * HC + j
                normed.append(dve(lambda e, j=j, t=t: e.tensor_scalar(
                    x_norm[:, j, :], x_tok[:, t, :], mean_var[:, j, 0:1], rstd[:, j:j + 1], ALU.subtract, ALU.mult),
                    [scale, moments]))
            norm_slot.readers = [normed[-1]]
            return normed[-1]

        norm_slot = Slot(None)
        xt_slots = [Slot(None) for _ in range(HALVES)]

        def turn_and_split(half, normed, ring):
            yield
            for w in range(WH):
                bank = ring.take()

                def turn(e, w=w, bank=bank):
                    for j in range(HC):
                        last = e.transpose(bank.t[:, j * P:(j + 1) * P], x_norm[:, j, w * P:(w + 1) * P], identity[:, :])
                    return last
                turned = pe(turn, [normed, ident_ready, *bank.readers])
                hi = act(lambda e, w=w, bank=bank: e.activation(xt_hi[half][:, w, :], bank.t[:, :], ACT.Copy),
                         [turned, *xt_slots[half].readers])
                lo = dve(lambda e, w=w, bank=bank: e.tensor_tensor(
                    xt_lo[half][:, w, :], bank.t[:, :], xt_hi[half][:, w, :].bitcast(F32), ALU.subtract),
                    [turned, hi, *xt_slots[half].readers])
                bank.readers = [hi, lo]
                norm_slot.readers = [turned]
            xt_slots[half].readers = []
            return lo

        def router_logits(half, xt_ready, w_hi, w_lo, n, w_ready, ring):
            yield
            bank = ring.take()

            def multiply(e):
                for j in range(HC):
                    for w in range(WH):
                        tok = slice(j * P, (j + 1) * P)
                        last = product3(e, bank.t[:, j * n:(j + 1) * n], xt_hi[half][:, w, tok], xt_lo[half][:, w, tok],
                                        w_hi[:, w, :], w_lo[:, w, :], w == 0, w == WH - 1)
                return last
            return bank, pe(multiply, [xt_ready, w_ready, *bank.readers])

        route_slot = Slot(None)
        route_t_slot = Slot(None, lane("route_stored", 16))

        def route_to_dram(layer, half, n, weighted, ring):
            yield
            yield
            bank = ring.take()

            def turn(e):
                for j in range(HC):
                    last = e.transpose(bank.t[0:n, j * P:(j + 1) * P], route_w[:, j, 0:n], identity[:, :])
                return last
            turned = pe(turn, [weighted, ident_ready, *bank.readers])
            copied = dve(lambda e: e.tensor_copy(route_t[0:n, :], bank.t[0:n, :]), [turned, *route_t_slot.readers])
            bank.readers = [copied]
            route_slot.readers = [turned]
            stored = sp(lambda e: e.dma_start(route_dram[layer][half], route_t[0:n, :]), [copied], route_t_slot.extra)
            route_t_slot.readers = [stored]
            stores.append(stored)
            return stored

        def route_layer0(half, xt_ready, ring):
            bank, product = yield from router_logits(half, xt_ready, gate_hi, gate_lo, E0, gate_ready, ring)
            kept = dve(lambda e: e.tensor_copy(logits[:, :, :], bank.t[:, 0:HC * E0].rearrange("p (j n) -> p j n", j=HC)),
                       [product, *route_slot.readers])
            bank.readers = [kept]
            for j in range(HC):
                best = dve(lambda e, j=j: e.max(out=top8[:, j, :], in_=logits[:, j, :]), [kept, *route_slot.readers])
            for j in range(HC):
                taken = dve(lambda e, j=j: e.match_replace(out=route_a[:, 1, j, :], in_to_replace=top8[:, j, :],
                                                           in_values=logits[:, j, :], imm_value=MASKED), [best])
            row_max = top8[:, :, 0:1].broadcast_to([P, HC, E0])
            dve(lambda e: e.tensor_tensor(route_a[:, 0, :, :], logits[:, :, :], row_max, ALU.subtract), [best])
            shifted = dve(lambda e: e.tensor_tensor(route_a[:, 1, :, :], route_a[:, 1, :, :], row_max, ALU.subtract),
                          [taken])
            flat = route_a[:, :, :, :].rearrange("p a j n -> p (a j n)")
            raised = act(lambda e: e.activation(flat, flat, ACT.Exp), [shifted])
            picked = dve(lambda e: e.tensor_tensor(route_w[:, :, :], route_a[:, 0, :, :], route_a[:, 1, :, :],
                                                   ALU.subtract), [raised])
            summed = dve(lambda e: e.tensor_reduce(route_sum[:, :], route_w[:, :, :], AX_X, ALU.add), [picked])
            inverse = dve(lambda e: e.reciprocal(route_sum[:, :], route_sum[:, :]), [summed])
            weighted = dve(lambda e: e.tensor_tensor(
                route_w[:, :, :], route_w[:, :, :], route_sum[:, :].unsqueeze(2).broadcast_to([P, HC, E0]), ALU.mult),
                [inverse])
            return (yield from route_to_dram(0, half, E0, weighted, ring))

        def route_layer1(half, xt_ready, ring):
            bank, product = yield from router_logits(half, xt_ready, cent_hi, cent_lo, E1, cent_ready, ring)
            aff = logits[:, :, 0:E1]
            biased = route_a[:, 0, :, 0:E1]
            affinity = act(lambda e: e.activation(aff, bank.t[:, 0:HC * E1].rearrange("p (j n) -> p j n", j=HC),
                                                  ACT.Sigmoid), [product, *route_slot.readers])
            bank.readers = [affinity]
            ranked = dve(lambda e: e.tensor_tensor(biased, aff, bias_bc[:, :].unsqueeze(1).broadcast_to([P, HC, E1]),
                                                   ALU.add), [affinity, bias_in])
            for j in range(HC):
                best = dve(lambda e, j=j: e.max(out=top8[:, j, :], in_=route_a[:, 0, j, 0:E1]),
                           [ranked, *route_slot.readers])
            for j in range(HC):
                found = dve(lambda e, j=j: e.max_index(top_idx[:, j, :], top8[:, j, :], route_a[:, 0, j, 0:E1]), [best])
            index_f = dve(lambda e: e.tensor_copy(top_idx_f[:, :, :], top_idx[:, :, 0:TOP1]), [found])
            for k in range(TOP1):
                for j in range(HC):
                    chosen = dve(lambda e, k=k, j=j: e.scalar_tensor_tensor(
                        out=route_a[:, k, j, E1:2 * E1], in0=expert_ids[:, :], scalar=top_idx_f[:, j, k:k + 1],
                        in1=logits[:, j, 0:E1], op0=ALU.is_equal, op1=ALU.mult), [index_f, ids_ready])
            both = dve(lambda e: e.tensor_tensor(route_w[:, :, 0:E1], route_a[:, 0, :, E1:2 * E1],
                                                 route_a[:, 1, :, E1:2 * E1], ALU.add), [chosen])
            summed = dve(lambda e: e.tensor_reduce(route_sum[:, :], route_w[:, :, 0:E1], AX_X, ALU.add), [both])
            guarded = dve(lambda e: e.tensor_scalar(route_sum[:, :], route_sum[:, :], TOP_EPS, None, ALU.add), [summed])
            inverse = dve(lambda e: e.reciprocal(route_sum[:, :], route_sum[:, :]), [guarded])
            weighted = dve(lambda e: e.tensor_tensor(
                route_w[:, :, 0:E1], route_w[:, :, 0:E1], route_sum[:, :].unsqueeze(2).broadcast_to([P, HC, E1]),
                ALU.mult), [inverse])
            return (yield from route_to_dram(1, half, E1, weighted, ring))

        acc_slot = Slot(None)

        def add_to_x(half, acc_banks, finished, ring):
            copies = []
            for w in range(WH):
                engine = (act, dve)[w]
                emit = ((lambda e, w=w: e.activation(acc_sb[:, w, :], acc_banks[w].t[:, :], ACT.Copy)),
                        (lambda e, w=w: e.tensor_copy(acc_sb[:, w, :], acc_banks[w].t[:, :])))[w]
                copies.append(engine(emit, [finished, *acc_slot.readers]))
                acc_banks[w].readers = [copies[w]]
            yield
            added = []
            for pair in range(HC // 2):
                bank = ring.take()

                def turn(e, pair=pair, bank=bank):
                    for j in range(2):
                        tok = slice((2 * pair + j) * P, (2 * pair + j + 1) * P)
                        for w in range(WH):
                            last = e.transpose(bank.t[:, j * WIDTH + w * P:j * WIDTH + (w + 1) * P],
                                               acc_sb[:, w, tok], identity[:, :])
                    return last
                turned = pe(turn, [*copies, ident_ready, *bank.readers])
                t = half * HC + 2 * pair
                added.append(dve(lambda e, t=t, bank=bank: e.tensor_tensor(
                    x_tok[:, t:t + 2, :].rearrange("p t w -> p (t w)"),
                    x_tok[:, t:t + 2, :].rearrange("p t w -> p (t w)"), bank.t[:, :], ALU.add), [turned]))
                bank.readers = [added[-1]]
                acc_slot.readers = [turned]
            return added

        y_banks = banks[0:EH]
        decays = {}

        def scan_decays(half, n):
            slot = da_slots.take()
            for c in range(EH):
                last = act(lambda e, c=c: e.activation(
                    slot.t[:, c, :].rearrange("p (b s) -> p b s", b=HB)[:, :, 1:],
                    delta[:, half, c, :].rearrange("p (b s) -> p b s", b=HB)[:, :, 1:],
                    ACT.Exp, scale=decay[:, c, n:n + 1]), [delta_ready[half][0], decay_ready, *slot.readers])
            decays[half, n] = (slot, last)

        bc_tiles = {}

        def scan_load(half, n):
            if n >= DS:
                return
            slot = bc_slots.take()
            src = bc_dram.rearrange("(k n) s -> n k s", k=2)[n:n + 1, :, half * HT:(half + 1) * HT]
            src = src.partition_broadcast(P).rearrange("p a k s -> p (a k) s")
            bc_tiles[half, n] = (slot, sp(lambda e: e.dma_start(slot.t[:, :, :], src),
                                          [bc_stored[half], *slot.readers], slot.extra))

        drives, read_outs = {}, {}

        def scan_drive(half, n):
            if n > 0:
                scan_load(half, n + 2)
            bc, bc_in = bc_tiles[half, n]
            dbu = dbu_slots.take()
            b_row = bc.t[:, 0:1, :].broadcast_to([P, EH, HT])
            drives[half, n] = (dbu, pool(lambda e: e.tensor_tensor(
                dbu.t[:, :, :], delta_u[:, half, :, :], b_row, ALU.mult),
                [bc_in, delta_ready[half][1], *dbu.readers]))

        def scan_state(half, n):
            bc, bc_in = bc_tiles.pop((half, n))
            da, da_ready = decays.pop((half, n))
            dbu, drive = drives.pop((half, n))
            h, hc = h_slots.take(), hc_slots.take()
            c_row = bc.t[:, 1:2, :].broadcast_to([P, EH, HT])
            flat = [s.t[:, :, :].rearrange("p c s -> p (c s)") for s in (da, dbu, h)]
            state = dve(lambda e: e.tensor_tensor_scan(flat[2], flat[0], flat[1], 0.0, ALU.mult, ALU.add),
                        [drive, da_ready, *h.readers])
            da.readers, dbu.readers = [state], [state]
            read = dve(lambda e: e.tensor_tensor(hc.t[:, :, :], h.t[:, :, :], c_row, ALU.mult),
                       [state, bc_in, *hc.readers])
            h.readers = [read]
            bc.readers = [drive, read]
            read_outs[half, n] = (hc, read)

        def scan_add(half, n):
            other, other_ready = read_outs.pop((half, n - 1))
            hc, ready = read_outs[half, n]
            both = dve(lambda e: e.tensor_tensor(hc.t[:, :, :], hc.t[:, :, :], other.t[:, :, :], ALU.add),
                       [ready, other_ready])
            other.readers = [both]
            read_outs[half, n] = (hc, both)

        def scan_sum(half, n, first):
            hc, ready = read_outs.pop((half, n))

            def accumulate(e):
                for c in range(EH):
                    last = e.matmul(y_banks[c].t[:, :], identity[:, :], hc.t[:, c, :], start=first, stop=n == DS - 1)
                return last
            before = [r for b in y_banks for r in b.readers] if first else []
            summed = pe(accumulate, [ready, ident_ready, *before])
            hc.readers = [summed]
            return summed

        def scan_finish(half, summed):
            y = hc_slots.take()
            for c in range(EH):
                with_skip = dve(lambda e, c=c: e.scalar_tensor_tensor(
                    out=y.t[:, c, :], in0=u_sb[:, half, c, :], scalar=skip_d[:, c:c + 1], in1=y_banks[c].t[:, :],
                    op0=ALU.mult, op1=ALU.add), [summed, *y.readers])
                y_banks[c].readers = [with_skip]
            z = z_gate[:, half * HC:(half + 1) * HC, :].rearrange("p (b c) s -> p c b s", c=EH)
            gated = dve(lambda e: e.tensor_tensor(y.t[:, :, :].rearrange("p c (b s) -> p c b s", b=HB),
                                                  y.t[:, :, :].rearrange("p c (b s) -> p c b s", b=HB), z, ALU.mult),
                        [with_skip, z_ready[half]])
            yield
            added = []
            for b in range(HB):
                bank = spare.take()

                def turn(e, b=b, bank=bank):
                    for l in range(SEQ // P):
                        for c in range(EH):
                            at = b * SEQ + l * P
                            last = e.transpose(bank.t[:, l * DI + c * P:l * DI + (c + 1) * P],
                                               y.t[:, c, at:at + P], identity[:, :])
                    return last
                turned = pe(turn, [gated, ident_ready, *bank.readers])
                t = half * HC + b * (SEQ // P)
                added.append(dve(lambda e, t=t, bank=bank: e.tensor_tensor(
                    x_tok[:, t:t + 2, :].rearrange("p t w -> p (t w)"),
                    x_tok[:, t:t + 2, :].rearrange("p t w -> p (t w)"), bank.t[:, :], ALU.add), [turned]))
                bank.readers = [added[-1]]
            y.readers = [turned]
            return added

        before_ffn = Ring(banks[EH:])
        conv_ready, u_ready, z_ready, bc_stored, x_dbl_ready, delta_ready = {}, {}, {}, {}, {}, {}

        def project_and_convolve(half):
            for c in range(EH):
                bank = before_ffn.take()
                projected = pe(lambda e, c=c, bank=bank: e.matmul(
                    bank.t[:, :], in_proj_sb[:, c * P:(c + 1) * P], ctx_sb[:, half * HT:(half + 1) * HT],
                    start=True, stop=True), [ctx_in[half], in_proj_in, *bank.readers])
                moved = act(lambda e, c=c, bank=bank: e.activation(
                    conv_in[:, c, half * HB:(half + 1) * HB, DC - 1:],
                    bank.t[:, :].rearrange("p (b s) -> p b s", b=HB), ACT.Copy), [projected])
                bank.readers = [moved]
                conv_out = u_sb[:, half, c, :].rearrange("p (b s) -> p b s", b=HB)
                taps = [conv_in[:, c, half * HB:(half + 1) * HB, j:j + SEQ] for j in range(DC)]
                step = dve(lambda e, c=c, taps=taps, conv_out=conv_out: e.tensor_scalar(
                    conv_out, taps[0], conv_w[0][:, c:c + 1], None, ALU.mult), [moved, pad_ready, small_in])
                for j in range(1, DC):
                    step = dve(lambda e, c=c, j=j, taps=taps, conv_out=conv_out: e.scalar_tensor_tensor(
                        out=conv_out, in0=taps[j], scalar=conv_w[j][:, c:c + 1], in1=conv_out,
                        op0=ALU.mult, op1=ALU.add), [step])
                conv_ready[half, c] = step

        def activate_u(half):
            for c in range(EH):
                u_ready[half] = act(lambda e, c=c: e.activation(
                    u_sb[:, half, c, :], u_sb[:, half, c, :], ACT.Silu, bias=conv_b[:, c:c + 1]),
                    [conv_ready[half, c]])

        def activate_z(half, normed):
            z_ready[half] = act(lambda e: e.activation(
                z_gate[:, half * HC:(half + 1) * HC, :], x_norm[:, :, :], ACT.Silu), [normed])
            norm_slot.readers = [z_ready[half]]

        def project_x_dbl(half):
            bank = before_ffn.take()
            tok = slice(half * HT, (half + 1) * HT)

            def multiply(e):
                for c in range(EH):
                    last = e.matmul(bank.t[0:DR + 2 * DS, :], x_proj_sb[:, c, :], u_sb[:, half, c, :],
                                    start=c == 0, stop=c == EH - 1)
                return last
            product = pe(multiply, [x_proj_in, u_ready[half], *bank.readers])
            x_dbl_ready[half] = act(lambda e: e.activation(x_dbl[:, tok], bank.t[0:DR + 2 * DS, :], ACT.Copy),
                                    [product])
            bank.readers = [x_dbl_ready[half]]
            bc_stored[half] = sp(lambda e: e.dma_start(bc_dram[:, tok], x_dbl[DR:, tok]), [x_dbl_ready[half]],
                                 lane(f"bc_stored{half}", 16))
            stores.append(bc_stored[half])

        def make_delta(half, s_buf, s_slot):
            for c in range(EH):
                bank = before_ffn.take()
                product = pe(lambda e, c=c, bank=bank: e.matmul(
                    bank.t[:, :], dt_proj_sb[:, c * P:(c + 1) * P], x_dbl[0:DR, half * HT:(half + 1) * HT],
                    start=True, stop=True), [x_dbl_ready[half], dt_proj_in, *bank.readers])
                away = act(lambda e, c=c, bank=bank: e.activation(
                    s_buf[:, c, :], bank.t[:, :], ACT.Abs, bias=dt_bias[:, c:c + 1]), [product, *s_slot.readers])
                floor = dve(lambda e, c=c, bank=bank: e.tensor_scalar(
                    delta[:, half, c, :], bank.t[:, :], dt_bias[:, c:c + 1], 0.0, ALU.add, ALU.max), [away])
                bank.readers = [floor]
            s_all = s_buf.rearrange("p c s -> p (c s)")
            d_all, one_all, u_all = (t[:, half, :, :].rearrange("p c s -> p (c s)") for t in (delta, delta_u, u_sb))
            log_all = acc_sb[:, :, :].rearrange("p c s -> p (c s)")
            raised = act(lambda e: e.activation(s_all, s_all, ACT.Exp, scale=-1.0), [away])
            logged = act(lambda e: e.activation(log_all, s_all, ACT.Ln, bias=1.0), [raised, *acc_slot.readers])
            plus = dve(lambda e: e.tensor_scalar(one_all, s_all, 1.0, None, ALU.add), [raised])
            excess = dve(lambda e: e.scalar_tensor_tensor(out=one_all, in0=one_all, scalar=1.0, in1=s_all,
                                                          op0=ALU.subtract, op1=ALU.subtract), [plus])
            log1p = dve(lambda e: e.tensor_tensor(log_all, log_all, one_all, ALU.subtract), [logged, excess])
            ready = dve(lambda e: e.tensor_tensor(d_all, d_all, log_all, ALU.add), [log1p, floor])
            driven = dve(lambda e: e.tensor_tensor(delta_u[:, half, :, :].rearrange("p c s -> p (c s)"), d_all, u_all,
                                                   ALU.mult), [ready, u_ready[half]])
            delta_ready[half] = (ready, driven)
            s_slot.readers = [logged, excess]
            acc_slot.readers = [ready]

        normed = layer_norm(0, [x_in[0]])
        project_and_convolve(0)
        activate_z(0, normed)
        activate_u(0)
        project_x_dbl(0)
        for n in range(3):
            scan_load(0, n)
        activate_z(1, layer_norm(1, [x_in[1]]))
        project_and_convolve(1)
        for slot in hc_slots.slots + h_slots.slots:
            slot.readers = [conv_ready[1, EH - 1]]
        a_exp = act(lambda e: e.activation(decay[:, :, :], a_log, ACT.Exp), [small_in])
        decay_ready = dve(lambda e: e.tensor_scalar(decay[:, :, :], decay[:, :, :], -1.0, None, ALU.mult), [a_exp])
        make_delta(0, da_slots.slots[-1].t[:, :, :], da_slots.slots[-1])
        for slot in da_slots.slots:
            slot.readers = [pool(lambda e, slot=slot: e.memset(
                slot.t[:, :, :].rearrange("p c (b s) -> p (c b) s", b=HB)[:, :, 0:1], 0.0), slot.readers)]

        def split_small(raw, hi, lo, landed):
            rounded = dve(lambda e: e.tensor_copy(hi[:, :, :], raw[:, :, :]), [landed])
            return dve(lambda e: e.tensor_tensor(lo[:, :, :], raw[:, :, :], hi[:, :, :].bitcast(F32), ALU.subtract),
                       [rounded])

        gate_ready = split_small(gate_raw, gate_hi, gate_lo, gate_in)
        cent_ready = split_small(cent_raw, cent_hi, cent_lo, cent_in)

        def ffn0_segments(c):
            at, end = c * P, (c + 1) * P
            while at < end:
                n = min(end, (at // I0 + 1) * I0) - at
                yield at // I0, at - c * P, n
                at += n

        def load_route(layer, half, c, stored):
            slot = mask_slots.take()
            parts = list(ffn0_segments(c)) if layer == 0 else [(c - SHARED_CHUNKS, 0, P)]
            for expert, at, n in parts:
                landed = sp(lambda e, expert=expert, at=at, n=n: e.dma_start(
                    slot.t[at:at + n, :], rows(route_dram[layer][half][expert:expert + 1, :], n)),
                    [stored, *slot.readers], slot.extra)
            return slot, landed

        def run_ffn(layer, units, stored, xt_ready, acc_of, between):
            gu = Ring([(banks[4], banks[5]), (banks[6], banks[7])])
            chunks, first_done, waiting, routes = {}, set(), [], {}
            last_use = {c: max(i for i, u in enumerate(units) if u[0] == c) for c, _ in units}
            finished = {}

            def need_route(i):
                if i < len(units) and not (layer == 1 and units[i][0] < SHARED_CHUNKS):
                    c, half = units[i]
                    routes[i] = load_route(layer, half, c, stored[half])

            def down(i, c, half, split, hidden_ready):
                slot, _ = chunks[c]
                hi, lo = slot.t
                first = half not in first_done
                first_done.add(half)
                final = i == max(k for k, u in enumerate(units) if u[1] == half)

                def multiply(e):
                    for w in range(WH):
                        at = slice(2 * WIDTH + w * P, 2 * WIDTH + (w + 1) * P)
                        last = product3(e, acc_of[half][w].t[:, :], hi[:, at], lo[:, at], split.t[0][:, :],
                                        split.t[1][:, :], first, final)
                    return last
                before = [r for b in acc_of[half] for r in b.readers] if first else []
                done = pe(multiply, [hidden_ready, *before])
                split.readers = [done]
                if last_use[c] == i:
                    slot.readers = [done]
                if final:
                    finished[half] = done

            for i in range(2):
                need_route(i)
            for i, (c, half) in enumerate(units):
                if c not in chunks:
                    key = ("ffn0", half, c) if layer == 0 else ("ffn1", c)
                    chunks[c] = split_weights(*key)
                slot, w_ready = chunks[c]
                hi, lo = slot.t
                g_bank, u_bank = gu.take()
                both = []
                for k, bank in enumerate((g_bank, u_bank)):
                    def multiply(e, k=k, bank=bank, hi=hi, lo=lo, half=half):
                        for w in range(WH):
                            at = slice(k * WIDTH + w * P, k * WIDTH + (w + 1) * P)
                            last = product3(e, bank.t[:, :], hi[:, at], lo[:, at], xt_hi[half][:, w, :],
                                            xt_lo[half][:, w, :], w == 0, w == WH - 1)
                        return last
                    both.append(pe(multiply, [w_ready, xt_ready[half], *bank.readers]))
                xt_slots[half].readers = [both[-1]]
                if len(waiting) == 2:
                    down(*waiting.pop(0))
                need_route(i + 2)
                gated, hidden, split = gated_slots.take(), hidden_slots.take(), hidden_split.take()
                silu = act(lambda e, g=gated, b=g_bank: e.activation(g.t[:, :], b.t[:, :], ACT.Silu),
                           [both[0], *gated.readers])
                g_bank.readers = [silu]
                if i in routes:
                    up = dve(lambda e, g=gated, h=hidden, b=u_bank: e.tensor_tensor(
                        h.t[:, :], g.t[:, :], b.t[:, :], ALU.mult), [silu, both[1], *hidden.readers])
                    route, route_in = routes.pop(i)
                    made = dve(lambda e, h=hidden, r=route: e.tensor_tensor(
                        h.t[:, :], h.t[:, :], r.t[:, :], ALU.mult), [up, route_in])
                    route.readers = [made]
                else:
                    up = made = dve(lambda e, g=gated, h=hidden, b=u_bank: e.scalar_tensor_tensor(
                        out=h.t[:, :], in0=g.t[:, :], scalar=SHARED_RATIO, in1=b.t[:, :], op0=ALU.mult,
                        op1=ALU.mult), [silu, both[1], *hidden.readers])
                u_bank.readers = [up]
                gated.readers = [up]
                if len(pieces_split) <= order[key] + 2:
                    split_piece()
                ahead = between(i)
                rounded = act(lambda e, h=hidden, s=split: e.activation(s.t[0][:, :], h.t[:, :], ACT.Copy),
                              [made, *split.readers])
                rest = dve(lambda e, h=hidden, s=split: e.tensor_tensor(
                    s.t[1][:, :], h.t[:, :], s.t[0][:, :].bitcast(F32), ALU.subtract), [rounded, *split.readers])
                hidden.readers = [rounded, rest]
                waiting.append((i, c, half, split, rest))
                if ahead:
                    ahead()
            for unit in waiting:
                down(*unit)
            return finished

        for n in range(4):
            scan_decays(0, n)
        for n in range(DS):
            scan_drive(0, n)
            scan_state(0, n)
            summed = scan_sum(0, n, n == 0)
            if n + 4 < DS:
                scan_decays(0, n + 4)
            if n == 1:
                activate_u(1)
            if n == 3:
                project_x_dbl(1)
            if n == 9:
                make_delta(1, x_norm[:, :, :].rearrange("p (c a) w -> p c (a w)", c=EH), norm_slot)
        split_piece()
        split_piece()
        def to_next_part(added, half, router):
            xt = yield from turn_and_split(half, layer_norm(half, added), spare)
            stored = yield from router(half, xt, spare)
            return xt, stored

        def scan_to_ffn(half, summed):
            added = yield from scan_finish(half, summed)
            return (yield from to_next_part(added, half, route_layer0))

        xt_ready, stored = {}, {}
        xt_ready[0], stored[0] = complete(scan_to_ffn(0, summed))
        for n in range(3):
            scan_load(1, n)
        for n in range(2):
            scan_decays(1, n)
        scan_drive(1, 0)
        after_scan = []

        def scan_below(i):
            n = i
            if n > 1 and n % 2 == 0 and n <= DS:
                scan_add(1, n - 1)
            if n > 2 and n % 2 == 1 and n <= DS:
                scan_sum(1, n - 2, n == 3)
            if n < DS:
                scan_state(1, n)
            if n + 1 < DS:
                scan_drive(1, n + 1)
            if n == DS + 1:
                after_scan.append(Below(scan_to_ffn(1, scan_sum(1, DS - 1, False))))
            if after_scan:
                after_scan[0].advance()
            if n % 2 == 0 and n + 2 < DS:
                return lambda: [scan_decays(1, n + k) for k in (2, 3)]

        finished = run_ffn(0, [(c, 0) for c in range(FFN0_CHUNKS)], stored, xt_ready, {0: banks[2:4]}, scan_below)
        xt_ready[1], stored[1] = after_scan[0].finish()

        def ffn_to_attention(half, finished):
            added = yield from add_to_x(half, banks[2:4], finished, spare)
            return (yield from turn_and_split(half, layer_norm(half, added), spare))

        first_half = Below(ffn_to_attention(0, finished[0]))

        def first_half_below(i):
            first_half.advance()

        finished1 = run_ffn(0, [(c, 1) for c in range(FFN0_CHUNKS)], stored, xt_ready, {1: banks[2:4]},
                            first_half_below)

        ctx_rounded = act(lambda e: e.activation(ctx_hi[:, :], ctx_sb[:, :], ACT.Copy), [xt_ready[1]])
        ctx_ready = pool(lambda e: e.tensor_tensor(ctx_lo[:, :], ctx_sb[:, :], ctx_hi[:, :].bitcast(F32), ALU.subtract),
                         [ctx_rounded])
        bias_ready = dve(lambda e: e.tensor_scalar(
            mask_bias[:, :, :], mask_u8[:, :, :], 1.0, -MASKED, ALU.subtract, ALU.mult), [mask_in, xt_ready[1]])
        valid_ready = dve(lambda e: e.tensor_reduce(any_valid[:, :], mask_u8[:, :, :], AX_X, ALU.max), [mask_in])

        def attention(half, xt_half_ready, between):
            score_banks, prob_bank, head_bank = Ring(banks[4:6]), banks[6], banks[7]
            acc = banks[2:4]
            tok = slice(half * HT, (half + 1) * HT)
            units = [(kv, q, b) for kv in range(KV_HEADS) for q in range(GROUP) for b in range(HB)]
            keys, values, queries, heads = {}, {}, {}, {}
            proj_w = {}

            def evacuate(bank, slot, product):
                out_hi, out_lo = ([t[:, :] if len(t.shape) == 2 else t[:, :, :].rearrange("p a b -> p (a b)")
                                   for t in slot.t])
                hi = act(lambda e: e.activation(out_hi, bank.t[:, :], ACT.Copy), [product, *slot.readers])
                lo = dve(lambda e: e.tensor_tensor(out_lo, bank.t[:, :], out_hi.bitcast(F32), ALU.subtract),
                         [hi, *slot.readers])
                bank.readers = [hi, lo]
                slot.readers = []
                return slot, lo

            def project(kv, part):
                if kv >= KV_HEADS:
                    return
                if part == 0:
                    proj_w[kv] = split_weights("proj", half, kv)
                slot, w_ready = proj_w[kv]
                hi, lo = slot.t
                bank = spare.take()
                k_at = GROUP * WH * HD
                v_at = k_at + HD
                if part == 0:
                    product = pe(lambda e: product3(e, bank.t[:, :], hi[:, k_at:k_at + HD], lo[:, k_at:k_at + HD],
                                                    ctx_hi[:, tok], ctx_lo[:, tok], True, True),
                                 [w_ready, ctx_ready, *bank.readers])
                    keys[kv] = evacuate(bank, k_slots.take(), product)
                elif part == 2:
                    def multiply(e):
                        for j in range(HC):
                            at = slice(half * HT + j * P, half * HT + (j + 1) * P)
                            last = product3(e, bank.t[:, j * HD:(j + 1) * HD], ctx_hi[:, at], ctx_lo[:, at],
                                            hi[:, v_at:v_at + HD], lo[:, v_at:v_at + HD], True, True)
                        return last
                    product = pe(multiply, [w_ready, ctx_ready, *bank.readers])
                    values[kv] = evacuate(bank, v_slots.take(), product)
                else:
                    q = (part - 1) // 2

                    def multiply(e):
                        for w in range(WH):
                            at = slice((q * WH + w) * HD, (q * WH + w + 1) * HD)
                            last = product3(e, bank.t[:, :], hi[:, at], lo[:, at], xt_hi[half][:, w, :],
                                            xt_lo[half][:, w, :], w == 0, w == WH - 1)
                        return last
                    product = pe(multiply, [w_ready, xt_half_ready, *bank.readers])
                    queries[kv, q] = evacuate(bank, q_slots.take(), product)
                    if part == GROUP + 1:
                        slot.readers = [product]
                        xt_slots[half].readers = [product]

            shifted, softened, probs, probs_t = {}, {}, {}, {}

            def scores(i):
                kv, q, b = units[i]
                bank, sc, pr = score_banks.take(), score_slots.take(), prob_slots.take()
                (k_slot, k_ready), (q_slot, q_ready) = keys[kv], queries[kv, q]
                key_tok = slice(b * SEQ, (b + 1) * SEQ)

                def multiply(e):
                    for r in range(2):
                        at = slice(b * SEQ + r * P, b * SEQ + (r + 1) * P)
                        last = product3(e, bank.t[:, r * SEQ:(r + 1) * SEQ], q_slot.t[0][:, at], q_slot.t[1][:, at],
                                        k_slot.t[0][:, key_tok], k_slot.t[1][:, key_tok], True, True)
                    return last
                product = pe(multiply, [k_ready, q_ready, *bank.readers])
                q_slot.readers = [product]
                k_slot.readers = [product]
                row_max, row_bias = sc.extra
                batch = half * HB + b
                for r in range(2):
                    masked = dve(lambda e, r=r: e.tensor_tensor_reduce(
                        sc.t[:, r, :], bank.t[:, r * SEQ:(r + 1) * SEQ], mask_bias[:, batch, :], 1.0, -3.0e38,
                        ALU.add, ALU.max, row_max[:, r:r + 1]), [product, bias_ready, *sc.readers])
                bank.readers = [masked]
                shift = dve(lambda e: e.tensor_scalar(row_bias[:, :], row_max[:, :], -SCALE, None, ALU.mult), [masked])
                shifted[i] = (sc, pr, shift)

            def soften(i):
                sc, pr, shift = shifted.pop(i)
                row_max, row_bias = sc.extra
                row_sum, row_scale = pr.extra
                for r in range(2):
                    raised = act(lambda e, r=r: e.activation(pr.t[:, r, :], sc.t[:, r, :], ACT.Exp, scale=SCALE,
                                                             bias=row_bias[:, r:r + 1], accum_out=row_sum[:, r:r + 1]),
                                 [shift, *pr.readers])
                sc.readers = [raised]
                softened[i] = (pr, raised)

            def normalize(i):
                pr, raised = softened.pop(i)
                row_sum, row_scale = pr.extra
                batch = half * HB + units[i][2]
                inverse = dve(lambda e: e.reciprocal(row_scale[:, :], row_sum[:, :]), [raised])
                kept = pool(lambda e: e.tensor_tensor(row_scale[:, :], row_scale[:, :],
                                                      any_valid[:, batch:batch + 1].broadcast_to([P, 2]), ALU.mult),
                            [inverse, valid_ready])
                normed = pool(lambda e: e.tensor_tensor(pr.t[:, :, :], pr.t[:, :, :],
                                                        row_scale[:, :].unsqueeze(2).broadcast_to([P, 2, SEQ]),
                                                        ALU.mult), [kept])
                probs[i] = (pr, normed)

            def turn_probs(i):
                pr, normed = probs.pop(i)

                def turn(e):
                    for s in range(2):
                        for r in range(2):
                            last = e.transpose(prob_bank.t[:, s * SEQ + r * P:s * SEQ + (r + 1) * P],
                                               pr.t[:, r, s * P:(s + 1) * P], identity[:, :])
                    return last
                turned = pe(turn, [normed, ident_ready, *prob_bank.readers])
                pr.readers = [turned]
                probs_t[i] = evacuate(prob_bank, prob_t_slots.take(), turned)

            def head_output(i):
                kv, q, b = units[i]
                pt, pt_ready = probs_t.pop(i)
                v_slot, v_ready = values[kv]

                def multiply(e):
                    for s in range(2):
                        j = b * (SEQ // P) + s
                        last = product3(e, head_bank.t[:, b * SEQ:(b + 1) * SEQ], v_slot.t[0][:, j, :],
                                        v_slot.t[1][:, j, :], pt.t[0][:, s, :], pt.t[1][:, s, :], s == 0, s == 1)
                    return last
                before = head_bank.readers if b == 0 else []
                product = pe(multiply, [pt_ready, v_ready, *before])
                pt.readers = [product]
                v_slot.readers = [product]
                if b == HB - 1:
                    heads[i] = evacuate(head_bank, head_slots.take(), product)

            def project_out(i):
                kv, q, b = units[i]
                if b != HB - 1:
                    return None
                head, head_ready = heads.pop(i)
                slot, w_ready = split_weights("out", half, kv)
                first, final = (kv, q) == (0, 0), (kv, q) == (KV_HEADS - 1, GROUP - 1)

                def multiply(e):
                    for w in range(WH):
                        at = slice(q * WIDTH + w * P, q * WIDTH + (w + 1) * P)
                        last = product3(e, acc[w].t[:, :], slot.t[0][:, at], slot.t[1][:, at], head.t[0][:, :],
                                        head.t[1][:, :], first, final)
                    return last
                before = [r for bk in acc for r in bk.readers] if first else []
                product = pe(multiply, [head_ready, w_ready, *before])
                head.readers = [product]
                if q == GROUP - 1:
                    slot.readers = [product]
                return product

            for part in range(GROUP + 2):
                project(0, part)
            for i in range(len(units) + 4):
                if 0 <= i - 1 < len(units):
                    normalize(i - 1)
                if i < len(units):
                    scores(i)
                if 0 <= i - 2 < len(units):
                    turn_probs(i - 2)
                if 0 <= i - 3 < len(units):
                    head_output(i - 3)
                if 0 <= i - 4 < len(units):
                    product = project_out(i - 4)
                if i < len(units):
                    kv, q, b = units[i]
                    project(kv + 1, q * HB + b)
                    split_piece()
                    soften(i)
                between(i)
            return product

        pending = {}

        second_half = Below(ffn_to_attention(1, finished1[1]))
        second_half.advance()

        def norm_second_below(i):
            if i % 2 == 0:
                second_half.advance()

        attended = attention(0, first_half.finish(), norm_second_below)

        def attention_to_ffn(half, attended):
            added = yield from add_to_x(half, banks[2:4], attended, spare)
            return (yield from to_next_part(added, half, route_layer1))

        first_half = Below(attention_to_ffn(0, attended))
        first_half.advance()

        def norm_first_below(i):
            if i % 2 == 0:
                first_half.advance()

        attended1 = attention(1, second_half.finish(), norm_first_below)

        ahead = 3
        units = [(c, 0) for c in range(ahead)] + [(c, 1) for c in range(ahead)]
        units += [(c, h) for c in range(ahead, FFN1_CHUNKS) for h in range(HALVES)]
        xt_ready, stored = {}, {}
        xt_ready[0], stored[0] = first_half.finish()
        xt_ready[1], stored[1] = complete(attention_to_ffn(1, attended1))
        finished = run_ffn(1, units, stored, xt_ready, {0: banks[2:4], 1: banks[0:2]}, lambda i: None)
        last_ring = Ring(banks[4:8])
        for half in range(HALVES):
            acc = banks[2:4] if half == 0 else banks[0:2]
            added = complete(add_to_x(half, acc, finished[half], last_ring))
            for pair, step in enumerate(added):
                t = half * HC + 2 * pair
                stores.append(sp(lambda e, t=t: e.dma_start(out_dram[:, t:t + 2, :], x_tok[:, t:t + 2, :]), [step],
                                 lane(f"out_stored{t}", 16)))

        sp(lambda e: e.drain(), stores)

        for q in (pe, act, dve, pool, sp):
            for _, _, step in q.todo:
                counted = number_steps(step)
                step.value = counted

        block = stack.enter_context(nc.Block())

        @block.tensor
        def _(e):
            pe.run(e)

        @block.scalar
        def _(e):
            act.run(e)

        @block.vector
        def _(e):
            dve.run(e)

        @block.gpsimd
        def _(e):
            pool.run(e)

        @block.sync
        def _(e):
            sp.run(e)


def number_steps(step):
    lane = step.lane
    if step.value is None:
        count = 0
        for s in lane.steps:
            count += lane.weight if s.awaited else 0
            s.value = count
    return step.value


def kernel(**inputs):
    import numpy as np
    import concourse.bacc as bacc
    from concourse.bass_utils import run_bass_kernel_spmd

    a = {name: np.asarray(value) for name, value in inputs.items()}

    def wide(w):
        return w.reshape(-1, P, w.shape[-1]).transpose(1, 0, 2)

    def ffn_chunks(gate, up, down):
        n = gate.shape[1] // P
        sides = [wide(w).reshape(P, WH, n, P).transpose(2, 0, 1, 3).reshape(n, P, WIDTH) for w in (gate, up)]
        return np.concatenate([*sides, down.reshape(n, P, WIDTH)], axis=2)

    by_channel = [a[f"L0_xattn_{n}"].reshape(EH, P, -1).transpose(1, 0, 2)
                  for n in ("conv_w", "conv_b", "D", "dt_proj_b", "A_log")]
    ffn1_shared = ffn_chunks(a["L1_ffn_wg_s"], a["L1_ffn_wu_s"], a["L1_ffn_wd_s"])
    ffn1_routed = ffn_chunks(a["L1_ffn_wg"].transpose(1, 0, 2).reshape(WIDTH, E1 * I1),
                             a["L1_ffn_wu"].transpose(1, 0, 2).reshape(WIDTH, E1 * I1),
                             a["L1_ffn_wd"].reshape(E1 * I1, WIDTH))
    wq = wide(a["L1_xattn_Wq"]).reshape(P, WH, KV_HEADS, GROUP, HD).transpose(2, 0, 3, 1, 4)
    wk = a["L1_xattn_Wk"].reshape(CTX, KV_HEADS, HD).transpose(1, 0, 2)
    wv = a["L1_xattn_Wv"].reshape(CTX, KV_HEADS, HD).transpose(1, 0, 2)
    wo = a["L1_xattn_Wo"].reshape(KV_HEADS, GROUP, HD, WIDTH).transpose(0, 2, 1, 3)
    laid_out = {
        "x": a["x"],
        "ctx_t": a["ctx_1024"].reshape(TOKENS, CTX).T,
        "key_mask": a["mask_BxS2_bf1"].reshape(1, TOKENS),
        "in_proj_t": a["L0_xattn_in_proj_w"].T,
        "ssm_small": np.concatenate(by_channel, axis=2),
        "x_proj_t": wide(a["L0_xattn_x_proj_w"].T),
        "dt_proj_t": a["L0_xattn_dt_proj_w"].T,
        "gate_t": wide(a["L0_ffn_gate_w"].T),
        "centroids_t": wide(a["L1_ffn_centroids"].T),
        "gate_bias": a["L1_ffn_gate_bias"].reshape(1, E1),
        "ffn0_w": ffn_chunks(a["L0_ffn_w_gate_proj"].reshape(E0 * I0, WIDTH).T,
                             a["L0_ffn_w_up_proj"].reshape(E0 * I0, WIDTH).T,
                             a["L0_ffn_w_down_proj"].transpose(0, 2, 1).reshape(E0 * I0, WIDTH)),
        "attn_proj_w": np.concatenate([wq.reshape(KV_HEADS, P, -1), wk, wv], axis=2),
        "attn_out_w": wo.reshape(KV_HEADS, HD, WO_PIECE),
        "ffn1_w": np.concatenate([ffn1_shared, ffn1_routed], axis=0),
    }
    nc = bacc.Bacc("TRN2", target_bir_lowering=False, num_devices=1)
    arrays, args = {}, []
    for name, value in laid_out.items():
        value = np.ascontiguousarray(value)
        arrays[f"in_{name}"] = value
        args.append(nc.dram_tensor(f"in_{name}", value.shape, mybir.dt.from_np(value.dtype), kind="ExternalInput").ap())
    args.append(nc.dram_tensor("out", (BATCHES, SEQ, WIDTH), F32, kind="ExternalOutput").ap())
    build(nc, *args)
    result = run_bass_kernel_spmd(nc, [arrays], core_ids=[0])
    return result.results[0]["out"]
```

```python
from contextlib import ExitStack

import concourse.bass as bass
from concourse import mybir

F32 = mybir.dt.float32
F32R = mybir.dt.float32r
U8 = mybir.dt.uint8
U32 = mybir.dt.uint32
ALU = mybir.AluOpType
ACT = mybir.ActivationFunctionType
AX_X = mybir.AxisListType.X

P = 128
BATCHES, SEQ, WIDTH = 4, 256, 256
TOKENS = BATCHES * SEQ
CHUNKS = TOKENS // P
HALVES = 2
HT = TOKENS // HALVES
HC = CHUNKS // HALVES
HB = BATCHES // HALVES
WH = WIDTH // P
CTX = 128
DI, DS, DC, DR = 256, 16, 4, 8
EH = DI // P
E0, I0, TOP0 = 32, 96, 8
E1, I1, TOP1 = 16, 128, 2
SHARED = 2 * I1
SHARED_RATIO = 0.1
FFN0_CHUNKS = E0 * I0 // P
SHARED_CHUNKS = SHARED // P
FFN1_CHUNKS = SHARED_CHUNKS + E1
HEADS, KV_HEADS, HD = 16, 8, 128
GROUP = HEADS // KV_HEADS
SCALE = float(HD) ** -0.5
LN_EPS = 1e-5
TOP_EPS = 1e-9
MASKED = -1e30
PIECE = 3 * WIDTH
WO_PIECE = GROUP * WIDTH
SCANNED_BEFORE = 1
ALONE = 8


class Lane:

    def __init__(self, sem, weight=1):
        self.sem, self.weight, self.steps = sem, weight, []


class Step:

    def __init__(self, lane):
        self.lane, self.awaited, self.value = lane, lane.weight == 16, None
        lane.steps.append(self)


class Queue:

    def __init__(self, lane):
        self.lane, self.todo = lane, []

    def __call__(self, emit, after=(), lane=None):
        step = Step(lane or self.lane)
        after = [s for s in after if s is not None]
        for s in after:
            s.awaited = True
        self.todo.append((emit, after, step))
        return step

    def run(self, engine):
        reached = {}
        for emit, after, step in self.todo:
            need = {}
            for s in after:
                need[s.lane] = max(need.get(s.lane, 0), s.value)
            for lane, value in need.items():
                if reached.get(lane, 0) < value:
                    engine.wait_ge(lane.sem, value)
                    reached[lane] = value
            last = emit(engine)
            if step.awaited:
                last.then_inc(step.lane.sem, step.lane.weight)


class Slot:

    def __init__(self, t, extra=None):
        self.t, self.extra, self.readers = t, extra, []


class Ring:
    def __init__(self, slots):
        self.slots, self.n = slots, 0

    def take(self):
        slot = self.slots[self.n % len(self.slots)]
        self.n += 1
        return slot

    def peek(self):
        return self.slots[self.n % len(self.slots)]


def product3(e, out, w_hi, w_lo, m_hi, m_lo, first, last):
    e.matmul(out, w_hi, m_hi, start=first, stop=False)
    e.matmul(out, w_hi, m_lo, start=False, stop=False)
    return e.matmul(out, w_lo, m_hi, start=False, stop=last)


def complete(work):
    while True:
        try:
            next(work)
        except StopIteration as end:
            return end.value


class Below:

    def __init__(self, work):
        self.work, self.result = work, None

    def advance(self):
        if self.result is None:
            try:
                next(self.work)
            except StopIteration as end:
                self.result = end.value

    def finish(self):
        if self.result is None:
            self.result = complete(self.work)
        return self.result


def build(nc, x, ctx_t, key_mask, in_proj_t, ssm_small, x_proj_t, dt_proj_t, gate_t, centroids_t, gate_bias,
          ffn0_w, attn_proj_w, attn_out_w, ffn1_w, out):
    stack = ExitStack()
    with stack:
        def lane(name, weight=1):
            return Lane(stack.enter_context(nc.semaphore(name)), weight)

        pe = Queue(lane("tensor_steps"))
        act = Queue(lane("scalar_steps"))
        dve = Queue(lane("vector_steps"))
        pool = Queue(lane("gpsimd_steps"))
        sp = Queue(lane("sync_steps"))
        stores = []

        def load_once(name, dst, src, after=()):
            return sp(lambda e: e.dma_start(dst, src), after, lane("landed_" + name, 16))

        top = [(nc.sbuf_base + 63) // 64 * 64]

        def place(name, shape, dtype=F32):
            size = 1
            for n in shape[1:]:
                size *= n
            size *= 1 if dtype == U8 else 4
            t = nc.alloc_sbuf_tensor_at(name, shape, dtype, offset=top[0])
            top[0] += (size + 31) // 32 * 32
            return t

        identity = place("identity", [P, P])
        x_tok = place("x_tok", [P, CHUNKS, WIDTH])
        ctx_sb = place("ctx_sb", [P, TOKENS])
        in_proj_sb = place("in_proj_sb", [P, DI])
        small_sb = place("small_sb", [P, EH, DC + 3 + DS])
        x_proj_sb = place("x_proj_sb", [P, EH, DR + 2 * DS])
        dt_proj_sb = place("dt_proj_sb", [DR, DI])
        decay = place("decay", [P, EH, DS])
        gate_raw = place("gate_raw", [P, WH, E0])
        gate_hi = place("gate_hi", [P, WH, E0], F32R)
        gate_lo = place("gate_lo", [P, WH, E0], F32R)
        cent_raw = place("cent_raw", [P, WH, E1])
        cent_hi = place("cent_hi", [P, WH, E1], F32R)
        cent_lo = place("cent_lo", [P, WH, E1], F32R)
        bias_bc = place("bias_bc", [P, E1])
        expert_ids = place("expert_ids", [P, E1])
        half_power = place("half_power", [P, HC])
        mask_u8 = place("mask_u8", [P, BATCHES, SEQ], U8)
        any_valid = place("any_valid", [P, BATCHES])
        stats = place("stats", [P, HC, 6])
        mean_var = place("mean_var", [P, HC, 2])
        rstd = place("rstd", [P, HC])
        x_norm = place("x_norm", [P, HC, WIDTH])
        xt_hi = [place(f"xt_hi{h}", [P, WH, HT], F32R) for h in range(HALVES)]
        xt_lo = [place(f"xt_lo{h}", [P, WH, HT], F32R) for h in range(HALVES)]
        acc_sb = place("acc_sb", [P, WH, HT])
        logits = place("logits", [P, HC, E0])
        top8 = place("top8", [P, HC, 8])
        top_idx = place("top_idx", [P, HC, 8], U32)
        top_idx_f = place("top_idx_f", [P, HC, TOP1])
        route_a = place("route_a", [P, 2, HC, E0])
        route_w = place("route_w", [P, HC, E0])
        route_sum = place("route_sum", [P, HC])
        route_t = place("route_t", [E0, HT])
        raw_slots = Ring([Slot(place(f"w_raw{i}", [P, PIECE]), lane(f"landed_w_raw{i}", 16)) for i in range(3)])
        split_slots = Ring([Slot((place(f"w_hi{i}", [P, PIECE], F32R), place(f"w_lo{i}", [P, PIECE], F32R)))
                            for i in range(4)])
        gated_slots = Ring([Slot(place(f"gated{i}", [P, HT])) for i in range(2)])
        hidden_slots = Ring([Slot(place(f"hidden{i}", [P, HT])) for i in range(2)])
        hidden_split = Ring([Slot((place(f"hidden_hi{i}", [P, HT], F32R), place(f"hidden_lo{i}", [P, HT], F32R)))
                             for i in range(3)])
        mask_slots = Ring([Slot(place(f"route_bc{i}", [P, HT]), lane(f"landed_route_bc{i}", 16)) for i in range(4)])

        shared_region = top[0]
        starts = [top[0]]
        u_sb = place("u_sb", [P, HALVES, EH, HT])
        starts.append(top[0])
        delta = place("delta", [P, HALVES, EH, HT])
        starts.append(top[0])
        delta_u = place("delta_u", [P, HALVES, EH, HT])
        starts.append(top[0])
        z_gate = place("z_gate", [P, CHUNKS, WIDTH])
        x_dbl = place("x_dbl", [DR + 2 * DS, TOKENS])
        b_slots, c_slots = (Ring([Slot(place(f"{name}_rows{i}", [P, HT]), lane(f"landed_{name}{i}", 16))
                                  for i in range(3)]) for name in "bc")
        da_slots = Ring([Slot(place(f"decay_t{i}", [P, EH, HT])) for i in range(5)])
        conv_in_at = top[0]
        hc_slots = Ring([Slot(place(f"read_out{i}", [P, EH, HT])) for i in range(4)])
        h_slots = Ring([Slot(place(f"state{i}", [P, EH, HT])) for i in range(2)])
        dbu_slots = Ring([Slot(place(f"drive{i}", [P, EH, HT])) for i in range(2)])
        scan_end = top[0]
        top[0] = conv_in_at
        conv_in = place("conv_in", [P, EH, BATCHES, DC - 1 + SEQ])
        assert top[0] <= scan_end
        more_split = []
        for i in range(2):
            pair = []
            for k, part in enumerate(("hi", "lo")):
                top[0] = starts[2 * i + k]
                pair.append(place(f"w_more_{part}{i}", [P, PIECE], F32R))
                assert top[0] <= starts[2 * i + k] + EH * HT * 4
            more_split.append(Slot(tuple(pair)))

        top[0] = shared_region
        ctx_hi = place("ctx_hi", [P, TOKENS], F32R)
        ctx_lo = place("ctx_lo", [P, TOKENS], F32R)
        mask_bias = place("mask_bias", [P, BATCHES, SEQ])

        def split_pair(name, shape):
            return (place(name + "_hi", shape, F32R), place(name + "_lo", shape, F32R))

        k_slots = Ring([Slot(split_pair(f"k_t{i}", [P, HT])) for i in range(2)])
        v_slots = Ring([Slot(split_pair(f"v{i}", [P, HC, HD])) for i in range(2)])
        q_slots = Ring([Slot(split_pair(f"q_t{i}", [P, HT])) for i in range(4)])
        score_slots = Ring([Slot(place(f"scores{i}", [P, 2, SEQ]),
                                 (place(f"row_max{i}", [P, 2]), place(f"row_bias{i}", [P, 2]))) for i in range(2)])
        prob_slots = Ring([Slot(place(f"probs{i}", [P, 2, SEQ]),
                                (place(f"row_sum{i}", [P, 2]), place(f"row_scale{i}", [P, 2]))) for i in range(3)])
        prob_t_slots = Ring([Slot(split_pair(f"probs_t{i}", [P, 2, SEQ])) for i in range(2)])
        head_slots = Ring([Slot(split_pair(f"head_out{i}", [P, HT])) for i in range(2)])
        assert max(scan_end, top[0]) <= nc.sbuf_usable_end

        banks = [Slot(stack.enter_context(nc.psum_tensor(f"bank{i}", [P, 512], F32))) for i in range(8)]
        spare = Ring(banks[0:2])

        bc_dram = nc.dram_tensor("bc_scratch", (2 * DS, TOKENS), F32).ap()
        route_dram = [[nc.dram_tensor(f"route_scratch{layer}_{h}", (n, HT), F32).ap() for h in range(HALVES)]
                      for layer, n in ((0, E0), (1, E1))]

        def rows(src, p):
            return src.partition_broadcast(p).rearrange("p a n -> p (a n)")

        in_proj_in = load_once("in_proj", in_proj_sb[:, :], in_proj_t)
        ctx_in = [load_once(f"ctx{h}", ctx_sb[:, h * HT:(h + 1) * HT], ctx_t[:, h * HT:(h + 1) * HT])
                  for h in range(HALVES)]
        small_in = load_once("ssm_small", small_sb[:, :, :], ssm_small)
        x_dram = x.rearrange("b (c p) w -> p (b c) w", p=P)
        out_dram = out.rearrange("b (c p) w -> p (b c) w", p=P)
        x_in = [load_once(f"x{h}", x_tok[:, h * HC:(h + 1) * HC, :], x_dram[:, h * HC:(h + 1) * HC, :])
                for h in range(HALVES)]
        x_proj_in = load_once("x_proj", x_proj_sb[:, :, :], x_proj_t)
        dt_proj_in = load_once("dt_proj", dt_proj_sb[:, :], dt_proj_t)
        gate_in = load_once("gate", gate_raw[:, :, :], gate_t)
        cent_in = load_once("centroids", cent_raw[:, :, :], centroids_t)
        bias_in = load_once("gate_bias", bias_bc[:, :], rows(gate_bias, P))
        mask_in = load_once("key_mask", mask_u8[:, :, :].rearrange("p b s -> p (b s)"), rows(key_mask, P))

        conv_w = [small_sb[:, :, j] for j in range(DC)]
        conv_b, skip_d, dt_bias = (small_sb[:, :, DC + j] for j in range(3))
        a_log = small_sb[:, :, DC + 3:]

        ident_zero = pool(lambda e: e.memset(identity[:, :], 0.0))
        ident_ready = pool(lambda e: e.affine_select(
            out=identity[:, :], in_=identity[:, :], compare_op=ALU.not_equal, fill=1.0, base=0,
            pattern=[[-1, P]], channel_multiplier=1), [ident_zero])
        pad_ready = pool(lambda e: e.memset(conv_in[:, :, :, 0:DC - 1].rearrange("p h b s -> p (h b) s"), 0.0))
        power_ready = pool(lambda e: e.memset(half_power[:, :], -0.5))
        ids_ready = pool(lambda e: e.iota(expert_ids[:, :], pattern=[[1, E1]], base=0, channel_multiplier=0,
                                          allow_small_or_imprecise_dtypes=True))

        pieces = {("ffn0", h, c): ffn0_w[c] for h in range(HALVES) for c in range(FFN0_CHUNKS)}
        groups = [(h, kv) for h in range(HALVES) for kv in range(KV_HEADS)]
        for g, (h, kv) in enumerate(groups):
            pieces["proj", h, kv] = attn_proj_w[kv]
            if g > 0:
                pieces["out", *groups[g - 1]] = attn_out_w[groups[g - 1][1]]
        pieces["out", *groups[-1]] = attn_out_w[groups[-1][1]]
        pieces.update({("ffn1", 0, c): ffn1_w[c] for c in range(FFN1_CHUNKS)})
        pieces.update({("ffn1", 1, c): ffn1_w[c] for c in range(ALONE)})
        order = {key: n for n, key in enumerate(pieces)}
        pieces = list(pieces.values())
        fetched, pieces_split, split_ring = [], [], [split_slots]

        def fetch_piece():
            if len(fetched) < len(pieces):
                src = pieces[len(fetched)]
                slot = raw_slots.take()
                n = src.shape[-1]
                landed = sp(lambda e: e.dma_start(slot.t[:, 0:n], src), slot.readers, slot.extra)
                fetched.append((slot, n, landed))

        def more_split_slots():
            ring = Ring(split_ring[0].slots[:])
            ring.n = split_ring[0].n % len(ring.slots)
            ring.slots[ring.n:ring.n] = more_split
            split_ring[0] = ring

        def split_piece():
            if len(pieces_split) == FFN0_CHUNKS - 2:
                split_ring[0] = split_slots
            if len(pieces_split) == len(pieces) or split_ring[0].peek().readers is None:
                return
            if len(fetched) < len(pieces_split) + 3:
                fetch_piece()
            raw, n, landed = fetched[len(pieces_split)]
            slot = split_ring[0].take()
            hi, lo = slot.t
            rounded = act(lambda e: e.activation(hi[:, 0:n], raw.t[:, 0:n], ACT.Copy), [landed, *slot.readers])
            rest = pool(lambda e: e.tensor_tensor(lo[:, 0:n], raw.t[:, 0:n], hi[:, 0:n].bitcast(F32), ALU.subtract),
                        [landed, rounded, *slot.readers])
            raw.readers = [rounded, rest]
            slot.readers = None
            pieces_split.append((slot, rest))

        def split_weights(*key):
            while len(pieces_split) <= order[key]:
                done = len(pieces_split)
                split_piece()
                assert len(pieces_split) > done, "no slot is free"
            return pieces_split[order[key]]

        for _ in range(3):
            fetch_piece()

        def layer_norm(half, source):
            done = []
            for j in range(HC):
                t = half * HC + j
                done.append(dve(lambda e, j=j, t=t: e.bn_stats(stats[:, j, :], x_tok[:, t, :]),
                                [*source, *norm_slot.readers]))
            for j in range(HC):
                moments = dve(lambda e, j=j: e.bn_aggr(mean_var[:, j, :], stats[:, j, :]), [done[j]])
            variance = dve(lambda e: e.tensor_scalar(rstd[:, :], mean_var[:, :, 1], LN_EPS, None, ALU.add), [moments])
            scale = pool(lambda e: e.tensor_tensor(rstd[:, :], rstd[:, :], half_power[:, :], ALU.pow),
                         [variance, power_ready])
            yield
            normed = []
            for j in range(HC):
                t = half * HC + j
                normed.append(dve(lambda e, j=j, t=t: e.tensor_scalar(
                    x_norm[:, j, :], x_tok[:, t, :], mean_var[:, j, 0:1], rstd[:, j:j + 1], ALU.subtract, ALU.mult),
                    [scale, moments]))
            norm_slot.readers = [normed[-1]]
            return normed[-1]

        norm_slot = Slot(None)
        xt_slots = [Slot(None) for _ in range(HALVES)]

        def turn_and_split(half, normed, ring):
            yield
            for w in range(WH):
                bank = ring.take()

                def turn(e, w=w, bank=bank):
                    for j in range(HC):
                        last = e.transpose(bank.t[:, j * P:(j + 1) * P], x_norm[:, j, w * P:(w + 1) * P], identity[:, :])
                    return last
                turned = pe(turn, [normed, ident_ready, *bank.readers])
                hi = act(lambda e, w=w, bank=bank: e.activation(xt_hi[half][:, w, :], bank.t[:, :], ACT.Copy),
                         [turned, *xt_slots[half].readers])
                lo = dve(lambda e, w=w, bank=bank: e.tensor_tensor(
                    xt_lo[half][:, w, :], bank.t[:, :], xt_hi[half][:, w, :].bitcast(F32), ALU.subtract),
                    [turned, hi, *xt_slots[half].readers])
                bank.readers = [hi, lo]
                norm_slot.readers = [turned]
            xt_slots[half].readers = []
            return lo

        route_t_slot = Slot(None, lane("route_stored", 16))
        def router_logits(half, xt_ready, w_hi, w_lo, n, w_ready, ring):
            yield
            bank = ring.take()

            def multiply(e):
                for w in range(WH):
                    last = product3(e, bank.t[0:n, :], w_hi[:, w, :], w_lo[:, w, :], xt_hi[half][:, w, :],
                                    xt_lo[half][:, w, :], w == 0, w == WH - 1)
                return last
            product = pe(multiply, [xt_ready, w_ready, *bank.readers])
            moved = act(lambda e: e.activation(route_t[0:n, :], bank.t[0:n, :], ACT.Copy),
                        [product, *route_t_slot.readers])
            bank.readers = [moved]
            yield
            turned_bank = ring.take()

            def turn(e):
                for j in range(HC):
                    last = e.transpose(turned_bank.t[:, j * n:(j + 1) * n], route_t[0:n, j * P:(j + 1) * P],
                                       identity[0:n, 0:n])
                return last
            turned = pe(turn, [moved, ident_ready, *turned_bank.readers])
            route_t_slot.readers = [turned]
            return turned_bank, turned

        route_slot = Slot(None)

        def route_to_dram(layer, half, n, weighted, ring):
            yield
            bank = ring.take()

            def turn(e):
                for j in range(HC):
                    last = e.transpose(bank.t[0:n, j * P:(j + 1) * P], route_w[:, j, 0:n], identity[:, :])
                return last
            turned = pe(turn, [weighted, ident_ready, *bank.readers])
            copied = dve(lambda e: e.tensor_copy(route_t[0:n, :], bank.t[0:n, :]), [turned, *route_t_slot.readers])
            bank.readers = [copied]
            route_slot.readers = [turned]
            stored = sp(lambda e: e.dma_start(route_dram[layer][half], route_t[0:n, :]), [copied], route_t_slot.extra)
            route_t_slot.readers = [stored]
            stores.append(stored)
            return stored

        def route_layer0(half, xt_ready, ring):
            bank, product = yield from router_logits(half, xt_ready, gate_hi, gate_lo, E0, gate_ready, ring)
            kept = dve(lambda e: e.tensor_copy(logits[:, :, :], bank.t[:, 0:HC * E0].rearrange("p (j n) -> p j n", j=HC)),
                       [product, *route_slot.readers])
            bank.readers = [kept]
            for j in range(HC):
                best = dve(lambda e, j=j: e.max(out=top8[:, j, :], in_=logits[:, j, :]), [kept, *route_slot.readers])
            for j in range(HC):
                taken = dve(lambda e, j=j: e.match_replace(out=route_a[:, 1, j, :], in_to_replace=top8[:, j, :],
                                                           in_values=logits[:, j, :], imm_value=MASKED), [best])
            row_max = top8[:, :, 0:1].broadcast_to([P, HC, E0])
            dve(lambda e: e.tensor_tensor(route_a[:, 0, :, :], logits[:, :, :], row_max, ALU.subtract), [best])
            shifted = dve(lambda e: e.tensor_tensor(route_a[:, 1, :, :], route_a[:, 1, :, :], row_max, ALU.subtract),
                          [taken])
            flat = route_a[:, :, :, :].rearrange("p a j n -> p (a j n)")
            raised = act(lambda e: e.activation(flat, flat, ACT.Exp), [shifted])
            picked = dve(lambda e: e.tensor_tensor(route_w[:, :, :], route_a[:, 0, :, :], route_a[:, 1, :, :],
                                                   ALU.subtract), [raised])
            summed = dve(lambda e: e.tensor_reduce(route_sum[:, :], route_w[:, :, :], AX_X, ALU.add), [picked])
            inverse = dve(lambda e: e.reciprocal(route_sum[:, :], route_sum[:, :]), [summed])
            weighted = dve(lambda e: e.tensor_tensor(
                route_w[:, :, :], route_w[:, :, :], route_sum[:, :].unsqueeze(2).broadcast_to([P, HC, E0]), ALU.mult),
                [inverse])
            return (yield from route_to_dram(0, half, E0, weighted, ring))

        def route_layer1(half, xt_ready, ring):
            bank, product = yield from router_logits(half, xt_ready, cent_hi, cent_lo, E1, cent_ready, ring)
            aff = logits[:, :, 0:E1]
            biased = route_a[:, 0, :, 0:E1]
            affinity = act(lambda e: e.activation(aff, bank.t[:, 0:HC * E1].rearrange("p (j n) -> p j n", j=HC),
                                                  ACT.Sigmoid), [product, *route_slot.readers])
            bank.readers = [affinity]
            ranked = dve(lambda e: e.tensor_tensor(biased, aff, bias_bc[:, :].unsqueeze(1).broadcast_to([P, HC, E1]),
                                                   ALU.add), [affinity, bias_in])
            for j in range(HC):
                best = dve(lambda e, j=j: e.max(out=top8[:, j, :], in_=route_a[:, 0, j, 0:E1]),
                           [ranked, *route_slot.readers])
            for j in range(HC):
                found = dve(lambda e, j=j: e.max_index(top_idx[:, j, :], top8[:, j, :], route_a[:, 0, j, 0:E1]), [best])
            index_f = dve(lambda e: e.tensor_copy(top_idx_f[:, :, :], top_idx[:, :, 0:TOP1]), [found])
            for k in range(TOP1):
                for j in range(HC):
                    chosen = dve(lambda e, k=k, j=j: e.scalar_tensor_tensor(
                        out=route_a[:, k, j, E1:2 * E1], in0=expert_ids[:, :], scalar=top_idx_f[:, j, k:k + 1],
                        in1=logits[:, j, 0:E1], op0=ALU.is_equal, op1=ALU.mult), [index_f, ids_ready])
            both = dve(lambda e: e.tensor_tensor(route_w[:, :, 0:E1], route_a[:, 0, :, E1:2 * E1],
                                                 route_a[:, 1, :, E1:2 * E1], ALU.add), [chosen])
            summed = dve(lambda e: e.tensor_reduce(route_sum[:, :], route_w[:, :, 0:E1], AX_X, ALU.add), [both])
            guarded = dve(lambda e: e.tensor_scalar(route_sum[:, :], route_sum[:, :], TOP_EPS, None, ALU.add), [summed])
            inverse = dve(lambda e: e.reciprocal(route_sum[:, :], route_sum[:, :]), [guarded])
            weighted = dve(lambda e: e.tensor_tensor(
                route_w[:, :, 0:E1], route_w[:, :, 0:E1], route_sum[:, :].unsqueeze(2).broadcast_to([P, HC, E1]),
                ALU.mult), [inverse])
            return (yield from route_to_dram(1, half, E1, weighted, ring))

        acc_slot = Slot(None)

        def add_to_x(half, acc_banks, finished, ring):
            copies = []
            for w in range(WH):
                engine = (act, dve)[w]
                emit = ((lambda e, w=w: e.activation(acc_sb[:, w, :], acc_banks[w].t[:, :], ACT.Copy)),
                        (lambda e, w=w: e.tensor_copy(acc_sb[:, w, :], acc_banks[w].t[:, :])))[w]
                copies.append(engine(emit, [finished, *acc_slot.readers]))
                acc_banks[w].readers = [copies[w]]
            yield
            added = []
            for pair in range(HC // 2):
                bank = ring.take()

                def turn(e, pair=pair, bank=bank):
                    for j in range(2):
                        tok = slice((2 * pair + j) * P, (2 * pair + j + 1) * P)
                        for w in range(WH):
                            last = e.transpose(bank.t[:, j * WIDTH + w * P:j * WIDTH + (w + 1) * P],
                                               acc_sb[:, w, tok], identity[:, :])
                    return last
                turned = pe(turn, [*copies, ident_ready, *bank.readers])
                t = half * HC + 2 * pair
                added.append(dve(lambda e, t=t, bank=bank: e.tensor_tensor(
                    x_tok[:, t:t + 2, :].rearrange("p t w -> p (t w)"),
                    x_tok[:, t:t + 2, :].rearrange("p t w -> p (t w)"), bank.t[:, :], ALU.add), [turned]))
                bank.readers = [added[-1]]
                acc_slot.readers = [turned]
            return added

        y_banks = banks[0:EH]
        decays = {}

        def scan_decays(half, n):
            slot = da_slots.take()
            for c in range(EH):
                last = act(lambda e, c=c: e.activation(
                    slot.t[:, c, :].rearrange("p (b s) -> p b s", b=HB)[:, :, 1:],
                    delta[:, half, c, :].rearrange("p (b s) -> p b s", b=HB)[:, :, 1:],
                    ACT.Exp, scale=decay[:, c, n:n + 1]), [delta_ready[half][0], decay_ready, *slot.readers])
            decays[half, n] = (slot, last)

        b_tiles, c_tiles = {}, {}

        def load_row(half, n, row, ring, tiles):
            if n < DS:
                slot = ring.take()
                src = rows(bc_dram[row:row + 1, half * HT:(half + 1) * HT], P)
                tiles[half, n] = (slot, sp(lambda e: e.dma_start(slot.t[:, :], src),
                                           [bc_stored[half], *slot.readers], slot.extra))

        def load_b(half, n):
            load_row(half, n, n, b_slots, b_tiles)

        def load_c(half, n):
            load_row(half, n, DS + n, c_slots, c_tiles)

        drives, read_outs = {}, {}

        def scan_drive(half, n):
            if n >= DS:
                return
            b, b_in = b_tiles.pop((half, n))
            dbu = dbu_slots.take()
            b_row = b.t[:, :].unsqueeze(1).broadcast_to([P, EH, HT])
            drive = pool(lambda e: e.tensor_tensor(dbu.t[:, :, :], delta_u[:, half, :, :], b_row, ALU.mult),
                         [b_in, delta_ready[half][1], *dbu.readers])
            b.readers = [drive]
            drives[half, n] = (dbu, drive)
            load_b(half, n + 3)

        def scan_state(half, n):
            c, c_in = c_tiles.pop((half, n))
            da, da_ready = decays.pop((half, n))
            dbu, drive = drives.pop((half, n))
            h, hc = h_slots.take(), hc_slots.take()
            c_row = c.t[:, :].unsqueeze(1).broadcast_to([P, EH, HT])
            flat = [s.t[:, :, :].rearrange("p c s -> p (c s)") for s in (da, dbu, h)]
            state = dve(lambda e: e.tensor_tensor_scan(flat[2], flat[0], flat[1], 0.0, ALU.mult, ALU.add),
                        [drive, da_ready, *h.readers])
            da.readers, dbu.readers = [state], [state]
            yield
            read = dve(lambda e: e.tensor_tensor(hc.t[:, :, :], h.t[:, :, :], c_row, ALU.mult),
                       [state, c_in, *hc.readers])
            h.readers = [read]
            c.readers = [read]
            load_c(half, n + 3)
            read_outs[half, n] = (hc, read)

        def scan_add(half, n):
            other, other_ready = read_outs.pop((half, n - 1))
            hc, ready = read_outs[half, n]
            both = dve(lambda e: e.tensor_tensor(hc.t[:, :, :], hc.t[:, :, :], other.t[:, :, :], ALU.add),
                       [ready, other_ready])
            other.readers = [both]
            read_outs[half, n] = (hc, both)

        def scan_sum(half, n, first):
            hc, ready = read_outs.pop((half, n))

            def accumulate(e):
                for c in range(EH):
                    last = e.matmul(y_banks[c].t[:, :], identity[:, :], hc.t[:, c, :], start=first, stop=n == DS - 1)
                return last
            before = [r for b in y_banks for r in b.readers] if first else []
            summed = pe(accumulate, [ready, ident_ready, *before])
            hc.readers = [summed]
            return summed

        def scan_finish(half, summed):
            y = hc_slots.take()
            for c in range(EH):
                with_skip = dve(lambda e, c=c: e.scalar_tensor_tensor(
                    out=y.t[:, c, :], in0=u_sb[:, half, c, :], scalar=skip_d[:, c:c + 1], in1=y_banks[c].t[:, :],
                    op0=ALU.mult, op1=ALU.add), [summed, *y.readers])
                y_banks[c].readers = [with_skip]
            z = z_gate[:, half * HC:(half + 1) * HC, :].rearrange("p (b c) s -> p c b s", c=EH)
            gated = dve(lambda e: e.tensor_tensor(y.t[:, :, :].rearrange("p c (b s) -> p c b s", b=HB),
                                                  y.t[:, :, :].rearrange("p c (b s) -> p c b s", b=HB), z, ALU.mult),
                        [with_skip, z_ready[half]])
            yield
            added = []
            for b in range(HB):
                bank = spare.take()

                def turn(e, b=b, bank=bank):
                    for l in range(SEQ // P):
                        for c in range(EH):
                            at = b * SEQ + l * P
                            last = e.transpose(bank.t[:, l * DI + c * P:l * DI + (c + 1) * P],
                                               y.t[:, c, at:at + P], identity[:, :])
                    return last
                turned = pe(turn, [gated, ident_ready, *bank.readers])
                t = half * HC + b * (SEQ // P)
                added.append(dve(lambda e, t=t, bank=bank: e.tensor_tensor(
                    x_tok[:, t:t + 2, :].rearrange("p t w -> p (t w)"),
                    x_tok[:, t:t + 2, :].rearrange("p t w -> p (t w)"), bank.t[:, :], ALU.add), [turned]))
                bank.readers = [added[-1]]
            y.readers = [turned]
            return added

        before_ffn = Ring(banks[EH:])
        conv_ready, u_ready, z_ready, bc_stored, x_dbl_ready, delta_ready = {}, {}, {}, {}, {}, {}

        def project_and_convolve(half):
            for c in range(EH):
                bank = before_ffn.take()
                projected = pe(lambda e, c=c, bank=bank: e.matmul(
                    bank.t[:, :], in_proj_sb[:, c * P:(c + 1) * P], ctx_sb[:, half * HT:(half + 1) * HT],
                    start=True, stop=True), [ctx_in[half], in_proj_in, *bank.readers])
                moved = act(lambda e, c=c, bank=bank: e.activation(
                    conv_in[:, c, half * HB:(half + 1) * HB, DC - 1:],
                    bank.t[:, :].rearrange("p (b s) -> p b s", b=HB), ACT.Copy), [projected])
                bank.readers = [moved]
                conv_out = u_sb[:, half, c, :].rearrange("p (b s) -> p b s", b=HB)
                taps = [conv_in[:, c, half * HB:(half + 1) * HB, j:j + SEQ] for j in range(DC)]
                step = dve(lambda e, c=c, taps=taps, conv_out=conv_out: e.tensor_scalar(
                    conv_out, taps[0], conv_w[0][:, c:c + 1], None, ALU.mult), [moved, pad_ready, small_in])
                for j in range(1, DC):
                    step = dve(lambda e, c=c, j=j, taps=taps, conv_out=conv_out: e.scalar_tensor_tensor(
                        out=conv_out, in0=taps[j], scalar=conv_w[j][:, c:c + 1], in1=conv_out,
                        op0=ALU.mult, op1=ALU.add), [step])
                conv_ready[half, c] = step
                yield

        def activate_u(half):
            for c in range(EH):
                u_ready[half] = act(lambda e, c=c: e.activation(
                    u_sb[:, half, c, :], u_sb[:, half, c, :], ACT.Silu, bias=conv_b[:, c:c + 1]),
                    [conv_ready[half, c]])

        def activate_z(half, normed):
            z_ready[half] = act(lambda e: e.activation(
                z_gate[:, half * HC:(half + 1) * HC, :], x_norm[:, :, :], ACT.Silu), [normed])
            norm_slot.readers = [z_ready[half]]

        def project_x_dbl(half):
            bank = before_ffn.take()
            tok = slice(half * HT, (half + 1) * HT)

            def multiply(e):
                for c in range(EH):
                    last = e.matmul(bank.t[0:DR + 2 * DS, :], x_proj_sb[:, c, :], u_sb[:, half, c, :],
                                    start=c == 0, stop=c == EH - 1)
                return last
            product = pe(multiply, [x_proj_in, u_ready[half], *bank.readers])
            x_dbl_ready[half] = act(lambda e: e.activation(x_dbl[:, tok], bank.t[0:DR + 2 * DS, :], ACT.Copy),
                                    [product])
            bank.readers = [x_dbl_ready[half]]

        def store_bc(half):
            tok = slice(half * HT, (half + 1) * HT)
            bc_stored[half] = sp(lambda e: e.dma_start(bc_dram[:, tok], x_dbl[DR:, tok]), [x_dbl_ready[half]],
                                 lane(f"bc_stored{half}", 16))
            stores.append(bc_stored[half])

        def make_delta(half, s_buf, s_slot):
            products = []
            for c in range(EH):
                bank = before_ffn.take()
                product = pe(lambda e, c=c, bank=bank: e.matmul(
                    bank.t[:, :], dt_proj_sb[:, c * P:(c + 1) * P], x_dbl[0:DR, half * HT:(half + 1) * HT],
                    start=True, stop=True), [x_dbl_ready[half], dt_proj_in, *bank.readers])
                away = act(lambda e, c=c, bank=bank: e.activation(
                    s_buf[:, c, :], bank.t[:, :], ACT.Abs, bias=dt_bias[:, c:c + 1]), [product, *s_slot.readers])
                products.append((bank, away))
            yield
            for c, (bank, away) in enumerate(products):
                floor = dve(lambda e, c=c, bank=bank: e.tensor_scalar(
                    delta[:, half, c, :], bank.t[:, :], dt_bias[:, c:c + 1], 0.0, ALU.add, ALU.max), [away])
                bank.readers = [floor]
            yield
            s_all = s_buf.rearrange("p c s -> p (c s)")
            d_all, one_all, u_all = (t[:, half, :, :].rearrange("p c s -> p (c s)") for t in (delta, delta_u, u_sb))
            log_all = acc_sb[:, :, :].rearrange("p c s -> p (c s)")
            raised = act(lambda e: e.activation(s_all, s_all, ACT.Exp, scale=-1.0), [away])
            logged = act(lambda e: e.activation(log_all, s_all, ACT.Ln, bias=1.0), [raised, *acc_slot.readers])
            yield
            plus = dve(lambda e: e.tensor_scalar(one_all, s_all, 1.0, None, ALU.add), [raised])
            excess = dve(lambda e: e.scalar_tensor_tensor(out=one_all, in0=one_all, scalar=1.0, in1=s_all,
                                                          op0=ALU.subtract, op1=ALU.subtract), [plus])
            log1p = dve(lambda e: e.tensor_tensor(log_all, log_all, one_all, ALU.subtract), [logged, excess])
            ready = dve(lambda e: e.tensor_tensor(d_all, d_all, log_all, ALU.add), [log1p, floor])
            engine = dve if half == 0 else pool
            driven = engine(lambda e: e.tensor_tensor(delta_u[:, half, :, :].rearrange("p c s -> p (c s)"), d_all, u_all,
                                                   ALU.mult), [ready, u_ready[half]])
            delta_ready[half] = (ready, driven)
            s_slot.readers = [logged, excess]
            acc_slot.readers = [ready]

        complete(project_and_convolve(0))
        activate_u(0)
        project_x_dbl(0)
        store_bc(0)
        for n in range(3):
            load_b(0, n)
            load_c(0, n)
        a_exp = act(lambda e: e.activation(decay[:, :, :], a_log, ACT.Exp), [small_in])
        delta0 = make_delta(0, da_slots.slots[-1].t[:, :, :], da_slots.slots[-1])
        next(delta0)
        next(delta0)
        convolution1 = project_and_convolve(1)
        next(convolution1)
        decay_ready = dve(lambda e: e.tensor_scalar(decay[:, :, :], decay[:, :, :], -1.0, None, ALU.mult), [a_exp])
        complete(delta0)
        complete(convolution1)
        for slot in hc_slots.slots + h_slots.slots:
            slot.readers = [conv_ready[1, EH - 1]]
        for slot in da_slots.slots:
            slot.readers = [pool(lambda e, slot=slot: e.memset(
                slot.t[:, :, :].rearrange("p c (b s) -> p (c b) s", b=HB)[:, :, 0:1], 0.0), slot.readers)]

        def split_small(raw, hi, lo, landed):
            rounded = dve(lambda e: e.tensor_copy(hi[:, :, :], raw[:, :, :]), [landed])
            return dve(lambda e: e.tensor_tensor(lo[:, :, :], raw[:, :, :], hi[:, :, :].bitcast(F32), ALU.subtract),
                       [rounded])

        gate_ready = split_small(gate_raw, gate_hi, gate_lo, gate_in)
        cent_ready = split_small(cent_raw, cent_hi, cent_lo, cent_in)

        def ffn0_segments(c):
            at, end = c * P, (c + 1) * P
            while at < end:
                n = min(end, (at // I0 + 1) * I0) - at
                yield at // I0, at - c * P, n
                at += n

        def load_route(layer, half, c, stored):
            slot = mask_slots.take()
            parts = list(ffn0_segments(c)) if layer == 0 else [(c - SHARED_CHUNKS, 0, P)]
            for expert, at, n in parts:
                landed = sp(lambda e, expert=expert, at=at, n=n: e.dma_start(
                    slot.t[at:at + n, :], rows(route_dram[layer][half][expert:expert + 1, :], n)),
                    [stored, *slot.readers], slot.extra)
            return slot, landed

        def run_ffn(layer, units, stored, xt_ready, acc_of, between, finished):
            gu = Ring([(banks[4], banks[5]), (banks[6], banks[7])])
            first_done, waiting, routes = set(), [], {}

            def need_route(i):
                if i < len(units) and not (layer == 1 and units[i][0] < SHARED_CHUNKS):
                    c, half = units[i]
                    if i not in routes and half in stored:
                        routes[i] = load_route(layer, half, c, stored[half])

            def shares(i):
                return 0 < i < len(units) and units[i][0] == units[i - 1][0]

            def down(i, slot, half, split, hidden_ready):
                hi, lo = slot.t
                first = half not in first_done
                first_done.add(half)
                final = i == max(k for k, u in enumerate(units) if u[1] == half)

                def multiply(e):
                    for w in range(WH):
                        at = slice(2 * WIDTH + w * P, 2 * WIDTH + (w + 1) * P)
                        last = product3(e, acc_of[half][w].t[:, :], hi[:, at], lo[:, at], split.t[0][:, :],
                                        split.t[1][:, :], first, final)
                    return last
                before = [r for b in acc_of[half] for r in b.readers] if first else []
                done = pe(multiply, [hidden_ready, *before])
                split.readers = [done]
                if not shares(i + 1):
                    slot.readers = [done]
                if final:
                    finished[half] = done

            for i in range(2):
                need_route(i)
            for i, (c, half) in enumerate(units):
                if not shares(i):
                    key = (f"ffn{layer}", half, c)
                    slot, w_ready = split_weights(*key)
                hi, lo = slot.t
                g_bank, u_bank = gu.take()
                both = []
                for k, bank in enumerate((g_bank, u_bank)):
                    def multiply(e, k=k, bank=bank, hi=hi, lo=lo, half=half):
                        for w in range(WH):
                            at = slice(k * WIDTH + w * P, k * WIDTH + (w + 1) * P)
                            last = product3(e, bank.t[:, :], hi[:, at], lo[:, at], xt_hi[half][:, w, :],
                                            xt_lo[half][:, w, :], w == 0, w == WH - 1)
                        return last
                    both.append(pe(multiply, [w_ready, xt_ready[half], *bank.readers]))
                xt_slots[half].readers = [both[-1]]
                if len(waiting) == 2:
                    down(*waiting.pop(0))
                for later in (i + 1, i + 2):
                    need_route(later)
                gated, hidden, split = gated_slots.take(), hidden_slots.take(), hidden_split.take()
                silu = act(lambda e, g=gated, b=g_bank: e.activation(g.t[:, :], b.t[:, :], ACT.Silu),
                           [both[0], *gated.readers])
                g_bank.readers = [silu]
                if i in routes:
                    up = dve(lambda e, g=gated, h=hidden, b=u_bank: e.tensor_tensor(
                        h.t[:, :], g.t[:, :], b.t[:, :], ALU.mult), [silu, both[1], *hidden.readers])
                    route, route_in = routes.pop(i)
                    made = dve(lambda e, h=hidden, r=route: e.tensor_tensor(
                        h.t[:, :], h.t[:, :], r.t[:, :], ALU.mult), [up, route_in])
                    route.readers = [made]
                else:
                    up = made = dve(lambda e, g=gated, h=hidden, b=u_bank: e.scalar_tensor_tensor(
                        out=h.t[:, :], in0=g.t[:, :], scalar=SHARED_RATIO, in1=b.t[:, :], op0=ALU.mult,
                        op1=ALU.mult), [silu, both[1], *hidden.readers])
                u_bank.readers = [up]
                gated.readers = [up]
                if len(pieces_split) <= order[key] + 3:
                    split_piece()
                below = between(i)
                if below:
                    next(below, None)
                rounded = act(lambda e, h=hidden, s=split: e.activation(s.t[0][:, :], h.t[:, :], ACT.Copy),
                              [made, *split.readers])
                rest = dve(lambda e, h=hidden, s=split: e.tensor_tensor(
                    s.t[1][:, :], h.t[:, :], s.t[0][:, :].bitcast(F32), ALU.subtract), [rounded, *split.readers])
                hidden.readers = [rounded, rest]
                waiting.append((i, slot, half, split, rest))
                if below:
                    complete(below)
            for unit in waiting:
                down(*unit)

        for n in range(4):
            scan_decays(0, n)
        scan_drive(0, 0)
        for n in range(DS):
            scan_drive(0, n + 1)
            complete(scan_state(0, n))
            summed = scan_sum(0, n, n == 0)
            if n + 4 < DS:
                scan_decays(0, n + 4)
            if n == 0:
                norm0 = layer_norm(0, [x_in[0]])
                next(norm0)
            if n == 1:
                activate_z(0, complete(norm0))
                activate_u(1)
            if n == 2:
                project_x_dbl(1)
            if n == 3:
                norm1 = layer_norm(1, [x_in[1]])
                next(norm1)
            if n == 4:
                activate_z(1, complete(norm1))
            if n == 6:
                store_bc(1)
                delta1 = make_delta(1, x_norm[:, :, :].rearrange("p (c a) w -> p c (a w)", c=EH), norm_slot)
                next(delta1)
            if n in (7, 8):
                next(delta1)
        split_piece()
        split_piece()

        def to_next_part(added, half, router):
            normed = yield from layer_norm(half, added)
            xt = yield from turn_and_split(half, normed, spare)
            stored = yield from router(half, xt, spare)
            return xt, stored

        def scan_to_ffn(half, summed):
            added = yield from scan_finish(half, summed)
            return (yield from to_next_part(added, half, route_layer0))

        xt_ready, stored = {}, {}
        added = complete(scan_finish(0, summed))
        for slot in more_split:
            slot.readers = [added[-1]]
        more_split_slots()
        for n in range(3):
            load_b(1, n)
            load_c(1, n)
        way = to_next_part(added, 0, route_layer0)
        next(way)
        split_piece()
        split_piece()
        next(way)
        next(way)
        complete(delta1)
        scan_drive(1, 0)
        next(way)
        scan_decays(1, 0)
        scan_decays(1, 1)
        xt_ready[0], stored[0] = complete(way)
        scan_decays(1, 2)
        scan_decays(1, 3)
        complete(scan_state(1, 0))
        scan_drive(1, 1)
        after_scan = []

        def scan_below(i):
            n = i + SCANNED_BEFORE
            if n % 2 == 0 and n + 2 < DS:
                scan_decays(1, n + 2)
                scan_decays(1, n + 3)
            if n > 1 and n % 2 == 0 and n <= DS:
                scan_add(1, n - 1)
            if n > 2 and n % 2 == 1 and n <= DS:
                scan_sum(1, n - 2, n == 3)
            if n < DS:
                state = scan_state(1, n)
                next(state)
                yield
                complete(state)
            else:
                yield
            if n + 1 < DS:
                scan_drive(1, n + 1)
            if n == DS + 1:
                after_scan.append(Below(scan_to_ffn(1, scan_sum(1, DS - 1, False))))
            if after_scan and 1 not in xt_ready:
                after_scan[0].advance()
                if after_scan[0].result:
                    xt_ready[1], stored[1] = after_scan[0].result

        def ffn_to_attention(half, ring):
            added = yield from add_to_x(half, banks[2:4], finished[half], ring)
            normed = yield from layer_norm(half, added)
            return (yield from turn_and_split(half, normed, spare))

        after_ffn, context_split = {}, []

        def below_ffn0(i):
            if i < FFN0_CHUNKS:
                yield from scan_below(i)
            if 0 in finished:
                if 0 not in after_ffn:
                    after_ffn[0] = Below(ffn_to_attention(0, spare))
                after_ffn[0].advance()
            if i == 2 * FFN0_CHUNKS - 8:
                context_split.append(split_context())

        def split_context():
            rounded = act(lambda e: e.activation(ctx_hi[:, :], ctx_sb[:, :], ACT.Copy), [xt_ready[1]])
            ctx_ready = pool(lambda e: e.tensor_tensor(ctx_lo[:, :], ctx_sb[:, :], ctx_hi[:, :].bitcast(F32),
                                                       ALU.subtract), [rounded])
            bias_ready = dve(lambda e: e.tensor_scalar(
                mask_bias[:, :, :], mask_u8[:, :, :], 1.0, -MASKED, ALU.subtract, ALU.mult), [mask_in, xt_ready[1]])
            valid_ready = dve(lambda e: e.tensor_reduce(any_valid[:, :], mask_u8[:, :, :], AX_X, ALU.max), [mask_in])
            return ctx_ready, bias_ready, valid_ready

        finished = {}
        run_ffn(0, [(c, h) for h in range(HALVES) for c in range(FFN0_CHUNKS)], stored, xt_ready,
                {h: banks[2:4] for h in range(HALVES)}, below_ffn0, finished)

        ctx_ready, bias_ready, valid_ready = context_split[0]

        def attention(xt_of, between):
            score_banks, prob_bank, head_bank = Ring(banks[4:6]), banks[6], banks[7]
            acc = banks[2:4]
            units = [(half, kv, q, b) for half, kv in groups for q in range(GROUP) for b in range(HB)]
            keys, values, queries, heads = {}, {}, {}, {}
            proj_w = {}

            def evacuate(bank, slot, product):
                out_hi, out_lo = ([t[:, :] if len(t.shape) == 2 else t[:, :, :].rearrange("p a b -> p (a b)")
                                   for t in slot.t])
                hi = act(lambda e: e.activation(out_hi, bank.t[:, :], ACT.Copy), [product, *slot.readers])
                lo = dve(lambda e: e.tensor_tensor(out_lo, bank.t[:, :], out_hi.bitcast(F32), ALU.subtract),
                         [hi, *slot.readers])
                bank.readers = [hi, lo]
                slot.readers = []
                return slot, lo

            def project(g, part):
                if g >= len(groups):
                    return
                half, kv = groups[g]
                tok = slice(half * HT, (half + 1) * HT)
                if part == 0:
                    proj_w[g] = split_weights("proj", half, kv)
                slot, w_ready = proj_w[g]
                hi, lo = slot.t
                bank = spare.take()
                k_at = GROUP * WH * HD
                v_at = k_at + HD
                if part == 0:
                    product = pe(lambda e: product3(e, bank.t[:, :], hi[:, k_at:k_at + HD], lo[:, k_at:k_at + HD],
                                                    ctx_hi[:, tok], ctx_lo[:, tok], True, True),
                                 [w_ready, ctx_ready, *bank.readers])
                    keys[half, kv] = evacuate(bank, k_slots.take(), product)
                elif part == 2:
                    def multiply(e):
                        for j in range(HC):
                            at = slice(half * HT + j * P, half * HT + (j + 1) * P)
                            last = product3(e, bank.t[:, j * HD:(j + 1) * HD], ctx_hi[:, at], ctx_lo[:, at],
                                            hi[:, v_at:v_at + HD], lo[:, v_at:v_at + HD], True, True)
                        return last
                    product = pe(multiply, [w_ready, ctx_ready, *bank.readers])
                    values[half, kv] = evacuate(bank, v_slots.take(), product)
                else:
                    q = (part - 1) // 2

                    def multiply(e):
                        for w in range(WH):
                            at = slice((q * WH + w) * HD, (q * WH + w + 1) * HD)
                            last = product3(e, bank.t[:, :], hi[:, at], lo[:, at], xt_hi[half][:, w, :],
                                            xt_lo[half][:, w, :], w == 0, w == WH - 1)
                        return last
                    product = pe(multiply, [w_ready, xt_of(half), *bank.readers])
                    queries[half, kv, q] = evacuate(bank, q_slots.take(), product)
                    if part == GROUP + 1:
                        slot.readers = [product]
                        xt_slots[half].readers = [product]

            shifted, softened, probs, probs_t = {}, {}, {}, {}

            def scores(i):
                half, kv, q, b = units[i]
                bank, sc, pr = score_banks.take(), score_slots.take(), prob_slots.take()
                (k_slot, k_ready), (q_slot, q_ready) = keys[half, kv], queries[half, kv, q]
                key_tok = slice(b * SEQ, (b + 1) * SEQ)

                def multiply(e):
                    for r in range(2):
                        at = slice(b * SEQ + r * P, b * SEQ + (r + 1) * P)
                        last = product3(e, bank.t[:, r * SEQ:(r + 1) * SEQ], q_slot.t[0][:, at], q_slot.t[1][:, at],
                                        k_slot.t[0][:, key_tok], k_slot.t[1][:, key_tok], True, True)
                    return last
                product = pe(multiply, [k_ready, q_ready, *bank.readers])
                q_slot.readers = [product]
                k_slot.readers = [product]
                row_max, row_bias = sc.extra
                batch = half * HB + b
                for r in range(2):
                    masked = dve(lambda e, r=r: e.tensor_tensor_reduce(
                        sc.t[:, r, :], bank.t[:, r * SEQ:(r + 1) * SEQ], mask_bias[:, batch, :], 1.0, -3.0e38,
                        ALU.add, ALU.max, row_max[:, r:r + 1]), [product, bias_ready, *sc.readers])
                bank.readers = [masked]
                shift = dve(lambda e: e.tensor_scalar(row_bias[:, :], row_max[:, :], -SCALE, None, ALU.mult), [masked])
                shifted[i] = (sc, pr, shift)

            def soften(i):
                sc, pr, shift = shifted.pop(i)
                row_max, row_bias = sc.extra
                row_sum, row_scale = pr.extra
                for r in range(2):
                    raised = act(lambda e, r=r: e.activation(pr.t[:, r, :], sc.t[:, r, :], ACT.Exp, scale=SCALE,
                                                             bias=row_bias[:, r:r + 1], accum_out=row_sum[:, r:r + 1]),
                                 [shift, *pr.readers])
                sc.readers = [raised]
                softened[i] = (pr, raised)

            def normalize(i):
                pr, raised = softened.pop(i)
                row_sum, row_scale = pr.extra
                batch = units[i][0] * HB + units[i][3]
                inverse = dve(lambda e: e.reciprocal(row_scale[:, :], row_sum[:, :]), [raised])
                kept = pool(lambda e: e.tensor_tensor(row_scale[:, :], row_scale[:, :],
                                                      any_valid[:, batch:batch + 1].broadcast_to([P, 2]), ALU.mult),
                            [inverse, valid_ready])
                normed = pool(lambda e: e.tensor_tensor(pr.t[:, :, :], pr.t[:, :, :],
                                                        row_scale[:, :].unsqueeze(2).broadcast_to([P, 2, SEQ]),
                                                        ALU.mult), [kept])
                probs[i] = (pr, normed)

            def turn_probs(i):
                pr, normed = probs.pop(i)

                def turn(e):
                    for s in range(2):
                        for r in range(2):
                            last = e.transpose(prob_bank.t[:, s * SEQ + r * P:s * SEQ + (r + 1) * P],
                                               pr.t[:, r, s * P:(s + 1) * P], identity[:, :])
                    return last
                turned = pe(turn, [normed, ident_ready, *prob_bank.readers])
                pr.readers = [turned]
                probs_t[i] = evacuate(prob_bank, prob_t_slots.take(), turned)

            def head_output(i):
                half, kv, q, b = units[i]
                pt, pt_ready = probs_t.pop(i)
                v_slot, v_ready = values[half, kv]

                def multiply(e):
                    for s in range(2):
                        j = b * (SEQ // P) + s
                        last = product3(e, head_bank.t[:, b * SEQ:(b + 1) * SEQ], v_slot.t[0][:, j, :],
                                        v_slot.t[1][:, j, :], pt.t[0][:, s, :], pt.t[1][:, s, :], s == 0, s == 1)
                    return last
                before = head_bank.readers if b == 0 else []
                product = pe(multiply, [pt_ready, v_ready, *before])
                pt.readers = [product]
                v_slot.readers = [product]
                if b == HB - 1:
                    heads[i] = evacuate(head_bank, head_slots.take(), product)

            def project_out(i):
                half, kv, q, b = units[i]
                if b != HB - 1:
                    return
                head, head_ready = heads.pop(i)
                slot, w_ready = split_weights("out", half, kv)
                first, final = (kv, q) == (0, 0), (kv, q) == (KV_HEADS - 1, GROUP - 1)

                def multiply(e):
                    for w in range(WH):
                        at = slice(q * WIDTH + w * P, q * WIDTH + (w + 1) * P)
                        last = product3(e, acc[w].t[:, :], slot.t[0][:, at], slot.t[1][:, at], head.t[0][:, :],
                                        head.t[1][:, :], first, final)
                    return last
                before = [r for bk in acc for r in bk.readers] if first else []
                product = pe(multiply, [head_ready, w_ready, *before])
                head.readers = [product]
                if q == GROUP - 1:
                    slot.readers = [product]
                if final:
                    attended[half] = product

            for part in range(GROUP + 2):
                project(0, part)
            for i in range(len(units) + 4):
                if 0 <= i - 1 < len(units):
                    normalize(i - 1)
                if i < len(units):
                    scores(i)
                if 0 <= i - 2 < len(units):
                    turn_probs(i - 2)
                if 0 <= i - 3 < len(units):
                    head_output(i - 3)
                if 0 <= i - 4 < len(units):
                    project_out(i - 4)
                if i < len(units):
                    split_piece()
                    soften(i)
                    project(i // (GROUP * HB) + 1, i % (GROUP * HB))
                between(i)

        def attention_to_ffn(half):
            added = yield from add_to_x(half, banks[2:4], attended[half], Ring(banks[2:4]))
            return (yield from to_next_part(added, half, route_layer1))

        attended = {}
        after_ffn[1] = Below(ffn_to_attention(1, Ring(banks[2:4])))
        after_ffn[1].advance()
        after_attention = {}

        def norms_below(i):
            if i == 0 or i % 2 == 1:
                after_ffn[1].advance()
            if 0 in attended:
                if 0 not in after_attention:
                    after_attention[0] = Below(attention_to_ffn(0))
                    after_attention[0].advance()
                elif (i - 35) % 2 == 1:
                    after_attention[0].advance()

        attention(lambda half: after_ffn[half].finish(), norms_below)

        units = [(c, 0) for c in range(ALONE)]
        units += [(c, h) for c in range(ALONE, FFN1_CHUNKS) for h in range(HALVES)]
        units += [(c, 1) for c in range(ALONE)]
        xt_ready, stored, finished = {}, {}, {}
        xt_ready[0], stored[0] = after_attention[0].finish()
        after_attention[1] = Below(attention_to_ffn(1))
        after_attention[1].advance()
        acc_of = {0: banks[2:4], 1: banks[0:2]}
        outputs = {}

        def to_output(half, ring):
            added = yield from add_to_x(half, acc_of[half], finished[half], ring)
            for pair, step in enumerate(added):
                t = half * HC + 2 * pair
                stores.append(sp(lambda e, t=t: e.dma_start(out_dram[:, t:t + 2, :], x_tok[:, t:t + 2, :]), [step],
                                 lane(f"out_stored{t}", 16)))
            return added

        def ends_below(i):
            if 1 not in xt_ready:
                after_attention[1].advance()
                if after_attention[1].result:
                    xt_ready[1], stored[1] = after_attention[1].result
            if 0 in finished:
                if 0 not in outputs:
                    outputs[0] = Below(to_output(0, Ring(acc_of[0])))
                outputs[0].advance()

        run_ffn(1, units, stored, xt_ready, acc_of, ends_below, finished)
        complete(to_output(1, Ring(banks[4:8])))

        sp(lambda e: e.drain(), stores)

        for q in (pe, act, dve, pool, sp):
            for _, _, step in q.todo:
                counted = number_steps(step)
                step.value = counted

        block = stack.enter_context(nc.Block())

        @block.tensor
        def _(e):
            pe.run(e)

        @block.scalar
        def _(e):
            act.run(e)

        @block.vector
        def _(e):
            dve.run(e)

        @block.gpsimd
        def _(e):
            pool.run(e)

        @block.sync
        def _(e):
            sp.run(e)


def number_steps(step):
    lane = step.lane
    if step.value is None:
        count = 0
        for s in lane.steps:
            count += lane.weight if s.awaited else 0
            s.value = count
    return step.value


def kernel(**inputs):
    import numpy as np
    import concourse.bacc as bacc
    from concourse.bass_utils import run_bass_kernel_spmd

    a = {name: np.asarray(value) for name, value in inputs.items()}

    def wide(w):
        return w.reshape(-1, P, w.shape[-1]).transpose(1, 0, 2)

    def ffn_chunks(gate, up, down):
        n = gate.shape[1] // P
        sides = [wide(w).reshape(P, WH, n, P).transpose(2, 0, 1, 3).reshape(n, P, WIDTH) for w in (gate, up)]
        return np.concatenate([*sides, down.reshape(n, P, WIDTH)], axis=2)

    by_channel = [a[f"L0_xattn_{n}"].reshape(EH, P, -1).transpose(1, 0, 2)
                  for n in ("conv_w", "conv_b", "D", "dt_proj_b", "A_log")]
    ffn1_shared = ffn_chunks(a["L1_ffn_wg_s"], a["L1_ffn_wu_s"], a["L1_ffn_wd_s"])
    ffn1_routed = ffn_chunks(a["L1_ffn_wg"].transpose(1, 0, 2).reshape(WIDTH, E1 * I1),
                             a["L1_ffn_wu"].transpose(1, 0, 2).reshape(WIDTH, E1 * I1),
                             a["L1_ffn_wd"].reshape(E1 * I1, WIDTH))
    wq = wide(a["L1_xattn_Wq"]).reshape(P, WH, KV_HEADS, GROUP, HD).transpose(2, 0, 3, 1, 4)
    wk = a["L1_xattn_Wk"].reshape(CTX, KV_HEADS, HD).transpose(1, 0, 2)
    wv = a["L1_xattn_Wv"].reshape(CTX, KV_HEADS, HD).transpose(1, 0, 2)
    wo = a["L1_xattn_Wo"].reshape(KV_HEADS, GROUP, HD, WIDTH).transpose(0, 2, 1, 3)
    laid_out = {
        "x": a["x"],
        "ctx_t": a["ctx_1024"].reshape(TOKENS, CTX).T,
        "key_mask": a["mask_BxS2_bf1"].reshape(1, TOKENS),
        "in_proj_t": a["L0_xattn_in_proj_w"].T,
        "ssm_small": np.concatenate(by_channel, axis=2),
        "x_proj_t": wide(a["L0_xattn_x_proj_w"].T),
        "dt_proj_t": a["L0_xattn_dt_proj_w"].T,
        "gate_t": wide(a["L0_ffn_gate_w"].T),
        "centroids_t": wide(a["L1_ffn_centroids"].T),
        "gate_bias": a["L1_ffn_gate_bias"].reshape(1, E1),
        "ffn0_w": ffn_chunks(a["L0_ffn_w_gate_proj"].reshape(E0 * I0, WIDTH).T,
                             a["L0_ffn_w_up_proj"].reshape(E0 * I0, WIDTH).T,
                             a["L0_ffn_w_down_proj"].transpose(0, 2, 1).reshape(E0 * I0, WIDTH)),
        "attn_proj_w": np.concatenate([wq.reshape(KV_HEADS, P, -1), wk, wv], axis=2),
        "attn_out_w": wo.reshape(KV_HEADS, HD, WO_PIECE),
        "ffn1_w": np.concatenate([ffn1_shared, ffn1_routed], axis=0),
    }
    nc = bacc.Bacc("TRN2", target_bir_lowering=False, num_devices=1)
    arrays, args = {}, []
    for name, value in laid_out.items():
        value = np.ascontiguousarray(value)
        arrays[f"in_{name}"] = value
        args.append(nc.dram_tensor(f"in_{name}", value.shape, mybir.dt.from_np(value.dtype), kind="ExternalInput").ap())
    args.append(nc.dram_tensor("out", (BATCHES, SEQ, WIDTH), F32, kind="ExternalOutput").ap())
    build(nc, *args)
    result = run_bass_kernel_spmd(nc, [arrays], core_ids=[0])
    return result.results[0]["out"]
```

```python
from contextlib import ExitStack

import concourse.bass as bass
from concourse import mybir

F32 = mybir.dt.float32
F32R = mybir.dt.float32r
U8 = mybir.dt.uint8
U32 = mybir.dt.uint32
ALU = mybir.AluOpType
ACT = mybir.ActivationFunctionType
AX_X = mybir.AxisListType.X

P = 128
BATCHES, SEQ, WIDTH = 4, 256, 256
TOKENS = BATCHES * SEQ
CHUNKS = TOKENS // P
HALVES = 2
HT = TOKENS // HALVES
HC = CHUNKS // HALVES
HB = BATCHES // HALVES
WH = WIDTH // P
CTX = 128
DI, DS, DC, DR = 256, 16, 4, 8
EH = DI // P
E0, I0, TOP0 = 32, 96, 8
E1, I1, TOP1 = 16, 128, 2
SHARED = 2 * I1
SHARED_RATIO = 0.1
FFN0_CHUNKS = E0 * I0 // P
SHARED_CHUNKS = SHARED // P
FFN1_CHUNKS = SHARED_CHUNKS + E1
HEADS, KV_HEADS, HD = 16, 8, 128
GROUP = HEADS // KV_HEADS
SCALE = float(HD) ** -0.5
LN_EPS = 1e-5
TOP_EPS = 1e-9
MASKED = -1e30
PIECE = 3 * WIDTH
WO_PIECE = GROUP * WIDTH
SCANNED_BEFORE = 1
ALONE = 8


class Lane:

    def __init__(self, sem, weight=1):
        self.sem, self.weight, self.steps = sem, weight, []


class Step:

    def __init__(self, lane):
        self.lane, self.awaited, self.value = lane, lane.weight == 16, None
        lane.steps.append(self)


class Queue:

    def __init__(self, lane):
        self.lane, self.todo = lane, []

    def __call__(self, emit, after=(), lane=None):
        step = Step(lane or self.lane)
        after = [s for s in after if s is not None]
        for s in after:
            s.awaited = True
        self.todo.append((emit, after, step))
        return step

    def run(self, engine):
        reached = {}
        for emit, after, step in self.todo:
            need = {}
            for s in after:
                need[s.lane] = max(need.get(s.lane, 0), s.value)
            for lane, value in need.items():
                if reached.get(lane, 0) < value:
                    engine.wait_ge(lane.sem, value)
                    reached[lane] = value
            last = emit(engine)
            if step.awaited:
                last.then_inc(step.lane.sem, step.lane.weight)


class Slot:

    def __init__(self, t, extra=None):
        self.t, self.extra, self.readers = t, extra, []


class Ring:
    def __init__(self, slots):
        self.slots, self.n = slots, 0

    def take(self):
        slot = self.slots[self.n % len(self.slots)]
        self.n += 1
        return slot

    def peek(self):
        return self.slots[self.n % len(self.slots)]


def product3(e, out, w_hi, w_lo, m_hi, m_lo, first, last):
    e.matmul(out, w_hi, m_hi, start=first, stop=False)
    e.matmul(out, w_hi, m_lo, start=False, stop=False)
    return e.matmul(out, w_lo, m_hi, start=False, stop=last)


def complete(work):
    while True:
        try:
            next(work)
        except StopIteration as end:
            return end.value


class Below:

    def __init__(self, work):
        self.work, self.result = work, None

    def advance(self):
        if self.result is None:
            try:
                next(self.work)
            except StopIteration as end:
                self.result = end.value

    def finish(self):
        if self.result is None:
            self.result = complete(self.work)
        return self.result


def build(nc, x, ctx_t, key_mask, in_proj_t, ssm_small, x_proj_t, dt_proj_t, gate_t, centroids_t, gate_bias,
          ffn0_w, attn_proj_w, attn_out_w, ffn1_w, out):
    stack = ExitStack()
    with stack:
        def lane(name, weight=1):
            return Lane(stack.enter_context(nc.semaphore(name)), weight)

        pe = Queue(lane("tensor_steps"))
        act = Queue(lane("scalar_steps"))
        dve = Queue(lane("vector_steps"))
        pool = Queue(lane("gpsimd_steps"))
        sp = Queue(lane("sync_steps"))
        stores = []

        def load_once(name, dst, src, after=()):
            return sp(lambda e: e.dma_start(dst, src), after, lane("landed_" + name, 16))

        top = [(nc.sbuf_base + 63) // 64 * 64]

        def place(name, shape, dtype=F32):
            size = 1
            for n in shape[1:]:
                size *= n
            size *= 1 if dtype == U8 else 4
            t = nc.alloc_sbuf_tensor_at(name, shape, dtype, offset=top[0])
            top[0] += (size + 31) // 32 * 32
            return t

        identity = place("identity", [P, P])
        x_tok = place("x_tok", [P, CHUNKS, WIDTH])
        ctx_sb = place("ctx_sb", [P, TOKENS])
        in_proj_sb = place("in_proj_sb", [P, DI])
        small_sb = place("small_sb", [P, EH, DC + 3 + DS])
        x_proj_sb = place("x_proj_sb", [P, EH, DR + 2 * DS])
        dt_proj_sb = place("dt_proj_sb", [DR, DI])
        decay = place("decay", [P, EH, DS])
        gate_raw = place("gate_raw", [P, WH, E0])
        gate_hi = place("gate_hi", [P, WH, E0], F32R)
        gate_lo = place("gate_lo", [P, WH, E0], F32R)
        cent_raw = place("cent_raw", [P, WH, E1])
        cent_hi = place("cent_hi", [P, WH, E1], F32R)
        cent_lo = place("cent_lo", [P, WH, E1], F32R)
        bias_bc = place("bias_bc", [P, E1])
        expert_ids = place("expert_ids", [P, E1])
        half_power = place("half_power", [P, HC])
        mask_u8 = place("mask_u8", [P, BATCHES, SEQ], U8)
        any_valid = place("any_valid", [P, BATCHES])
        moment_slots = [Slot((place(f"stats{h}", [P, HC, 6]), place(f"mean_var{h}", [P, HC, 2]),
                              place(f"rstd{h}", [P, HC]))) for h in range(HALVES)]
        x_norm = place("x_norm", [P, HC, WIDTH])
        xt_hi = [place(f"xt_hi{h}", [P, WH, HT], F32R) for h in range(HALVES)]
        xt_lo = [place(f"xt_lo{h}", [P, WH, HT], F32R) for h in range(HALVES)]
        acc_sb = place("acc_sb", [P, WH, HT])
        logits = place("logits", [P, HC, E0])
        top8 = place("top8", [P, HC, 8])
        top_idx = place("top_idx", [P, HC, 8], U32)
        top_idx_f = place("top_idx_f", [P, HC, TOP1])
        route_a = place("route_a", [P, 2, HC, E0])
        route_w = place("route_w", [P, HC, E0])
        route_sum = place("route_sum", [P, HC])
        route_t = place("route_t", [E0, HT])
        raw_slots = Ring([Slot(place(f"w_raw{i}", [P, PIECE]), lane(f"landed_w_raw{i}", 16)) for i in range(3)])
        split_slots = Ring([Slot((place(f"w_hi{i}", [P, PIECE], F32R), place(f"w_lo{i}", [P, PIECE], F32R)))
                            for i in range(4)])
        gated_slots = Ring([Slot(place(f"gated{i}", [P, HT])) for i in range(2)])
        hidden_slots = Ring([Slot(place(f"hidden{i}", [P, HT])) for i in range(2)])
        hidden_split = Ring([Slot((place(f"hidden_hi{i}", [P, HT], F32R), place(f"hidden_lo{i}", [P, HT], F32R)))
                             for i in range(3)])
        mask_slots = Ring([Slot(place(f"route_bc{i}", [P, HT]), lane(f"landed_route_bc{i}", 16)) for i in range(4)])

        shared_region = top[0]
        starts = [top[0]]
        u_sb = place("u_sb", [P, HALVES, EH, HT])
        starts.append(top[0])
        delta = place("delta", [P, HALVES, EH, HT])
        starts.append(top[0])
        delta_u = place("delta_u", [P, HALVES, EH, HT])
        starts.append(top[0])
        z_gate = place("z_gate", [P, CHUNKS, WIDTH])
        x_dbl = place("x_dbl", [DR + 2 * DS, TOKENS])
        b_slots, c_slots = (Ring([Slot(place(f"{name}_rows{i}", [P, HT]), lane(f"landed_{name}{i}", 16))
                                  for i in range(3)]) for name in "bc")
        da_slots = Ring([Slot(place(f"decay_t{i}", [P, EH, HT])) for i in range(5)])
        conv_in_at = top[0]
        hc_slots = Ring([Slot(place(f"read_out{i}", [P, EH, HT])) for i in range(4)])
        h_slots = Ring([Slot(place(f"state{i}", [P, EH, HT])) for i in range(2)])
        dbu_slots = Ring([Slot(place(f"drive{i}", [P, EH, HT])) for i in range(2)])
        scan_end = top[0]
        top[0] = conv_in_at
        conv_in = place("conv_in", [P, EH, BATCHES, DC - 1 + SEQ])
        assert top[0] <= scan_end
        more_split = []
        for i in range(2):
            pair = []
            for k, part in enumerate(("hi", "lo")):
                top[0] = starts[2 * i + k]
                pair.append(place(f"w_more_{part}{i}", [P, PIECE], F32R))
                assert top[0] <= starts[2 * i + k] + EH * HT * 4
            more_split.append(Slot(tuple(pair)))

        top[0] = shared_region
        ctx_hi = place("ctx_hi", [P, TOKENS], F32R)
        ctx_lo = place("ctx_lo", [P, TOKENS], F32R)
        mask_bias = place("mask_bias", [P, BATCHES, SEQ])

        def split_pair(name, shape):
            return (place(name + "_hi", shape, F32R), place(name + "_lo", shape, F32R))

        k_slots = Ring([Slot(split_pair(f"k_t{i}", [P, HT])) for i in range(2)])
        v_slots = Ring([Slot(split_pair(f"v{i}", [P, HC, HD])) for i in range(2)])
        q_slots = Ring([Slot(split_pair(f"q_t{i}", [P, HT])) for i in range(4)])
        score_slots = Ring([Slot(place(f"scores{i}", [P, 2, SEQ]),
                                 (place(f"row_max{i}", [P, 2]), place(f"row_bias{i}", [P, 2]))) for i in range(2)])
        prob_slots = Ring([Slot(place(f"probs{i}", [P, 2, SEQ]),
                                (place(f"row_sum{i}", [P, 2]), place(f"row_scale{i}", [P, 2]))) for i in range(3)])
        prob_t_slots = Ring([Slot(split_pair(f"probs_t{i}", [P, 2, SEQ])) for i in range(2)])
        head_slots = Ring([Slot(split_pair(f"head_out{i}", [P, HT])) for i in range(2)])
        assert max(scan_end, top[0]) <= nc.sbuf_usable_end

        banks = [Slot(stack.enter_context(nc.psum_tensor(f"bank{i}", [P, 512], F32))) for i in range(8)]
        spare = Ring(banks[0:2])

        bc_dram = nc.dram_tensor("bc_scratch", (2 * DS, TOKENS), F32).ap()
        route_dram = [[nc.dram_tensor(f"route_scratch{layer}_{h}", (n, HT), F32).ap() for h in range(HALVES)]
                      for layer, n in ((0, E0), (1, E1))]

        def rows(src, p):
            return src.partition_broadcast(p).rearrange("p a n -> p (a n)")

        in_proj_in = load_once("in_proj", in_proj_sb[:, :], in_proj_t)
        ctx_in = [load_once(f"ctx{h}", ctx_sb[:, h * HT:(h + 1) * HT], ctx_t[:, h * HT:(h + 1) * HT])
                  for h in range(HALVES)]
        small_in = load_once("ssm_small", small_sb[:, :, :], ssm_small)
        x_dram = x.rearrange("b (c p) w -> p (b c) w", p=P)
        out_dram = out.rearrange("b (c p) w -> p (b c) w", p=P)
        x_in = [load_once(f"x{h}", x_tok[:, h * HC:(h + 1) * HC, :], x_dram[:, h * HC:(h + 1) * HC, :])
                for h in range(HALVES)]
        x_proj_in = load_once("x_proj", x_proj_sb[:, :, :], x_proj_t)
        dt_proj_in = load_once("dt_proj", dt_proj_sb[:, :], dt_proj_t)
        gate_in = load_once("gate", gate_raw[:, :, :], gate_t)
        cent_in = load_once("centroids", cent_raw[:, :, :], centroids_t)
        bias_in = load_once("gate_bias", bias_bc[:, :], rows(gate_bias, P))
        mask_in = load_once("key_mask", mask_u8[:, :, :].rearrange("p b s -> p (b s)"), rows(key_mask, P))

        conv_w = [small_sb[:, :, j] for j in range(DC)]
        conv_b, skip_d, dt_bias = (small_sb[:, :, DC + j] for j in range(3))
        a_log = small_sb[:, :, DC + 3:]

        ident_zero = pool(lambda e: e.memset(identity[:, :], 0.0))
        ident_ready = pool(lambda e: e.affine_select(
            out=identity[:, :], in_=identity[:, :], compare_op=ALU.not_equal, fill=1.0, base=0,
            pattern=[[-1, P]], channel_multiplier=1), [ident_zero])
        pad_ready = pool(lambda e: e.memset(conv_in[:, :, :, 0:DC - 1].rearrange("p h b s -> p (h b) s"), 0.0))
        power_ready = pool(lambda e: e.memset(half_power[:, :], -0.5))
        ids_ready = pool(lambda e: e.iota(expert_ids[:, :], pattern=[[1, E1]], base=0, channel_multiplier=0,
                                          allow_small_or_imprecise_dtypes=True))

        pieces = {("ffn0", h, c): ffn0_w[c] for h in range(HALVES) for c in range(FFN0_CHUNKS)}
        groups = [(h, kv) for h in range(HALVES) for kv in range(KV_HEADS)]
        for g, (h, kv) in enumerate(groups):
            pieces["proj", h, kv] = attn_proj_w[kv]
            if g > 0:
                pieces["out", *groups[g - 1]] = attn_out_w[groups[g - 1][1]]
        pieces["out", *groups[-1]] = attn_out_w[groups[-1][1]]
        pieces.update({("ffn1", 0, c): ffn1_w[c] for c in range(FFN1_CHUNKS)})
        pieces.update({("ffn1", 1, c): ffn1_w[c] for c in range(ALONE)})
        order = {key: n for n, key in enumerate(pieces)}
        pieces = list(pieces.values())
        fetched, pieces_split, split_ring = [], [], [split_slots]

        def fetch_piece():
            if len(fetched) < len(pieces):
                src = pieces[len(fetched)]
                slot = raw_slots.take()
                n = src.shape[-1]
                landed = sp(lambda e: e.dma_start(slot.t[:, 0:n], src), slot.readers, slot.extra)
                fetched.append((slot, n, landed))

        def more_split_slots():
            ring = Ring(split_ring[0].slots[:])
            ring.n = split_ring[0].n % len(ring.slots)
            ring.slots[ring.n:ring.n] = more_split
            split_ring[0] = ring

        def split_piece():
            if len(pieces_split) == FFN0_CHUNKS - 2:
                split_ring[0] = split_slots
            if len(pieces_split) == len(pieces) or split_ring[0].peek().readers is None:
                return
            if len(fetched) < len(pieces_split) + 3:
                fetch_piece()
            raw, n, landed = fetched[len(pieces_split)]
            slot = split_ring[0].take()
            hi, lo = slot.t
            rounded = act(lambda e: e.activation(hi[:, 0:n], raw.t[:, 0:n], ACT.Copy), [landed, *slot.readers])
            rest = pool(lambda e: e.tensor_tensor(lo[:, 0:n], raw.t[:, 0:n], hi[:, 0:n].bitcast(F32), ALU.subtract),
                        [landed, rounded, *slot.readers])
            raw.readers = [rounded, rest]
            slot.readers = None
            pieces_split.append((slot, rest))

        def split_weights(*key):
            while len(pieces_split) <= order[key]:
                done = len(pieces_split)
                split_piece()
                assert len(pieces_split) > done, "no slot is free"
            return pieces_split[order[key]]

        for _ in range(3):
            fetch_piece()

        def chunk_stats(half, j, source):
            stats, _, _ = moment_slots[half].t
            return dve(lambda e: e.bn_stats(stats[:, j, :], x_tok[:, half * HC + j, :]),
                       [source, *moment_slots[half].readers])

        def layer_norm(half, done, out, out_slot):
            stats, mean_var, rstd = moment_slots[half].t
            for j in range(HC):
                moments = dve(lambda e, j=j: e.bn_aggr(mean_var[:, j, :], stats[:, j, :]), [done[j]])
            variance = dve(lambda e: e.tensor_scalar(rstd[:, :], mean_var[:, :, 1], LN_EPS, None, ALU.add), [moments])
            scale = pool(lambda e: e.tensor_tensor(rstd[:, :], rstd[:, :], half_power[:, :], ALU.pow),
                         [variance, power_ready])
            yield
            for j in range(HC):
                t = half * HC + j
                normed = dve(lambda e, j=j, t=t: e.tensor_scalar(
                    out[:, j, :], x_tok[:, t, :], mean_var[:, j, 0:1], rstd[:, j:j + 1], ALU.subtract, ALU.mult),
                    [scale, moments, *out_slot.readers])
            moment_slots[half].readers = [normed]
            return normed

        norm_slot = Slot(None)
        xt_slots = [Slot(None) for _ in range(HALVES)]

        def turn_and_split(half, normed, ring, spread=False):
            yield
            for w in range(WH):
                bank = ring.take()

                def turn(e, w=w, bank=bank):
                    for j in range(HC):
                        last = e.transpose(bank.t[:, j * P:(j + 1) * P], x_norm[:, j, w * P:(w + 1) * P], identity[:, :])
                    return last
                turned = pe(turn, [normed, ident_ready, *bank.readers])
                hi = act(lambda e, w=w, bank=bank: e.activation(xt_hi[half][:, w, :], bank.t[:, :], ACT.Copy),
                         [turned, *xt_slots[half].readers])
                lo = dve(lambda e, w=w, bank=bank: e.tensor_tensor(
                    xt_lo[half][:, w, :], bank.t[:, :], xt_hi[half][:, w, :].bitcast(F32), ALU.subtract),
                    [turned, hi, *xt_slots[half].readers])
                bank.readers = [hi, lo]
                norm_slot.readers = [turned]
                if spread and w < WH - 1:
                    yield
            xt_slots[half].readers = []
            return lo

        route_t_slot = Slot(None, lane("route_stored", 16))
        def router_logits(half, xt_ready, w_hi, w_lo, n, w_ready, ring):
            yield
            bank = ring.take()

            def multiply(e):
                for w in range(WH):
                    last = product3(e, bank.t[0:n, :], w_hi[:, w, :], w_lo[:, w, :], xt_hi[half][:, w, :],
                                    xt_lo[half][:, w, :], w == 0, w == WH - 1)
                return last
            product = pe(multiply, [xt_ready, w_ready, *bank.readers])
            moved = act(lambda e: e.activation(route_t[0:n, :], bank.t[0:n, :], ACT.Copy),
                        [product, *route_t_slot.readers])
            bank.readers = [moved]
            yield
            turned_bank = ring.take()

            def turn(e):
                for j in range(HC):
                    last = e.transpose(turned_bank.t[:, j * n:(j + 1) * n], route_t[0:n, j * P:(j + 1) * P],
                                       identity[0:n, 0:n])
                return last
            turned = pe(turn, [moved, ident_ready, *turned_bank.readers])
            route_t_slot.readers = [turned]
            return turned_bank, turned

        route_slot = Slot(None)

        def route_to_dram(layer, half, n, weighted, ring, spread):
            yield
            bank = ring.take()

            def turn(e):
                for j in range(HC):
                    last = e.transpose(bank.t[0:n, j * P:(j + 1) * P], route_w[:, j, 0:n], identity[:, :])
                return last
            turned = pe(turn, [weighted, ident_ready, *bank.readers])
            copied = dve(lambda e: e.tensor_copy(route_t[0:n, :], bank.t[0:n, :]), [turned, *route_t_slot.readers])
            bank.readers = [copied]
            route_slot.readers = [turned]
            stored = sp(lambda e: e.dma_start(route_dram[layer][half], route_t[0:n, :]), [copied], route_t_slot.extra)
            route_t_slot.readers = [stored]
            stores.append(stored)
            return stored

        def route_layer0(half, xt_ready, ring, spread):
            bank, product = yield from router_logits(half, xt_ready, gate_hi, gate_lo, E0, gate_ready, ring)
            kept = dve(lambda e: e.tensor_copy(logits[:, :, :], bank.t[:, 0:HC * E0].rearrange("p (j n) -> p j n", j=HC)),
                       [product, *route_slot.readers])
            bank.readers = [kept]
            for j in range(HC):
                best = dve(lambda e, j=j: e.max(out=top8[:, j, :], in_=logits[:, j, :]), [kept, *route_slot.readers])
            for j in range(HC):
                taken = dve(lambda e, j=j: e.match_replace(out=route_a[:, 1, j, :], in_to_replace=top8[:, j, :],
                                                           in_values=logits[:, j, :], imm_value=MASKED), [best])
            row_max = top8[:, :, 0:1].broadcast_to([P, HC, E0])
            dve(lambda e: e.tensor_tensor(route_a[:, 0, :, :], logits[:, :, :], row_max, ALU.subtract), [best])
            shifted = dve(lambda e: e.tensor_tensor(route_a[:, 1, :, :], route_a[:, 1, :, :], row_max, ALU.subtract),
                          [taken])
            flat = route_a[:, :, :, :].rearrange("p a j n -> p (a j n)")
            raised = act(lambda e: e.activation(flat, flat, ACT.Exp), [shifted])
            picked = dve(lambda e: e.tensor_tensor(route_w[:, :, :], route_a[:, 0, :, :], route_a[:, 1, :, :],
                                                   ALU.subtract), [raised])
            summed = dve(lambda e: e.tensor_reduce(route_sum[:, :], route_w[:, :, :], AX_X, ALU.add), [picked])
            inverse = dve(lambda e: e.reciprocal(route_sum[:, :], route_sum[:, :]), [summed])
            weighted = dve(lambda e: e.tensor_tensor(
                route_w[:, :, :], route_w[:, :, :], route_sum[:, :].unsqueeze(2).broadcast_to([P, HC, E0]), ALU.mult),
                [inverse])
            return (yield from route_to_dram(0, half, E0, weighted, ring, spread))

        def route_layer1(half, xt_ready, ring, spread):
            bank, product = yield from router_logits(half, xt_ready, cent_hi, cent_lo, E1, cent_ready, ring)
            aff = logits[:, :, 0:E1]
            biased = route_a[:, 0, :, 0:E1]
            affinity = act(lambda e: e.activation(aff, bank.t[:, 0:HC * E1].rearrange("p (j n) -> p j n", j=HC),
                                                  ACT.Sigmoid), [product, *route_slot.readers])
            bank.readers = [affinity]
            if spread:
                yield
            ranked = dve(lambda e: e.tensor_tensor(biased, aff, bias_bc[:, :].unsqueeze(1).broadcast_to([P, HC, E1]),
                                                   ALU.add), [affinity, bias_in])
            for j in range(HC):
                best = dve(lambda e, j=j: e.max(out=top8[:, j, :], in_=route_a[:, 0, j, 0:E1]),
                           [ranked, *route_slot.readers])
            for j in range(HC):
                found = dve(lambda e, j=j: e.max_index(top_idx[:, j, :], top8[:, j, :], route_a[:, 0, j, 0:E1]), [best])
            if spread:
                yield
            index_f = dve(lambda e: e.tensor_copy(top_idx_f[:, :, :], top_idx[:, :, 0:TOP1]), [found])
            for k in range(TOP1):
                for j in range(HC):
                    chosen = dve(lambda e, k=k, j=j: e.scalar_tensor_tensor(
                        out=route_a[:, k, j, E1:2 * E1], in0=expert_ids[:, :], scalar=top_idx_f[:, j, k:k + 1],
                        in1=logits[:, j, 0:E1], op0=ALU.is_equal, op1=ALU.mult), [index_f, ids_ready])
            both = dve(lambda e: e.tensor_tensor(route_w[:, :, 0:E1], route_a[:, 0, :, E1:2 * E1],
                                                 route_a[:, 1, :, E1:2 * E1], ALU.add), [chosen])
            summed = dve(lambda e: e.tensor_reduce(route_sum[:, :], route_w[:, :, 0:E1], AX_X, ALU.add), [both])
            guarded = dve(lambda e: e.tensor_scalar(route_sum[:, :], route_sum[:, :], TOP_EPS, None, ALU.add), [summed])
            inverse = dve(lambda e: e.reciprocal(route_sum[:, :], route_sum[:, :]), [guarded])
            weighted = dve(lambda e: e.tensor_tensor(
                route_w[:, :, 0:E1], route_w[:, :, 0:E1], route_sum[:, :].unsqueeze(2).broadcast_to([P, HC, E1]),
                ALU.mult), [inverse])
            return (yield from route_to_dram(1, half, E1, weighted, ring, spread))

        acc_slot = Slot(None)

        def add_to_x(half, acc_banks, finished, ring, stats=True):
            copies = []
            for w in range(WH):
                engine = (act, dve)[w]
                emit = ((lambda e, w=w: e.activation(acc_sb[:, w, :], acc_banks[w].t[:, :], ACT.Copy)),
                        (lambda e, w=w: e.tensor_copy(acc_sb[:, w, :], acc_banks[w].t[:, :])))[w]
                copies.append(engine(emit, [finished, *acc_slot.readers]))
                acc_banks[w].readers = [copies[w]]
            yield
            done = []
            for pair in range(HC // 2):
                bank = ring.take()

                def turn(e, pair=pair, bank=bank):
                    for j in range(2):
                        tok = slice((2 * pair + j) * P, (2 * pair + j + 1) * P)
                        for w in range(WH):
                            last = e.transpose(bank.t[:, j * WIDTH + w * P:j * WIDTH + (w + 1) * P],
                                               acc_sb[:, w, tok], identity[:, :])
                    return last
                turned = pe(turn, [*copies, ident_ready, *bank.readers])
                t = half * HC + 2 * pair
                added = dve(lambda e, t=t, bank=bank: e.tensor_tensor(
                    x_tok[:, t:t + 2, :].rearrange("p t w -> p (t w)"),
                    x_tok[:, t:t + 2, :].rearrange("p t w -> p (t w)"), bank.t[:, :], ALU.add), [turned])
                bank.readers = [added]
                acc_slot.readers = [turned]
                done += [chunk_stats(half, 2 * pair + k, added) for k in range(2)] if stats else [added]
                yield
            return done

        y_banks = banks[0:EH]
        decays = {}

        def scan_decays(half, n):
            slot = da_slots.take()
            for c in range(EH):
                last = act(lambda e, c=c: e.activation(
                    slot.t[:, c, :].rearrange("p (b s) -> p b s", b=HB)[:, :, 1:],
                    delta[:, half, c, :].rearrange("p (b s) -> p b s", b=HB)[:, :, 1:],
                    ACT.Exp, scale=decay[:, c, n:n + 1]), [delta_ready[half][0], decay_ready, *slot.readers])
            decays[half, n] = (slot, last)

        b_tiles, c_tiles = {}, {}

        def load_row(half, n, row, ring, tiles):
            if n < DS:
                slot = ring.take()
                src = rows(bc_dram[row:row + 1, half * HT:(half + 1) * HT], P)
                tiles[half, n] = (slot, sp(lambda e: e.dma_start(slot.t[:, :], src),
                                           [bc_stored[half], *slot.readers], slot.extra))

        def load_b(half, n):
            load_row(half, n, n, b_slots, b_tiles)

        def load_c(half, n):
            load_row(half, n, DS + n, c_slots, c_tiles)

        drives, read_outs = {}, {}

        def scan_drive(half, n):
            if n >= DS:
                return
            b, b_in = b_tiles.pop((half, n))
            dbu = dbu_slots.take()
            b_row = b.t[:, :].unsqueeze(1).broadcast_to([P, EH, HT])
            drive = pool(lambda e: e.tensor_tensor(dbu.t[:, :, :], delta_u[:, half, :, :], b_row, ALU.mult),
                         [b_in, delta_ready[half][1], *dbu.readers])
            b.readers = [drive]
            drives[half, n] = (dbu, drive)
            load_b(half, n + 3)

        def scan_state(half, n):
            c, c_in = c_tiles.pop((half, n))
            da, da_ready = decays.pop((half, n))
            dbu, drive = drives.pop((half, n))
            h, hc = h_slots.take(), hc_slots.take()
            c_row = c.t[:, :].unsqueeze(1).broadcast_to([P, EH, HT])
            flat = [s.t[:, :, :].rearrange("p c s -> p (c s)") for s in (da, dbu, h)]
            state = dve(lambda e: e.tensor_tensor_scan(flat[2], flat[0], flat[1], 0.0, ALU.mult, ALU.add),
                        [drive, da_ready, *h.readers])
            da.readers, dbu.readers = [state], [state]
            yield
            read = dve(lambda e: e.tensor_tensor(hc.t[:, :, :], h.t[:, :, :], c_row, ALU.mult),
                       [state, c_in, *hc.readers])
            h.readers = [read]
            c.readers = [read]
            load_c(half, n + 3)
            read_outs[half, n] = (hc, read)

        def scan_add(half, n):
            other, other_ready = read_outs.pop((half, n - 1))
            hc, ready = read_outs[half, n]
            both = dve(lambda e: e.tensor_tensor(hc.t[:, :, :], hc.t[:, :, :], other.t[:, :, :], ALU.add),
                       [ready, other_ready])
            other.readers = [both]
            read_outs[half, n] = (hc, both)

        def scan_sum(half, n, first):
            hc, ready = read_outs.pop((half, n))

            def accumulate(e):
                for c in range(EH):
                    last = e.matmul(y_banks[c].t[:, :], identity[:, :], hc.t[:, c, :], start=first, stop=n == DS - 1)
                return last
            before = [r for b in y_banks for r in b.readers] if first else []
            summed = pe(accumulate, [ready, ident_ready, *before])
            hc.readers = [summed]
            return summed

        def scan_finish(half, summed):
            y = hc_slots.take()
            for c in range(EH):
                with_skip = dve(lambda e, c=c: e.scalar_tensor_tensor(
                    out=y.t[:, c, :], in0=u_sb[:, half, c, :], scalar=skip_d[:, c:c + 1], in1=y_banks[c].t[:, :],
                    op0=ALU.mult, op1=ALU.add), [summed, *y.readers])
                y_banks[c].readers = [with_skip]
            z = z_gate[:, half * HC:(half + 1) * HC, :].rearrange("p (b c) s -> p c b s", c=EH)
            gated = []
            for b in range(HB):
                y_b = y.t[:, :, b * SEQ:(b + 1) * SEQ]
                gated.append(dve(lambda e, b=b, y_b=y_b: e.tensor_tensor(y_b, y_b, z[:, :, b, :], ALU.mult),
                                 [with_skip, z_ready[half]]))
            yield
            done = []
            for b in range(HB):
                bank = spare.take()

                def turn(e, b=b, bank=bank):
                    for l in range(SEQ // P):
                        for c in range(EH):
                            at = b * SEQ + l * P
                            last = e.transpose(bank.t[:, l * DI + c * P:l * DI + (c + 1) * P],
                                               y.t[:, c, at:at + P], identity[:, :])
                    return last
                turned = pe(turn, [gated[b], ident_ready, *bank.readers])
                t = half * HC + b * (SEQ // P)
                added = dve(lambda e, t=t, bank=bank: e.tensor_tensor(
                    x_tok[:, t:t + 2, :].rearrange("p t w -> p (t w)"),
                    x_tok[:, t:t + 2, :].rearrange("p t w -> p (t w)"), bank.t[:, :], ALU.add), [turned])
                bank.readers = [added]
                done += [chunk_stats(half, b * (SEQ // P) + l, added) for l in range(SEQ // P)]
            y.readers = [turned]
            return done

        before_ffn = Ring(banks[EH:])
        conv_ready, u_ready, z_ready, bc_stored, x_dbl_ready, delta_ready = {}, {}, {}, {}, {}, {}

        moved = {}

        def project_in(half, c):
            bank = before_ffn.take()
            projected = pe(lambda e: e.matmul(
                bank.t[:, :], in_proj_sb[:, c * P:(c + 1) * P], ctx_sb[:, half * HT:(half + 1) * HT],
                start=True, stop=True), [ctx_in[half], in_proj_in, *bank.readers])
            moved[half, c] = act(lambda e: e.activation(
                conv_in[:, c, half * HB:(half + 1) * HB, DC - 1:],
                bank.t[:, :].rearrange("p (b s) -> p b s", b=HB), ACT.Copy), [projected])
            bank.readers = [moved[half, c]]

        def convolve(half, c):
            conv_out = u_sb[:, half, c, :].rearrange("p (b s) -> p b s", b=HB)
            taps = [conv_in[:, c, half * HB:(half + 1) * HB, j:j + SEQ] for j in range(DC)]
            step = dve(lambda e: e.tensor_scalar(conv_out, taps[0], conv_w[0][:, c:c + 1], None, ALU.mult),
                       [moved[half, c], pad_ready, small_in])
            for j in range(1, DC):
                step = dve(lambda e, j=j: e.scalar_tensor_tensor(
                    out=conv_out, in0=taps[j], scalar=conv_w[j][:, c:c + 1], in1=conv_out,
                    op0=ALU.mult, op1=ALU.add), [step])
            conv_ready[half, c] = step

        def activate_u(half, c):
            u_ready[half, c] = act(lambda e: e.activation(
                u_sb[:, half, c, :], u_sb[:, half, c, :], ACT.Silu, bias=conv_b[:, c:c + 1]), [conv_ready[half, c]])

        def norm_z(half):
            done = [chunk_stats(half, j, x_in[half]) for j in range(HC)]
            return layer_norm(half, done, z_gate[:, half * HC:(half + 1) * HC, :], Slot(None))

        def activate_z(half, normed):
            z = z_gate[:, half * HC:(half + 1) * HC, :]
            z_ready[half] = act(lambda e: e.activation(z, z, ACT.Silu), [normed])

        def project_x_dbl(half):
            bank = before_ffn.take()
            tok = slice(half * HT, (half + 1) * HT)
            before = bank.readers
            for c in range(EH):
                product = pe(lambda e, c=c: e.matmul(bank.t[0:DR + 2 * DS, :], x_proj_sb[:, c, :], u_sb[:, half, c, :],
                                                     start=c == 0, stop=c == EH - 1),
                             [x_proj_in, u_ready[half, c], *before])
            x_dbl_ready[half] = act(lambda e: e.activation(x_dbl[:, tok], bank.t[0:DR + 2 * DS, :], ACT.Copy),
                                    [product])
            bank.readers = [x_dbl_ready[half]]

        def store_bc(half):
            tok = slice(half * HT, (half + 1) * HT)
            bc_stored[half] = sp(lambda e: e.dma_start(bc_dram[:, tok], x_dbl[DR:, tok]), [x_dbl_ready[half]],
                                 lane(f"bc_stored{half}", 16))
            stores.append(bc_stored[half])

        def make_delta(half, s_buf, s_slot):
            products = []
            for c in range(EH):
                bank = before_ffn.take()
                product = pe(lambda e, c=c, bank=bank: e.matmul(
                    bank.t[:, :], dt_proj_sb[:, c * P:(c + 1) * P], x_dbl[0:DR, half * HT:(half + 1) * HT],
                    start=True, stop=True), [x_dbl_ready[half], dt_proj_in, *bank.readers])
                away = act(lambda e, c=c, bank=bank: e.activation(
                    s_buf[:, c, :], bank.t[:, :], ACT.Abs, bias=dt_bias[:, c:c + 1]), [product, *s_slot.readers])
                products.append((bank, away))
            yield
            for c, (bank, away) in enumerate(products):
                floor = dve(lambda e, c=c, bank=bank: e.tensor_scalar(
                    delta[:, half, c, :], bank.t[:, :], dt_bias[:, c:c + 1], 0.0, ALU.add, ALU.max), [away])
                bank.readers = [floor]
            yield
            raised, logged, excess = [], [], []
            for c in range(EH):
                raised.append(act(lambda e, c=c: e.activation(s_buf[:, c, :], s_buf[:, c, :], ACT.Exp, scale=-1.0),
                                  [products[c][1]]))
            for c in range(EH):
                logged.append(act(lambda e, c=c: e.activation(acc_sb[:, c, :], s_buf[:, c, :], ACT.Ln, bias=1.0),
                                  [raised[c], *acc_slot.readers]))
            yield
            for c in range(EH):
                one_s = delta_u[:, half, c, :]
                plus = dve(lambda e, c=c, one_s=one_s: e.tensor_scalar(one_s, s_buf[:, c, :], 1.0, None, ALU.add),
                           [raised[c]])
                excess.append(dve(lambda e, c=c, one_s=one_s: e.scalar_tensor_tensor(
                    out=one_s, in0=one_s, scalar=1.0, in1=s_buf[:, c, :], op0=ALU.subtract, op1=ALU.subtract), [plus]))
            for c in range(EH):
                d, du, u, log1p = (t for t in (delta[:, half, c, :], delta_u[:, half, c, :], u_sb[:, half, c, :],
                                               acc_sb[:, c, :]))
                step = dve(lambda e, du=du, log1p=log1p: e.tensor_tensor(log1p, log1p, du, ALU.subtract),
                           [logged[c], excess[c]])
                ready = dve(lambda e, d=d, log1p=log1p: e.tensor_tensor(d, d, log1p, ALU.add), [step, floor])
                engine = dve if half == 0 else pool
                driven = engine(lambda e, d=d, du=du, u=u: e.tensor_tensor(du, d, u, ALU.mult),
                                [ready, u_ready[half, c]])
            delta_ready[half] = (ready, driven)
            s_slot.readers = [logged[-1], excess[-1]]
            acc_slot.readers = [ready]

        for c in range(EH):
            project_in(0, c)
        for c in range(EH):
            convolve(0, c)
        for c in range(EH):
            activate_u(0, c)
            project_in(1, c)
        for c in range(EH):
            convolve(1, c)
        for slot in hc_slots.slots + h_slots.slots:
            slot.readers = [conv_ready[1, EH - 1]]
        project_x_dbl(0)
        store_bc(0)
        for n in range(3):
            load_b(0, n)
            load_c(0, n)
        norm0 = norm_z(0)
        next(norm0)
        a_exp = act(lambda e: e.activation(decay[:, :, :], a_log, ACT.Exp), [small_in])
        decay_ready = dve(lambda e: e.tensor_scalar(decay[:, :, :], decay[:, :, :], -1.0, None, ALU.mult), [a_exp])
        complete(make_delta(0, da_slots.slots[-1].t[:, :, :], da_slots.slots[-1]))
        for slot in da_slots.slots:
            slot.readers = [pool(lambda e, slot=slot: e.memset(
                slot.t[:, :, :].rearrange("p c (b s) -> p (c b) s", b=HB)[:, :, 0:1], 0.0), slot.readers)]

        def split_small(raw, hi, lo, landed):
            rounded = dve(lambda e: e.tensor_copy(hi[:, :, :], raw[:, :, :]), [landed])
            return dve(lambda e: e.tensor_tensor(lo[:, :, :], raw[:, :, :], hi[:, :, :].bitcast(F32), ALU.subtract),
                       [rounded])

        gate_ready = split_small(gate_raw, gate_hi, gate_lo, gate_in)
        cent_ready = split_small(cent_raw, cent_hi, cent_lo, cent_in)

        def ffn0_segments(c):
            at, end = c * P, (c + 1) * P
            while at < end:
                n = min(end, (at // I0 + 1) * I0) - at
                yield at // I0, at - c * P, n
                at += n

        def load_route(layer, half, c, stored):
            slot = mask_slots.take()
            parts = list(ffn0_segments(c)) if layer == 0 else [(c - SHARED_CHUNKS, 0, P)]
            for expert, at, n in parts:
                landed = sp(lambda e, expert=expert, at=at, n=n: e.dma_start(
                    slot.t[at:at + n, :], rows(route_dram[layer][half][expert:expert + 1, :], n)),
                    [stored, *slot.readers], slot.extra)
            return slot, landed

        def run_ffn(layer, units, stored, xt_ready, acc_of, between, finished):
            gu = Ring([(banks[4], banks[5]), (banks[6], banks[7])])
            first_done, waiting, routes, loaded = set(), [], {}, set()

            def need_route(i):
                if i < len(units) and not (layer == 1 and units[i][0] < SHARED_CHUNKS):
                    c, half = units[i]
                    if i not in loaded and half in stored:
                        loaded.add(i)
                        routes[i] = load_route(layer, half, c, stored[half])

            def shares(i):
                return 0 < i < len(units) and units[i][0] == units[i - 1][0]

            def down(i, slot, half, split, hidden_ready):
                hi, lo = slot.t
                first = half not in first_done
                first_done.add(half)
                final = i == max(k for k, u in enumerate(units) if u[1] == half)

                def multiply(e):
                    for w in range(WH):
                        at = slice(2 * WIDTH + w * P, 2 * WIDTH + (w + 1) * P)
                        last = product3(e, acc_of[half][w].t[:, :], hi[:, at], lo[:, at], split.t[0][:, :],
                                        split.t[1][:, :], first, final)
                    return last
                before = [r for b in acc_of[half] for r in b.readers] if first else []
                done = pe(multiply, [hidden_ready, *before])
                split.readers = [done]
                if not shares(i + 1):
                    slot.readers = [done]
                if final:
                    finished[half] = done

            for i, (c, half) in enumerate(units):
                if not shares(i):
                    key = (f"ffn{layer}", half, c)
                    slot, w_ready = split_weights(*key)
                hi, lo = slot.t
                g_bank, u_bank = gu.take()
                both = []
                for k, bank in enumerate((g_bank, u_bank)):
                    def multiply(e, k=k, bank=bank, hi=hi, lo=lo, half=half):
                        for w in range(WH):
                            at = slice(k * WIDTH + w * P, k * WIDTH + (w + 1) * P)
                            last = product3(e, bank.t[:, :], hi[:, at], lo[:, at], xt_hi[half][:, w, :],
                                            xt_lo[half][:, w, :], w == 0, w == WH - 1)
                        return last
                    both.append(pe(multiply, [w_ready, xt_ready[half], *bank.readers]))
                xt_slots[half].readers = [both[-1]]
                if i == 0:
                    yield
                if len(waiting) == 2:
                    down(*waiting.pop(0))
                for later in (i, i + 1, i + 2):
                    need_route(later)
                gated, hidden, split = gated_slots.take(), hidden_slots.take(), hidden_split.take()
                silu = act(lambda e, g=gated, b=g_bank: e.activation(g.t[:, :], b.t[:, :], ACT.Silu),
                           [both[0], *gated.readers])
                g_bank.readers = [silu]
                assert layer == 1 or i in routes
                if i in routes:
                    up = dve(lambda e, g=gated, h=hidden, b=u_bank: e.tensor_tensor(
                        h.t[:, :], g.t[:, :], b.t[:, :], ALU.mult), [silu, both[1], *hidden.readers])
                    route, route_in = routes.pop(i)
                    made = dve(lambda e, h=hidden, r=route: e.tensor_tensor(
                        h.t[:, :], h.t[:, :], r.t[:, :], ALU.mult), [up, route_in])
                    route.readers = [made]
                else:
                    up = made = dve(lambda e, g=gated, h=hidden, b=u_bank: e.scalar_tensor_tensor(
                        out=h.t[:, :], in0=g.t[:, :], scalar=SHARED_RATIO, in1=b.t[:, :], op0=ALU.mult,
                        op1=ALU.mult), [silu, both[1], *hidden.readers])
                u_bank.readers = [up]
                gated.readers = [up]
                if len(pieces_split) <= order[key] + 3:
                    split_piece()
                below = between(i)
                if below:
                    next(below, None)
                rounded = act(lambda e, h=hidden, s=split: e.activation(s.t[0][:, :], h.t[:, :], ACT.Copy),
                              [made, *split.readers])
                rest = dve(lambda e, h=hidden, s=split: e.tensor_tensor(
                    s.t[1][:, :], h.t[:, :], s.t[0][:, :].bitcast(F32), ALU.subtract), [rounded, *split.readers])
                hidden.readers = [rounded, rest]
                waiting.append((i, slot, half, split, rest))
                if below:
                    complete(below)
            for unit in waiting:
                down(*unit)

        for n in range(4):
            scan_decays(0, n)
        scan_drive(0, 0)
        for n in range(DS):
            scan_drive(0, n + 1)
            complete(scan_state(0, n))
            summed = scan_sum(0, n, n == 0)
            if n + 4 < DS:
                scan_decays(0, n + 4)
            if n == 0:
                norm1 = norm_z(1)
                next(norm1)
            if n == 1:
                activate_z(0, complete(norm0))
                activate_z(1, complete(norm1))
                for c in range(EH):
                    activate_u(1, c)
            if n == 2:
                project_x_dbl(1)
            if n == 6:
                store_bc(1)
                delta1 = make_delta(1, x_norm[:, :, :].rearrange("p (c a) w -> p c (a w)", c=EH), norm_slot)
                next(delta1)
            if n in (7, 8):
                next(delta1)
        split_piece()
        split_piece()

        def to_next_part(done, half, router, spread=False):
            normed = yield from layer_norm(half, done, x_norm, norm_slot)
            xt = yield from turn_and_split(half, normed, spare, spread)
            stored = yield from router(half, xt, spare, spread)
            return xt, stored

        def scan_to_ffn(half, summed):
            done = yield from scan_finish(half, summed)
            return (yield from to_next_part(done, half, route_layer0))

        xt_ready, stored = {}, {}
        done = complete(scan_finish(0, summed))
        for slot in more_split:
            slot.readers = [done[-1]]
        more_split_slots()
        for n in range(3):
            load_b(1, n)
            load_c(1, n)
        way = to_next_part(done, 0, route_layer0)
        next(way)
        split_piece()
        split_piece()
        next(way)
        next(way)
        complete(delta1)
        scan_drive(1, 0)
        next(way)
        xt_ready[0], stored[0] = complete(way)
        for n in range(4):
            scan_decays(1, n)
        complete(scan_state(1, 0))
        scan_drive(1, 1)
        after_scan = []

        def scan_below(i):
            n = i + SCANNED_BEFORE
            if n % 2 == 0 and n + 2 < DS:
                scan_decays(1, n + 2)
                scan_decays(1, n + 3)
            if n > 1 and n % 2 == 0 and n <= DS:
                scan_add(1, n - 1)
            if n > 2 and n % 2 == 1 and n <= DS:
                scan_sum(1, n - 2, n == 3)
            if n < DS:
                state = scan_state(1, n)
                next(state)
                yield
                complete(state)
            else:
                yield
            if n + 1 < DS:
                scan_drive(1, n + 1)
            if n == DS + 1:
                after_scan.append(Below(scan_to_ffn(1, scan_sum(1, DS - 1, False))))
            if after_scan and 1 not in xt_ready:
                after_scan[0].advance()
                if after_scan[0].result:
                    xt_ready[1], stored[1] = after_scan[0].result

        def ffn_to_attention(half, ring):
            done = yield from add_to_x(half, banks[2:4], finished[half], ring)
            normed = yield from layer_norm(half, done, x_norm, norm_slot)
            return (yield from turn_and_split(half, normed, spare, True))

        after_ffn, context_split = {}, []

        def below_ffn0(i):
            if i < FFN0_CHUNKS:
                yield from scan_below(i)
            if 0 in finished:
                if 0 not in after_ffn:
                    after_ffn[0] = Below(ffn_to_attention(0, spare))
                after_ffn[0].advance()
            if i == 2 * FFN0_CHUNKS - 8:
                context_split.append(split_context())
            if i == 2 * FFN0_CHUNKS - 1:
                next(attend)
                next(attend)

        def split_context():
            rounded = act(lambda e: e.activation(ctx_hi[:, :], ctx_sb[:, :], ACT.Copy), [xt_ready[1]])
            ctx_ready = pool(lambda e: e.tensor_tensor(ctx_lo[:, :], ctx_sb[:, :], ctx_hi[:, :].bitcast(F32),
                                                       ALU.subtract), [rounded])
            bias_ready = dve(lambda e: e.tensor_scalar(
                mask_bias[:, :, :], mask_u8[:, :, :], 1.0, -MASKED, ALU.subtract, ALU.mult), [mask_in, xt_ready[1]])
            valid_ready = dve(lambda e: e.tensor_reduce(any_valid[:, :], mask_u8[:, :, :], AX_X, ALU.max), [mask_in])
            return ctx_ready, bias_ready, valid_ready

        def attention(xt_of, between):
            ctx_ready, bias_ready, valid_ready = context_split[0]
            score_banks, prob_bank, head_bank = Ring(banks[4:6]), banks[6], banks[7]
            acc = banks[2:4]
            units = [(half, kv, q, b) for half, kv in groups for q in range(GROUP) for b in range(HB)]
            keys, values, queries, heads = {}, {}, {}, {}
            proj_w = {}

            def evacuate(bank, slot, product):
                out_hi, out_lo = ([t[:, :] if len(t.shape) == 2 else t[:, :, :].rearrange("p a b -> p (a b)")
                                   for t in slot.t])
                hi = act(lambda e: e.activation(out_hi, bank.t[:, :], ACT.Copy), [product, *slot.readers])
                lo = dve(lambda e: e.tensor_tensor(out_lo, bank.t[:, :], out_hi.bitcast(F32), ALU.subtract),
                         [hi, *slot.readers])
                bank.readers = [hi, lo]
                slot.readers = []
                return slot, lo

            def project(g, part):
                if g >= len(groups):
                    return
                half, kv = groups[g]
                tok = slice(half * HT, (half + 1) * HT)
                if g not in proj_w:
                    proj_w[g] = split_weights("proj", half, kv)
                slot, w_ready = proj_w[g]
                hi, lo = slot.t
                bank = spare.take()
                k_at = GROUP * WH * HD
                v_at = k_at + HD
                if part == 0:
                    product = pe(lambda e: product3(e, bank.t[:, :], hi[:, k_at:k_at + HD], lo[:, k_at:k_at + HD],
                                                    ctx_hi[:, tok], ctx_lo[:, tok], True, True),
                                 [w_ready, ctx_ready, *bank.readers])
                    keys[half, kv] = evacuate(bank, k_slots.take(), product)
                elif part == 2:
                    def multiply(e):
                        for j in range(HC):
                            at = slice(half * HT + j * P, half * HT + (j + 1) * P)
                            last = product3(e, bank.t[:, j * HD:(j + 1) * HD], ctx_hi[:, at], ctx_lo[:, at],
                                            hi[:, v_at:v_at + HD], lo[:, v_at:v_at + HD], True, True)
                        return last
                    product = pe(multiply, [w_ready, ctx_ready, *bank.readers])
                    values[half, kv] = evacuate(bank, v_slots.take(), product)
                else:
                    q = (part - 1) // 2

                    def multiply(e):
                        for w in range(WH):
                            at = slice((q * WH + w) * HD, (q * WH + w + 1) * HD)
                            last = product3(e, bank.t[:, :], hi[:, at], lo[:, at], xt_hi[half][:, w, :],
                                            xt_lo[half][:, w, :], w == 0, w == WH - 1)
                        return last
                    product = pe(multiply, [w_ready, xt_of(half), *bank.readers])
                    queries[half, kv, q] = evacuate(bank, q_slots.take(), product)
                    if part == GROUP + 1:
                        slot.readers = [product]
                        xt_slots[half].readers = [product]

            shifted, softened, probs, probs_t = {}, {}, {}, {}

            def scores(i):
                half, kv, q, b = units[i]
                bank, sc, pr = score_banks.take(), score_slots.take(), prob_slots.take()
                (k_slot, k_ready), (q_slot, q_ready) = keys[half, kv], queries[half, kv, q]
                key_tok = slice(b * SEQ, (b + 1) * SEQ)

                def multiply(e):
                    for r in range(2):
                        at = slice(b * SEQ + r * P, b * SEQ + (r + 1) * P)
                        last = product3(e, bank.t[:, r * SEQ:(r + 1) * SEQ], q_slot.t[0][:, at], q_slot.t[1][:, at],
                                        k_slot.t[0][:, key_tok], k_slot.t[1][:, key_tok], True, True)
                    return last
                product = pe(multiply, [k_ready, q_ready, *bank.readers])
                q_slot.readers = [product]
                k_slot.readers = [product]
                row_max, row_bias = sc.extra
                batch = half * HB + b
                for r in range(2):
                    masked = dve(lambda e, r=r: e.tensor_tensor_reduce(
                        sc.t[:, r, :], bank.t[:, r * SEQ:(r + 1) * SEQ], mask_bias[:, batch, :], 1.0, -3.0e38,
                        ALU.add, ALU.max, row_max[:, r:r + 1]), [product, bias_ready, *sc.readers])
                bank.readers = [masked]
                shift = dve(lambda e: e.tensor_scalar(row_bias[:, :], row_max[:, :], -SCALE, None, ALU.mult), [masked])
                shifted[i] = (sc, pr, shift)

            def soften(i):
                sc, pr, shift = shifted.pop(i)
                row_max, row_bias = sc.extra
                row_sum, row_scale = pr.extra
                for r in range(2):
                    raised = act(lambda e, r=r: e.activation(pr.t[:, r, :], sc.t[:, r, :], ACT.Exp, scale=SCALE,
                                                             bias=row_bias[:, r:r + 1], accum_out=row_sum[:, r:r + 1]),
                                 [shift, *pr.readers])
                sc.readers = [raised]
                softened[i] = (pr, raised)

            def normalize(i):
                pr, raised = softened.pop(i)
                row_sum, row_scale = pr.extra
                batch = units[i][0] * HB + units[i][3]
                inverse = dve(lambda e: e.reciprocal(row_scale[:, :], row_sum[:, :]), [raised])
                kept = pool(lambda e: e.tensor_tensor(row_scale[:, :], row_scale[:, :],
                                                      any_valid[:, batch:batch + 1].broadcast_to([P, 2]), ALU.mult),
                            [inverse, valid_ready])
                normed = pool(lambda e: e.tensor_tensor(pr.t[:, :, :], pr.t[:, :, :],
                                                        row_scale[:, :].unsqueeze(2).broadcast_to([P, 2, SEQ]),
                                                        ALU.mult), [kept])
                probs[i] = (pr, normed)

            def turn_probs(i):
                pr, normed = probs.pop(i)

                def turn(e):
                    for s in range(2):
                        for r in range(2):
                            last = e.transpose(prob_bank.t[:, s * SEQ + r * P:s * SEQ + (r + 1) * P],
                                               pr.t[:, r, s * P:(s + 1) * P], identity[:, :])
                    return last
                turned = pe(turn, [normed, ident_ready, *prob_bank.readers])
                pr.readers = [turned]
                probs_t[i] = evacuate(prob_bank, prob_t_slots.take(), turned)

            def head_output(i):
                half, kv, q, b = units[i]
                pt, pt_ready = probs_t.pop(i)
                v_slot, v_ready = values[half, kv]

                def multiply(e):
                    for s in range(2):
                        j = b * (SEQ // P) + s
                        last = product3(e, head_bank.t[:, b * SEQ:(b + 1) * SEQ], v_slot.t[0][:, j, :],
                                        v_slot.t[1][:, j, :], pt.t[0][:, s, :], pt.t[1][:, s, :], s == 0, s == 1)
                    return last
                before = head_bank.readers if b == 0 else []
                product = pe(multiply, [pt_ready, v_ready, *before])
                pt.readers = [product]
                v_slot.readers = [product]
                if b == HB - 1:
                    heads[i] = evacuate(head_bank, head_slots.take(), product)

            def project_out(i):
                half, kv, q, b = units[i]
                if b != HB - 1:
                    return
                head, head_ready = heads.pop(i)
                slot, w_ready = split_weights("out", half, kv)
                first, final = (kv, q) == (0, 0), (kv, q) == (KV_HEADS - 1, GROUP - 1)

                def multiply(e):
                    for w in range(WH):
                        at = slice(q * WIDTH + w * P, q * WIDTH + (w + 1) * P)
                        last = product3(e, acc[w].t[:, :], slot.t[0][:, at], slot.t[1][:, at], head.t[0][:, :],
                                        head.t[1][:, :], first, final)
                    return last
                before = [r for bk in acc for r in bk.readers] if first else []
                product = pe(multiply, [head_ready, w_ready, *before])
                head.readers = [product]
                if q == GROUP - 1:
                    slot.readers = [product]
                if final:
                    attended[half] = product

            for part in range(GROUP + 2):
                project(0, part)
                yield
            for i in range(len(units) + 4):
                if 0 <= i - 1 < len(units):
                    normalize(i - 1)
                if i < len(units):
                    scores(i)
                if 0 <= i - 2 < len(units):
                    turn_probs(i - 2)
                if 0 <= i - 3 < len(units):
                    head_output(i - 3)
                if 0 <= i - 4 < len(units):
                    project_out(i - 4)
                if i < len(units):
                    split_piece()
                    soften(i)
                    project(i // (GROUP * HB) + 1, (1, 0, 2, 3)[i % (GROUP * HB)])
                between(i)

        def attention_to_ffn(half):
            done = yield from add_to_x(half, banks[2:4], attended[half], Ring([banks[2], banks[1]]))
            return (yield from to_next_part(done, half, route_layer1, half == 0))

        attended, after_attention = {}, {}
        xt_ready1, stored1, finished1 = {}, {}, {}

        def norms_below(i):
            if i >= 3:
                after_ffn[1].advance()
            if 0 in attended:
                if 0 not in after_attention:
                    after_attention[0] = Below(attention_to_ffn(0))
                after_attention[0].advance()
            if i == len(groups) * GROUP * HB:
                xt_ready1[0], stored1[0] = after_attention[0].finish()
                next(last_ffn)

        attend = attention(lambda half: after_ffn[half].finish(), norms_below)

        units = [(c, 0) for c in range(ALONE)]
        units += [(c, h) for c in range(ALONE, FFN1_CHUNKS) for h in range(HALVES)]
        units += [(c, 1) for c in range(ALONE)]
        acc_of = {0: banks[2:4], 1: banks[0:2]}
        outputs = {}

        def to_output(half, ring):
            added = yield from add_to_x(half, acc_of[half], finished1[half], ring, stats=False)
            for pair, step in enumerate(added):
                t = half * HC + 2 * pair
                stores.append(sp(lambda e, t=t: e.dma_start(out_dram[:, t:t + 2, :], x_tok[:, t:t + 2, :]), [step],
                                 lane(f"out_stored{t}", 16)))
            return added

        def ends_below(i):
            if 1 not in xt_ready1:
                after_attention[1].advance()
                if after_attention[1].result:
                    xt_ready1[1], stored1[1] = after_attention[1].result
            if 0 in finished1:
                if 0 not in outputs:
                    outputs[0] = Below(to_output(0, Ring(acc_of[0])))
                outputs[0].advance()

        last_ffn = run_ffn(1, units, stored1, xt_ready1, acc_of, ends_below, finished1)

        finished = {}
        complete(run_ffn(0, [(c, h) for h in range(HALVES) for c in range(FFN0_CHUNKS)], stored, xt_ready,
                         {h: banks[2:4] for h in range(HALVES)}, below_ffn0, finished))

        after_ffn[1] = Below(ffn_to_attention(1, Ring(banks[2:4])))
        after_ffn[1].advance()
        complete(attend)
        after_attention[1] = Below(attention_to_ffn(1))
        after_attention[1].advance()
        complete(last_ffn)
        complete(to_output(1, Ring(banks[4:8])))

        sp(lambda e: e.drain(), stores)

        for q in (pe, act, dve, pool, sp):
            for _, _, step in q.todo:
                counted = number_steps(step)
                step.value = counted

        block = stack.enter_context(nc.Block())

        @block.tensor
        def _(e):
            pe.run(e)

        @block.scalar
        def _(e):
            act.run(e)

        @block.vector
        def _(e):
            dve.run(e)

        @block.gpsimd
        def _(e):
            pool.run(e)

        @block.sync
        def _(e):
            sp.run(e)


def number_steps(step):
    lane = step.lane
    if step.value is None:
        count = 0
        for s in lane.steps:
            count += lane.weight if s.awaited else 0
            s.value = count
    return step.value


def kernel(**inputs):
    import numpy as np
    import concourse.bacc as bacc
    from concourse.bass_utils import run_bass_kernel_spmd

    a = {name: np.asarray(value) for name, value in inputs.items()}

    def wide(w):
        return w.reshape(-1, P, w.shape[-1]).transpose(1, 0, 2)

    def ffn_chunks(gate, up, down):
        n = gate.shape[1] // P
        sides = [wide(w).reshape(P, WH, n, P).transpose(2, 0, 1, 3).reshape(n, P, WIDTH) for w in (gate, up)]
        return np.concatenate([*sides, down.reshape(n, P, WIDTH)], axis=2)

    by_channel = [a[f"L0_xattn_{n}"].reshape(EH, P, -1).transpose(1, 0, 2)
                  for n in ("conv_w", "conv_b", "D", "dt_proj_b", "A_log")]
    ffn1_shared = ffn_chunks(a["L1_ffn_wg_s"], a["L1_ffn_wu_s"], a["L1_ffn_wd_s"])
    ffn1_routed = ffn_chunks(a["L1_ffn_wg"].transpose(1, 0, 2).reshape(WIDTH, E1 * I1),
                             a["L1_ffn_wu"].transpose(1, 0, 2).reshape(WIDTH, E1 * I1),
                             a["L1_ffn_wd"].reshape(E1 * I1, WIDTH))
    wq = wide(a["L1_xattn_Wq"]).reshape(P, WH, KV_HEADS, GROUP, HD).transpose(2, 0, 3, 1, 4)
    wk = a["L1_xattn_Wk"].reshape(CTX, KV_HEADS, HD).transpose(1, 0, 2)
    wv = a["L1_xattn_Wv"].reshape(CTX, KV_HEADS, HD).transpose(1, 0, 2)
    wo = a["L1_xattn_Wo"].reshape(KV_HEADS, GROUP, HD, WIDTH).transpose(0, 2, 1, 3)
    laid_out = {
        "x": a["x"],
        "ctx_t": a["ctx_1024"].reshape(TOKENS, CTX).T,
        "key_mask": a["mask_BxS2_bf1"].reshape(1, TOKENS),
        "in_proj_t": a["L0_xattn_in_proj_w"].T,
        "ssm_small": np.concatenate(by_channel, axis=2),
        "x_proj_t": wide(a["L0_xattn_x_proj_w"].T),
        "dt_proj_t": a["L0_xattn_dt_proj_w"].T,
        "gate_t": wide(a["L0_ffn_gate_w"].T),
        "centroids_t": wide(a["L1_ffn_centroids"].T),
        "gate_bias": a["L1_ffn_gate_bias"].reshape(1, E1),
        "ffn0_w": ffn_chunks(a["L0_ffn_w_gate_proj"].reshape(E0 * I0, WIDTH).T,
                             a["L0_ffn_w_up_proj"].reshape(E0 * I0, WIDTH).T,
                             a["L0_ffn_w_down_proj"].transpose(0, 2, 1).reshape(E0 * I0, WIDTH)),
        "attn_proj_w": np.concatenate([wq.reshape(KV_HEADS, P, -1), wk, wv], axis=2),
        "attn_out_w": wo.reshape(KV_HEADS, HD, WO_PIECE),
        "ffn1_w": np.concatenate([ffn1_shared, ffn1_routed], axis=0),
    }
    nc = bacc.Bacc("TRN2", target_bir_lowering=False, num_devices=1)
    arrays, args = {}, []
    for name, value in laid_out.items():
        value = np.ascontiguousarray(value)
        arrays[f"in_{name}"] = value
        args.append(nc.dram_tensor(f"in_{name}", value.shape, mybir.dt.from_np(value.dtype), kind="ExternalInput").ap())
    args.append(nc.dram_tensor("out", (BATCHES, SEQ, WIDTH), F32, kind="ExternalOutput").ap())
    build(nc, *args)
    result = run_bass_kernel_spmd(nc, [arrays], core_ids=[0])
    return result.results[0]["out"]
```
